# Optimizing a Trainium2 kernel written in Bass

```python
import numpy as np
import jax
import jax.numpy as jnp

def _softmax(x, axis=-1):
    return jax.nn.softmax(x, axis=axis)

def _gelu(x):
    return jax.nn.gelu(x, approximate=True)

def _silu(x):
    return jax.nn.silu(x)

def _sigmoid(x):
    return jax.nn.sigmoid(x)

def _layernorm(x, axis=-1, eps=1e-05):
    m = jnp.mean(x, axis=axis, keepdims=True)
    v = jnp.var(x, axis=axis, keepdims=True)
    return (x - m) / jnp.sqrt(v + eps)

def _scatter_add(tgt, idx, src, axis=0):
    return tgt.at[idx].add(src)

def _segment_sum(src, seg, n):
    return jax.ops.segment_sum(src, seg, n)
kernel_name = 'mk_flamingo_gated_d2_seqx_r8_a87105'

def setup_inputs(seed: int=0):
    np.random.seed(seed)
    _w = jnp.asarray

    def _rec_inputs():
        import jax
        import jax.numpy as jnp
        _rk = jax.random.key(seed)
        x = 7.22e-05 + 1 * jax.random.normal(jax.random.fold_in(_rk, 1), (16, 128, 256), jnp.float32)
        _lenS = 128 - jax.random.randint(jax.random.fold_in(_rk, 7), (16,), 0, max(1, 128 // 4) + 1, jnp.int32)
        _lenS2 = 128 - jax.random.randint(jax.random.fold_in(_rk, 8), (16,), 0, max(1, 128 // 4) + 1, jnp.int32)
        _ctx_2048P = jax.random.normal(jax.random.fold_in(_rk, 11), (16, 16, 256), jnp.float32)
        _ctx_2048c = jax.random.dirichlet(jax.random.fold_in(_rk, 511), 0.3 * jnp.ones((16,), jnp.float32), (16, 128))
        _ctx_2048t = jnp.einsum('bsk,bkd->bsd', _ctx_2048c, _ctx_2048P)
        _ctx_2048t = _ctx_2048t * jax.lax.rsqrt(jnp.mean(jnp.square(_ctx_2048t)) + 1e-12) * 0.953939
        ctx_2048 = -0.000514642 + 1.00011 * (_ctx_2048t + 0.3 * jax.random.normal(jax.random.fold_in(_rk, 611), (16, 128, 256), jnp.float32))
        _g = jax.random.normal(jax.random.fold_in(_rk, 9001), (2, 2), jnp.float32)
        _g = jnp.sign(_g) * jnp.maximum(jnp.abs(_g), 1.0) + (_g == 0) * 1.0
        g_xattn = _g[0]
        g_ffn = _g[1]
        return (x, ctx_2048, g_xattn, g_ffn)
    x, ctx_2048, g_xattn, g_ffn = _rec_inputs()

    def _L0_xattn_setup():
        import jax, jax.numpy as jnp
        import numpy as np
        D_MODEL = 256
        NUM_HEADS = 16
        HEAD_DIM = D_MODEL // NUM_HEADS

        def _fq_sym(x, axis):
            s = jnp.max(jnp.abs(x), axis=axis, keepdims=True) / 127.0
            s = jnp.maximum(s, 1e-08)
            q = jnp.clip(jnp.round(x / s), -127.0, 127.0) * s
            return x + jax.lax.stop_gradient(q - x)

        def _fq_unsigned(x, axis):
            s = jnp.max(x, axis=axis, keepdims=True) / 255.0
            s = jnp.maximum(s, 1e-08)
            q = jnp.clip(jnp.round(x / s), 0.0, 255.0) * s
            return x + jax.lax.stop_gradient(q - x)
        key = jax.random.key(seed)
        ks = jax.random.split(key, 8)
        B, N, M, C = (2, 256, 64, D_MODEL)
        return {'x': jax.random.normal(ks[0], (B, N, C), jnp.float32), 'cond': jax.random.normal(ks[1], (B, M, C), jnp.float32), 'Wq': jax.random.normal(ks[2], (C, C), jnp.float32) * 0.02, 'bq': jnp.zeros((C,), jnp.float32), 'Wkv': jax.random.normal(ks[3], (C, 2 * C), jnp.float32) * 0.02, 'bkv': jnp.zeros((2 * C,), jnp.float32), 'Wp': jax.random.normal(ks[4], (C, C), jnp.float32) * 0.02, 'bp': jnp.zeros((C,), jnp.float32)}
    _L0_xattn_all = _L0_xattn_setup()
    _L0_xattn_in = {k: v for k, v in _L0_xattn_all.items() if k in ('Wq', 'bq', 'Wkv', 'bkv', 'Wp', 'bp')}
    del _L0_xattn_all

    def _L0_ffn_setup():
        import jax, jax.numpy as jnp
        import numpy as np
        B, S, H = (2, 256, 256)
        E, K, F = (32, 4, 176)
        FS = 704
        EPS = 1e-06
        CAP = 128
        key = jax.random.key(seed)
        ks = jax.random.split(key, 10)
        s = 0.02
        return {'hidden_states': jax.random.normal(ks[0], (B, S, H), jnp.float32), 'w_norm': 1.0 + 0.02 * jax.random.normal(ks[1], (H,), jnp.float32), 'w_router': s * jax.random.normal(ks[2], (H, E), jnp.float32), 'w_gate': s * jax.random.normal(ks[3], (E, H, F), jnp.float32), 'w_up': s * jax.random.normal(ks[4], (E, H, F), jnp.float32), 'w_down': s * jax.random.normal(ks[5], (E, F, H), jnp.float32), 'sw_gate': s * jax.random.normal(ks[6], (H, FS), jnp.float32), 'sw_up': s * jax.random.normal(ks[7], (H, FS), jnp.float32), 'sw_down': s * jax.random.normal(ks[8], (FS, H), jnp.float32), 'w_shared_gate': s * jax.random.normal(ks[9], (H, 1), jnp.float32)}
    _L0_ffn_all = _L0_ffn_setup()
    _L0_ffn_in = {k: v for k, v in _L0_ffn_all.items() if k in ('w_norm', 'w_router', 'w_gate', 'w_up', 'w_down', 'sw_gate', 'sw_up', 'sw_down', 'w_shared_gate')}
    del _L0_ffn_all

    def _L1_xattn_setup():
        import jax, jax.numpy as jnp
        import numpy as np

        def _wkv(time_decay, time_first, k, v):
            w = -jnp.exp(time_decay)
            u = time_first
            B, T, C = k.shape
            aa = jnp.zeros((B, C), dtype=k.dtype)
            bb = jnp.zeros((B, C), dtype=k.dtype)
            pp = jnp.full((B, C), -1e+38, dtype=k.dtype)

            def step(carry, kv_t):
                aa, bb, pp = carry
                kt, vt = kv_t
                ww = u + kt
                q = jnp.maximum(pp, ww)
                e1 = jnp.exp(pp - q)
                e2 = jnp.exp(ww - q)
                y_t = (e1 * aa + e2 * vt) / (e1 * bb + e2)
                ww2 = pp + w
                q2 = jnp.maximum(ww2, kt)
                e1b = jnp.exp(ww2 - q2)
                e2b = jnp.exp(kt - q2)
                new_carry = (e1b * aa + e2b * vt, e1b * bb + e2b, q2)
                return (new_carry, y_t)
            ks = jnp.transpose(k, (1, 0, 2))
            vs = jnp.transpose(v, (1, 0, 2))
            _, ys = jax.lax.scan(step, (aa, bb, pp), (ks, vs))
            return jnp.transpose(ys, (1, 0, 2))
        key = jax.random.key(seed)
        k1, k2, k3, k4 = jax.random.split(key, 4)
        B, T, C = (8, 128, 256)
        return {'batch_size': B, 'seq_len': T, 'embedding_dim': C, 'time_decay': jax.random.normal(k1, (C,), dtype=jnp.float32), 'time_first': jax.random.normal(k2, (C,), dtype=jnp.float32), 'k': jax.random.normal(k3, (B, T, C), dtype=jnp.float32), 'v': jax.random.normal(k4, (B, T, C), dtype=jnp.float32)}
    _L1_xattn_all = _L1_xattn_setup()
    _L1_xattn_in = {k: v for k, v in _L1_xattn_all.items() if k in ('time_decay', 'time_first')}
    del _L1_xattn_all

    def _L1_ffn_setup():
        import jax, jax.numpy as jnp
        import numpy as np
        B, S, D = (4, 64, 256)
        E, K, H = (8, 2, 176)
        HS = 2 * 176
        ALPHA = 0.001
        W_SCALE = 0.02

        def _moe_forward(hidden_states, gate_w, w_gate, w_up, w_down, sw_gate, sw_up, sw_down):
            b, s, d = hidden_states.shape
            x = hidden_states.reshape(-1, d)
            T = x.shape[0]
            logits = x @ gate_w
            scores = jax.nn.softmax(logits, axis=-1)
            topk_w, topk_idx = jax.lax.top_k(scores, K)
            mask = jax.nn.one_hot(topk_idx, E, dtype=scores.dtype).sum(axis=1)
            ce = mask.mean(axis=0)
            Pi = scores.mean(axis=0)
            aux_loss = (Pi * ce * E).sum() * ALPHA
            comb = jnp.zeros((T, E), dtype=x.dtype)
            comb = comb.at[jnp.arange(T)[:, None], topk_idx].add(topk_w)
            g = jax.nn.silu(jnp.einsum('td,edh->teh', x, w_gate)) * jnp.einsum('td,edh->teh', x, w_up)
            routed = jnp.einsum('teh,ehd,te->td', g, w_down, comb)
            shared = jax.nn.silu(x @ sw_gate) * (x @ sw_up) @ sw_down
            out = (routed + shared).reshape(b, s, d)
            return (out, aux_loss)
        key = jax.random.key(seed)
        ks = jax.random.split(key, 8)
        rn = lambda k, sh: jax.random.normal(k, sh, dtype=jnp.float32)
        return {'hidden_states': rn(ks[0], (B, S, D)), 'gate_w': rn(ks[1], (D, E)) * W_SCALE, 'w_gate': rn(ks[2], (E, D, H)) * W_SCALE, 'w_up': rn(ks[3], (E, D, H)) * W_SCALE, 'w_down': rn(ks[4], (E, H, D)) * W_SCALE, 'sw_gate': rn(ks[5], (D, HS)) * W_SCALE, 'sw_up': rn(ks[6], (D, HS)) * W_SCALE, 'sw_down': rn(ks[7], (HS, D)) * W_SCALE}
    _L1_ffn_all = _L1_ffn_setup()
    _L1_ffn_in = {k: v for k, v in _L1_ffn_all.items() if k in ('gate_w', 'w_gate', 'w_up', 'w_down', 'sw_gate', 'sw_up', 'sw_down')}
    del _L1_ffn_all
    return {'x': x, 'ctx_2048': ctx_2048, 'g_xattn': g_xattn, 'g_ffn': g_ffn, 'L0_xattn_Wq': _L0_xattn_in['Wq'], 'L0_xattn_bq': _L0_xattn_in['bq'], 'L0_xattn_Wkv': _L0_xattn_in['Wkv'], 'L0_xattn_bkv': _L0_xattn_in['bkv'], 'L0_xattn_Wp': _L0_xattn_in['Wp'], 'L0_xattn_bp': _L0_xattn_in['bp'], 'L0_ffn_w_norm': _L0_ffn_in['w_norm'], 'L0_ffn_w_router': _L0_ffn_in['w_router'], 'L0_ffn_w_gate': _L0_ffn_in['w_gate'], 'L0_ffn_w_up': _L0_ffn_in['w_up'], 'L0_ffn_w_down': _L0_ffn_in['w_down'], 'L0_ffn_sw_gate': _L0_ffn_in['sw_gate'], 'L0_ffn_sw_up': _L0_ffn_in['sw_up'], 'L0_ffn_sw_down': _L0_ffn_in['sw_down'], 'L0_ffn_w_shared_gate': _L0_ffn_in['w_shared_gate'], 'L1_xattn_time_decay': _L1_xattn_in['time_decay'], 'L1_xattn_time_first': _L1_xattn_in['time_first'], 'L1_ffn_gate_w': _L1_ffn_in['gate_w'], 'L1_ffn_w_gate': _L1_ffn_in['w_gate'], 'L1_ffn_w_up': _L1_ffn_in['w_up'], 'L1_ffn_w_down': _L1_ffn_in['w_down'], 'L1_ffn_sw_gate': _L1_ffn_in['sw_gate'], 'L1_ffn_sw_up': _L1_ffn_in['sw_up'], 'L1_ffn_sw_down': _L1_ffn_in['sw_down']}

def reference(x, ctx_2048, g_xattn, g_ffn, L0_xattn_Wq, L0_xattn_bq, L0_xattn_Wkv, L0_xattn_bkv, L0_xattn_Wp, L0_xattn_bp, L0_ffn_w_norm, L0_ffn_w_router, L0_ffn_w_gate, L0_ffn_w_up, L0_ffn_w_down, L0_ffn_sw_gate, L0_ffn_sw_up, L0_ffn_sw_down, L0_ffn_w_shared_gate, L1_xattn_time_decay, L1_xattn_time_first, L1_ffn_gate_w, L1_ffn_w_gate, L1_ffn_w_up, L1_ffn_w_down, L1_ffn_sw_gate, L1_ffn_sw_up, L1_ffn_sw_down):
    import jax
    import jax.numpy as jnp

    def _L0_xattn_ref(x, cond, Wq, bq, Wkv, bkv, Wp, bp):
        import jax, jax.numpy as jnp
        import numpy as np
        D_MODEL = 256
        NUM_HEADS = 16
        HEAD_DIM = D_MODEL // NUM_HEADS

        def _fq_sym(x, axis):
            s = jnp.max(jnp.abs(x), axis=axis, keepdims=True) / 127.0
            s = jnp.maximum(s, 1e-08)
            q = jnp.clip(jnp.round(x / s), -127.0, 127.0) * s
            return x + jax.lax.stop_gradient(q - x)

        def _fq_unsigned(x, axis):
            s = jnp.max(x, axis=axis, keepdims=True) / 255.0
            s = jnp.maximum(s, 1e-08)
            q = jnp.clip(jnp.round(x / s), 0.0, 255.0) * s
            return x + jax.lax.stop_gradient(q - x)
        B, N, C = x.shape
        H, hd = (NUM_HEADS, HEAD_DIM)
        q = (x @ Wq + bq).reshape(1, B * N, H, hd)
        kv = (cond @ Wkv + bkv).reshape(1, -1, 2, H, hd)
        k, v = (kv[:, :, 0], kv[:, :, 1])
        scale = 1.0 / np.sqrt(hd).astype(np.float32)
        q = jnp.transpose(q * scale, (0, 2, 1, 3))
        k = jnp.transpose(k, (0, 2, 1, 3))
        v = jnp.transpose(v, (0, 2, 1, 3))
        q = _fq_sym(q, axis=-1)
        k = _fq_sym(k, axis=-1)
        v = _fq_sym(v, axis=2)
        attn = jnp.einsum('bhqd,bhkd->bhqk', q, k)
        attn = jax.nn.softmax(attn.astype(jnp.float32), axis=-1)
        attn = _fq_unsigned(attn, axis=-1)
        out = jnp.einsum('bhqk,bhkd->bhqd', attn, v)
        out = jnp.transpose(out, (0, 2, 1, 3)).reshape(B, N, C)
        return out @ Wp + bp

    def _L0_ffn_ref(hidden_states, w_norm, w_router, w_gate, w_up, w_down, sw_gate, sw_up, sw_down, w_shared_gate):
        import jax, jax.numpy as jnp
        import numpy as np
        B, S, H = (2, 256, 256)
        E, K, F = (32, 4, 176)
        FS = 704
        EPS = 1e-06
        CAP = 128
        inp = hidden_states
        xf = inp.astype(jnp.float32)
        var = jnp.mean(xf * xf, axis=-1, keepdims=True)
        x = (w_norm * (xf * jax.lax.rsqrt(var + EPS))).astype(inp.dtype)
        Bq, Sq, Hq = x.shape
        x = x.reshape(-1, Hq)
        T = Bq * Sq
        logits = x @ w_router
        probs = jax.nn.softmax(logits.astype(jnp.float32), axis=-1)
        w_topk, sel = jax.lax.top_k(probs, K)
        w_topk = w_topk.astype(x.dtype)
        flat_e = sel.reshape(-1)
        order = jnp.argsort(flat_e)
        sorted_e = flat_e[order]
        counts = jnp.zeros((E,), jnp.int32).at[flat_e].add(1)
        starts = jnp.cumsum(counts) - counts
        pos = jnp.arange(T * K) - starts[sorted_e]
        tok = order // K
        valid = pos < CAP
        dest = jnp.where(valid, pos, CAP)
        buf = jnp.zeros((E, CAP + 1, Hq), x.dtype).at[sorted_e, dest].set(x[tok])
        buf = buf[:, :CAP]
        g = jnp.einsum('ech,ehf->ecf', buf, w_gate)
        u = jnp.einsum('ech,ehf->ecf', buf, w_up)
        y = jnp.einsum('ecf,efh->ech', jax.nn.silu(g) * u, w_down)
        wv = w_topk.reshape(-1)[order] * valid.astype(x.dtype)
        gath = y[sorted_e, jnp.minimum(pos, CAP - 1)]
        out = jnp.zeros((T, Hq), x.dtype).at[tok].add(gath * wv[:, None])
        sh = jax.nn.silu(x @ sw_gate) * (x @ sw_up) @ sw_down
        sh = jax.nn.sigmoid(x @ w_shared_gate) * sh
        out = out + sh
        return inp + out.reshape(Bq, Sq, Hq)

    def _L1_xattn_ref(batch_size, seq_len, embedding_dim, time_decay, time_first, k, v):
        import jax, jax.numpy as jnp
        import numpy as np

        def _wkv(time_decay, time_first, k, v):
            w = -jnp.exp(time_decay)
            u = time_first
            B, T, C = k.shape
            aa = jnp.zeros((B, C), dtype=k.dtype)
            bb = jnp.zeros((B, C), dtype=k.dtype)
            pp = jnp.full((B, C), -1e+38, dtype=k.dtype)

            def step(carry, kv_t):
                aa, bb, pp = carry
                kt, vt = kv_t
                ww = u + kt
                q = jnp.maximum(pp, ww)
                e1 = jnp.exp(pp - q)
                e2 = jnp.exp(ww - q)
                y_t = (e1 * aa + e2 * vt) / (e1 * bb + e2)
                ww2 = pp + w
                q2 = jnp.maximum(ww2, kt)
                e1b = jnp.exp(ww2 - q2)
                e2b = jnp.exp(kt - q2)
                new_carry = (e1b * aa + e2b * vt, e1b * bb + e2b, q2)
                return (new_carry, y_t)
            ks = jnp.transpose(k, (1, 0, 2))
            vs = jnp.transpose(v, (1, 0, 2))
            _, ys = jax.lax.scan(step, (aa, bb, pp), (ks, vs))
            return jnp.transpose(ys, (1, 0, 2))
        assert seq_len <= 128
        return _wkv(time_decay, time_first, k, v)

    def _L1_ffn_ref(hidden_states, gate_w, w_gate, w_up, w_down, sw_gate, sw_up, sw_down):
        import jax, jax.numpy as jnp
        import numpy as np
        B, S, D = (4, 64, 256)
        E, K, H = (8, 2, 176)
        HS = 2 * 176
        ALPHA = 0.001
        W_SCALE = 0.02

        def _moe_forward(hidden_states, gate_w, w_gate, w_up, w_down, sw_gate, sw_up, sw_down):
            b, s, d = hidden_states.shape
            x = hidden_states.reshape(-1, d)
            T = x.shape[0]
            logits = x @ gate_w
            scores = jax.nn.softmax(logits, axis=-1)
            topk_w, topk_idx = jax.lax.top_k(scores, K)
            mask = jax.nn.one_hot(topk_idx, E, dtype=scores.dtype).sum(axis=1)
            ce = mask.mean(axis=0)
            Pi = scores.mean(axis=0)
            aux_loss = (Pi * ce * E).sum() * ALPHA
            comb = jnp.zeros((T, E), dtype=x.dtype)
            comb = comb.at[jnp.arange(T)[:, None], topk_idx].add(topk_w)
            g = jax.nn.silu(jnp.einsum('td,edh->teh', x, w_gate)) * jnp.einsum('td,edh->teh', x, w_up)
            routed = jnp.einsum('teh,ehd,te->td', g, w_down, comb)
            shared = jax.nn.silu(x @ sw_gate) * (x @ sw_up) @ sw_down
            out = (routed + shared).reshape(b, s, d)
            return (out, aux_loss)
        out, _aux = _moe_forward(hidden_states, gate_w, w_gate, w_up, w_down, sw_gate, sw_up, sw_down)
        return out
    x = x + jnp.tanh(g_xattn[0]) * _L0_xattn_ref(_layernorm(x, axis=-1), ctx_2048, L0_xattn_Wq, L0_xattn_bq, L0_xattn_Wkv, L0_xattn_bkv, L0_xattn_Wp, L0_xattn_bp)
    x = x + jnp.tanh(g_ffn[0]) * _L0_ffn_ref(_layernorm(x, axis=-1), L0_ffn_w_norm, L0_ffn_w_router, L0_ffn_w_gate, L0_ffn_w_up, L0_ffn_w_down, L0_ffn_sw_gate, L0_ffn_sw_up, L0_ffn_sw_down, L0_ffn_w_shared_gate)
    x = x + jnp.tanh(g_xattn[1]) * _L1_xattn_ref(16, 128, 256, L1_xattn_time_decay, L1_xattn_time_first, _layernorm(x, axis=-1), ctx_2048)
    x = x + jnp.tanh(g_ffn[1]) * _L1_ffn_ref(_layernorm(x, axis=-1), L1_ffn_gate_w, L1_ffn_w_gate, L1_ffn_w_up, L1_ffn_w_down, L1_ffn_sw_gate, L1_ffn_sw_up, L1_ffn_sw_down)
    return x

_drawn_inputs = setup_inputs


def setup_inputs(seed=0):
    import zlib

    import numpy as np

    out = dict(_drawn_inputs(seed))
    spreads = {'g_ffn': (-1.0, 0.6),
     'L0_xattn_bq': (0.0, 0.8),
     'L0_xattn_bkv': (0.0, 0.8),
     'L0_xattn_bp': (0.0, 0.273)}
    factors = {'L0_xattn_Wq': 8.0,
     'L0_xattn_Wkv': 8.0,
     'L0_xattn_Wp': 5.849,
     'L0_ffn_w_norm': 8.0,
     'L0_ffn_w_router': 8.0,
     'L0_ffn_w_gate': 8.0,
     'L0_ffn_w_up': 8.0,
     'L0_ffn_w_down': 8.0,
     'L0_ffn_w_shared_gate': 63.29,
     'L1_ffn_gate_w': 22.721,
     'L1_ffn_w_gate': 23.402,
     'L1_ffn_w_up': 8.0,
     'L1_ffn_w_down': 8.0,
     'L1_ffn_sw_gate': 21.616,
     'L1_ffn_sw_down': 21.408,
     'L0_ffn_sw_gate': 6.094,
     'L0_ffn_sw_up': 5.609,
     'L0_ffn_sw_down': 5.566,
     'L1_xattn_time_decay': 8.0,
     'L1_xattn_time_first': 8.0,
     'L1_ffn_sw_up': 8.0}
    for name, (base, spread) in spreads.items():
        noise = np.random.default_rng([zlib.crc32(name.encode()), seed]).standard_normal(out[name].shape)
        drawn = base * np.exp(spread * noise) if base else spread * noise
        out[name] = jnp.asarray(drawn.astype(out[name].dtype))
    for name, factor in factors.items():
        out[name] = (out[name] * factor).astype(out[name].dtype)
    return out
```

```python
from contextlib import ExitStack, contextmanager

import numpy as np

import concourse.bass as bass
from concourse import mybir

ALU = mybir.AluOpType
ACT = mybir.ActivationFunctionType
AX = mybir.AxisListType
F32 = mybir.dt.float32
BF16 = mybir.dt.bfloat16
F16 = mybir.dt.float16
U8 = mybir.dt.uint8
U16 = mybir.dt.uint16
U32 = mybir.dt.uint32
ds = bass.ds

P = 128
ROUND = 12582912.0
LN_EPS = 1e-5
RMS_EPS = 1e-6
FAR = float(1 << 20)


class Mark:

    def __init__(self, name, rel, loop):
        self.name, self.rel, self.loop = name, rel, loop


class Loop:
    def __init__(self, number, i, n, per, start):
        self.number, self.i, self.n, self.per, self.start, self.open = number, i, n, per, start, True


class Ledger:

    HEAD_START = 1024

    def __init__(self, nc, ctx):
        self.nc = nc
        self.engines = {"pe": nc.tensor, "dve": nc.vector, "act": nc.scalar, "pool": nc.gpsimd, "sp": nc.sync}
        self.sem = {n: ctx.enter_context(nc.semaphore(f"finished_{n}")) for n in ("pe", "dve", "act", "pool")}
        self.count = {n: self.HEAD_START for n in self.sem}
        self.loop = None
        self.loops = 0
        self.seen = {}
        for n in self.sem:
            self.engines[n].sem_inc(self.sem[n], self.HEAD_START)

    def done(self, name, instruction):
        self.count[name] += 1
        instruction.then_inc(self.sem[name], 1)
        return Mark(name, self.count[name], self.loop)

    def wait(self, waiter, marks, back=0):
        best = {}
        for m in marks:
            if m is None:
                continue
            key = (m.name, m.loop.number if m.loop else 0)
            if key not in best or best[key].rel < m.rel:
                best[key] = m
        for m in best.values():
            lp = m.loop
            if lp is None:
                known, value = m.rel, m.rel
            elif lp.open:
                known, value = None, lp.i * lp.per[m.name] + (lp.start[m.name] + m.rel - back * lp.per[m.name])
            else:
                known = value = lp.start[m.name] + (lp.n - 1) * lp.per[m.name] + m.rel
            key = (waiter, m.name)
            if known is not None:
                if self.seen.get(key, 0) >= known:
                    continue
                self.seen[key] = known
            else:
                key = (waiter, m.name, lp.number)
                if self.seen.get(key, -10**9) >= m.rel - back * lp.per[m.name]:
                    continue
                self.seen[key] = m.rel - back * lp.per[m.name]
            self.engines[waiter].wait_ge(self.sem[m.name], value)

    def run(self, name, after, build):
        self.wait(name, after)
        return self.done(name, build(self.engines[name]))

    @contextmanager
    def repeat(self, n, **per):
        per = {e: per.get(e, 0) for e in self.sem}
        start = dict(self.count)
        with self.nc.Fori(0, n) as i:
            self.loops += 1
            self.loop = Loop(self.loops, i, n, per, start)
            self.count = {e: 0 for e in self.sem}
            yield i
            assert self.count == per, f"counts in one iteration: {self.count}"
        self.loop.open = False
        self.loop = None
        self.count = {e: start[e] + n * per[e] for e in self.sem}

    def meet(self):
        marks = [Mark(n, self.count[n], None) for n in self.sem]
        for waiter in self.engines:
            self.wait(waiter, marks)


def program(nc, a, out, stop=None):
    x, ctx_in = a["x"], a["ctx_2048"]
    B, T, C = x.shape
    NT = B
    NTOK = NT * T
    H = 16
    HD = C // H
    CK = C // P
    NPAIR = H // 2
    KB = 64
    E0, K0, F0 = a["L0_ffn_w_gate"].shape[0], 4, a["L0_ffn_w_gate"].shape[2]
    CAP = 128
    FS0 = a["L0_ffn_sw_gate"].shape[1]
    E1, K1, F1 = a["L1_ffn_w_gate"].shape[0], 2, a["L1_ffn_w_gate"].shape[2]
    FS1 = a["L1_ffn_sw_gate"].shape[1]
    FC = F0 // 2
    G = 4
    NG = NT // G
    assert T == P and F0 == F1 and CK == 2 and NTOK == 2048

    dispatched = nc.dram_tensor("dispatched_rows", [E0 * CAP, C], F32).ap()
    answered = nc.dram_tensor("answered_rows", [E0 * CAP, C], F32).ap()

    with ExitStack() as whole:
        led = Ledger(nc, whole)

        def sem(name):
            return whole.enter_context(nc.semaphore(name))

        def dve(after, build):
            return led.run("dve", after, build)

        def act(after, build):
            return led.run("act", after, build)

        def pool(after, build):
            return led.run("pool", after, build)

        def buffers(stack):
            return lambda name, shape, dt=F32: stack.enter_context(nc.sbuf_tensor(name, shape, dt))

        sb = buffers(whole)
        bank = whole.enter_context(nc.psum_tensor("bank", [P, 8, 512], F32))

        def flat(b0, b1):
            return bank[:, b0:b1, :].rearrange("p b n -> p (b n)")

        def matmuls(after, groups):
            led.wait("pe", after)
            for dst, terms in groups:
                for n, (lhsT, rhs) in enumerate(terms):
                    mm = nc.tensor.matmul(dst, lhsT, rhs, start=(n == 0), stop=(n == len(terms) - 1))
            return led.done("pe", mm)

        def transposes(after, pairs, ident):
            led.wait("pe", after)
            for dst, src in pairs:
                mm = nc.tensor.transpose(dst, src, ident)
            return led.done("pe", mm)

        def previous_iteration(waiter, *names):
            for n in names:
                led.wait(waiter, [Mark(n, led.loop.per[n], led.loop)], back=1)

        x_sb = sb("x_sb", [P, NT, C])
        ctxT = sb("ctxT", [P, CK, NTOK])
        ident = sb("ident", [P, P])
        ident_b = sb("ident_b", [P, P], BF16)
        ones_row = sb("ones_row", [1, P])
        eps_ln = sb("eps_ln", [P, 1])
        eps_rms = sb("eps_rms", [P, 1])
        gates = sb("gates", [P, 4])
        tgates = sb("tgates", [P, 4])
        stats = sb("stats", [P, NT, 6])
        mv = sb("mv", [P, NT, 2])
        std = sb("std", [P, NT])
        rstd = sb("rstd", [P, NT])
        nmr = sb("nmr", [P, NT])

        s_x, s_ctx, s_wa, s_g = sem("x_loaded"), sem("ctx_loaded"), sem("attention_weights_loaded"), sem("gates_loaded")
        s_zero = sem("dispatched_rows_zeroed")

        xr = x.rearrange("t p c -> p t c")
        cr = ctx_in.rearrange("t p c -> p t c")
        outr = out.rearrange("t p c -> p t c")

        with ExitStack() as attention:
            sa = buffers(attention)
            kT = sa("kT", [P, NPAIR, NTOK], BF16)
            qT_all = sa("qT_all", [P, NPAIR, (NT + 1) * P], BF16)
            v_sb = sa("v_sb", [P, NT, C], BF16)
            sq_all = sa("sq_all", [P, (NT + 1) * H])
            nsq_all = sa("nsq_all", [P, (NT + 1) * H])
            wp = sa("wp", [P, CK, C])
            bp_row = sa("bp_row", [1, C])

            with ExitStack() as prepare:
                sp_ = buffers(prepare)
                ctx_sb = sp_("ctx_sb", [P, NT, C])
                vT = sp_("vT", [P, CK, NTOK])
                wq, wkv = sp_("wq", [P, CK, C]), sp_("wkv", [P, CK, 2 * C])
                bq_row, bk_row = sp_("bq_row", [1, C]), sp_("bk_row", [1, C])
                bv = sp_("bv", [P, CK])
                xn = sp_("xn", [P, G, C])
                xnT = sp_("xnT", [P, CK, G * P])
                cT = sp_("cT", [P, CK, G * P])
                y1, y2 = sp_("y1", [P, G, C]), sp_("y2", [P, G, C])
                qint = sp_("qint", [P, G, C], BF16)
                qrep = sp_("qrep", [P, G, H, KB], BF16)
                ksplit = sp_("ksplit", [P, G, H, KB], BF16)
                small = sp_("small", [P, 6, G * H])

                for g in range(NG):
                    nc.sync.dma_start(x_sb[:, g * G:(g + 1) * G, :], xr[:, g * G:(g + 1) * G, :]).then_inc(s_x, 16)
                    nc.scalar.dma_start(ctx_sb[:, g * G:(g + 1) * G, :], cr[:, g * G:(g + 1) * G, :]).then_inc(s_ctx, 16)
                nc.sync.dma_start(wq[:], a["L0_xattn_Wq"].rearrange("(c p) n -> p c n", p=P)).then_inc(s_wa, 16)
                nc.sync.dma_start(wkv[:], a["L0_xattn_Wkv"].rearrange("(c p) n -> p c n", p=P)).then_inc(s_wa, 16)
                nc.sync.dma_start(wp[:], a["L0_xattn_Wp"].rearrange("(c p) n -> p c n", p=P)).then_inc(s_wa, 16)
                nc.sync.dma_start(bq_row[:], a["L0_xattn_bq"].rearrange("(a n) -> a n", a=1)).then_inc(s_wa, 16)
                nc.sync.dma_start(bk_row[:], a["L0_xattn_bkv"][0:C].rearrange("(a n) -> a n", a=1)).then_inc(s_wa, 16)
                with nc.allow_non_contiguous_dma(reason="256 biases, one per partition"):
                    nc.sync.dma_start(bv[:], a["L0_xattn_bkv"][C:2 * C].rearrange("(c p) -> p c", p=P)).then_inc(s_wa, 16)
                nc.sync.dma_start(bp_row[:], a["L0_xattn_bp"].rearrange("(a n) -> a n", a=1)).then_inc(s_wa, 16)
                nc.sync.dma_start(gates[:, 0:2], a["g_xattn"].partition_broadcast(P)).then_inc(s_g, 16)
                nc.sync.dma_start(gates[:, 2:4], a["g_ffn"].partition_broadcast(P)).then_inc(s_g, 16)

                m = pool([], lambda e: e.memset(ident[:], 0.0))
                m_id = pool([m], lambda e: e.affine_select(out=ident[:], in_=ident[:], compare_op=ALU.not_equal, fill=1.0,
                                                           base=0, pattern=[[-1, P]], channel_multiplier=1))
                m_idb = pool([m_id], lambda e: e.tensor_copy(ident_b[:], ident[:]))
                pool([], lambda e: e.memset(ones_row[:], 1.0))
                m_pad = [pool([], lambda e: e.memset(qrep[:, :, :, 3 * HD:KB], 0.0)),
                         pool([], lambda e: e.memset(ksplit[:, :, :, 3 * HD:KB], 0.0)),
                         pool([], lambda e: e.memset(qT_all[:, :, NT * P:], 0.0)),
                         pool([], lambda e: e.memset(sq_all[:, NT * H:], 0.0)),
                         pool([], lambda e: e.memset(nsq_all[:, NT * H:], 0.0))]
                m_eps = dve([], lambda e: e.memset(eps_ln[:], LN_EPS))
                dve([], lambda e: e.memset(eps_rms[:], RMS_EPS))

                def layer_stats(ready):
                    led.wait("dve", ready)
                    for t in range(NT):
                        m = dve([], lambda e: e.bn_stats(stats[:, t, :], x_sb[:, t, :]))
                    led.wait("dve", [m])
                    for t in range(NT):
                        m = dve([], lambda e: e.bn_aggr(mv[:, t, :], stats[:, t, :]))
                    m = act([m, m_eps], lambda e: e.activation(std[:], mv[:, :, 1], ACT.Sqrt, bias=eps_ln[:], scale=1.0))
                    m = dve([m], lambda e: e.reciprocal(rstd[:], std[:]))
                    return dve([m], lambda e: e.scalar_tensor_tensor(nmr[:], mv[:, :, 0], -1.0, rstd[:], ALU.mult, ALU.mult))

                nc.vector.wait_ge(s_x, 16 * NG)
                m_stats = layer_stats([])

                for e in ("pe", "act", "dve", "pool"):
                    led.engines[e].wait_ge(s_wa, 16 * 7)
                led.wait("pe", [m_idb])
                nc.gpsimd.wait_ge(s_ctx, 16 * NG)
                led.wait("act", m_pad)
                led.wait("pool", m_pad)
                with led.repeat(NG, pe=13, dve=25, act=13, pool=3) as i:
                    previous_iteration("dve", "pe", "act", "pool")
                    previous_iteration("pe", "act", "dve")
                    previous_iteration("act", "pe", "pool", "dve")
                    previous_iteration("pool", "pe", "dve", "act")
                    for k in range(G):
                        m_xn = dve([m_stats], lambda e: e.tensor_scalar(xn[:, k, :], x_sb[:, i * G + k, :], rstd[:, ds(i * G + k, 1)],
                                                                         nmr[:, ds(i * G + k, 1)], ALU.mult, ALU.add))
                    m_x = transposes([m_xn], [(flat(0, 2)[:, (c * G + k) * P:(c * G + k + 1) * P], xn[:, k, c * P:(c + 1) * P])
                                              for c in range(CK) for k in range(G)], ident[:])
                    m_cs = pool([], lambda e: e.tensor_copy(y1[:], ctx_sb[:, ds(i * G, G), :]))
                    m_c = transposes([m_cs], [(flat(2, 4)[:, (c * G + k) * P:(c * G + k + 1) * P], y1[:, k, c * P:(c + 1) * P])
                                              for c in range(CK) for k in range(G)], ident[:])
                    m_xT = act([m_x], lambda e: e.copy(xnT[:].rearrange("p c n -> p (c n)"), flat(0, 2)))
                    m_cT = act([m_c], lambda e: e.copy(cT[:].rearrange("p c n -> p (c n)"), flat(2, 4)))
                    m_cT2 = pool([m_cT], lambda e: e.tensor_copy(ctxT[:, :, ds(i * G * P, G * P)], cT[:]))

                    def project(m_in, srcT, w, c0, bias, banks):
                        return matmuls(m_in, [(flat(*banks)[:, k * C:(k + 1) * C],
                                               [(ones_row[:], bias[:])] + [(srcT[:, c, k * P:(k + 1) * P], w[:, c, c0:c0 + C]) for c in range(CK)])
                                              for k in range(G)])

                    m_q = project([m_xT], xnT, wq, 0, bq_row, (4, 6))
                    m_k = project([m_cT], cT, wkv, 0, bk_row, (6, 8))
                    m_v = matmuls([], [(bank[:, c, :], [(wkv[:, k, C + c * P:C + (c + 1) * P], cT[:, k, :]) for k in range(CK)]) for c in range(CK)])
                    for c in range(CK):
                        m_vT = act([m_v], lambda e: e.activation(vT[:, c, ds(i * G * P, G * P)], bank[:, c, :], ACT.Identity,
                                                                 bias=bv[:, c:c + 1], scale=1.0))

                    def quantise(m_in, banks, premult, n):
                        src = flat(*banks).rearrange("p (t h d) -> p (t h) d", t=G, h=H)
                        y = y1[:].rearrange("p t (h d) -> p (t h) d", h=H)
                        am, sc, rc = small[:, n, :], small[:, n + 1, :], small[:, n + 2, :]
                        m = dve([m_in], lambda e: e.tensor_reduce(am, src, AX.X, ALU.max, apply_absolute_value=True))
                        m_s = dve([m], lambda e: e.tensor_scalar(sc, am, premult / 127.0, 1e-8, ALU.mult, ALU.max))
                        m = dve([m_s], lambda e: e.reciprocal(rc, sc))
                        if premult != 1.0:
                            m = dve([m], lambda e: e.tensor_scalar(rc, rc, premult, None, ALU.mult))
                        m = dve([m, m_c], lambda e: e.tensor_tensor(y, src, rc.unsqueeze(2).broadcast_to([P, G * H, HD]), ALU.mult))
                        m = dve([m], lambda e: e.tensor_scalar(y, y, 127.0, -127.0, ALU.min, ALU.max))
                        return sc, m_s, m

                    sc, m_s, m = quantise(m_q, (4, 6), 0.25, 0)
                    m_sq = pool([m_s], lambda e: e.tensor_copy(sq_all[:, ds(i * G * H, G * H)], sc))
                    dve([m_s], lambda e: e.tensor_scalar(nsq_all[:, ds(i * G * H, G * H)], sc, -1.0, None, ALU.mult))
                    m = dve([m], lambda e: e.tensor_scalar(qint[:], y1[:], ROUND, -ROUND, ALU.add, ALU.add))
                    for r in range(3):
                        m_qr = act([m], lambda e: e.copy(qrep[:, :, :, r * HD:(r + 1) * HD].rearrange("p t h d -> p (t h) d"),
                                                         qint[:].rearrange("p t (h d) -> p (t h) d", h=H)))

                    sc, m_s, m = quantise(m_k, (6, 8), 1.0, 3)
                    m = dve([m], lambda e: e.tensor_scalar(y1[:], y1[:], ROUND, -ROUND, ALU.add, ALU.add))
                    y1h = y1[:].rearrange("p t (h d) -> p (t h) d", h=H)
                    y2h = y2[:].rearrange("p t (h d) -> p (t h) d", h=H)
                    part = [ksplit[:, :, :, r * HD:(r + 1) * HD].rearrange("p t h d -> p (t h) d") for r in range(3)]
                    m = dve([m], lambda e: e.tensor_tensor(y1h, y1h, sc.unsqueeze(2).broadcast_to([P, G * H, HD]), ALU.mult))
                    m_hi = act([m], lambda e: e.copy(part[0], y1h))
                    m = dve([m_hi], lambda e: e.tensor_tensor(y2h, y1h, part[0], ALU.subtract))
                    m_mid = act([m], lambda e: e.copy(part[1], y2h))
                    m = dve([m_mid], lambda e: e.tensor_tensor(part[2], y2h, part[1], ALU.subtract))
                    m_ks = m

                    def turn(m_in, free, src, banks, put):
                        for k in range(G):
                            view = bank[:, banks[k], :].bitcast(BF16)
                            mt = transposes([m_in, free[k]], [(view[:, p * P:(p + 1) * P], src[:, k, 2 * p:2 * p + 2, :].rearrange("p h d -> p (h d)"))
                                                              for p in range(NPAIR)], ident_b[:])
                            put(k, mt, view.rearrange("p (a n) -> p a n", a=NPAIR))

                    turned = {}

                    def put_q(k, mt, view):
                        turned[k] = act([mt], lambda e: e.copy(qT_all[:, :, ds(i * G * P + k * P, P)], view))

                    def put_k(k, mt, view):
                        dve([mt], lambda e: e.tensor_copy(kT[:, :, ds(i * G * P + (k // 2) * 2 * P + k % 2, P, step=2)], view))

                    turn(m_qr, [m_cT, m_cT, m_ks, m_ks], qrep, (2, 3, 4, 5), put_q)
                    turn(m_ks, [m_ks, m_ks, m_vT, m_vT], ksplit, (6, 7, 0, 1), put_k)
                led.meet()

                sv, rv = small[:, 0, 0:CK], small[:, 1, 0:CK]
                m = dve([], lambda e: e.tensor_reduce(sv, vT[:], AX.X, ALU.max, apply_absolute_value=True))
                m_sv = dve([m], lambda e: e.tensor_scalar(sv, sv, 1.0 / 127.0, 1e-8, ALU.mult, ALU.max))
                m = dve([m_sv], lambda e: e.reciprocal(rv, sv))
                vint = ctx_sb[:].rearrange("p t c -> p (t c)").bitcast(BF16)[:, 0:CK * NTOK].rearrange("p (c n) -> p c n", c=CK)
                for c in range(CK):
                    mc = dve([m], lambda e: e.tensor_scalar(vT[:, c, :], vT[:, c, :], rv[:, c:c + 1], 127.0, ALU.mult, ALU.min))
                    mc = dve([mc], lambda e: e.tensor_scalar(vT[:, c, :], vT[:, c, :], -127.0, ROUND, ALU.max, ALU.add))
                    mc = dve([mc], lambda e: e.tensor_scalar(vint[:, c, :], vT[:, c, :], -ROUND, None, ALU.add))
                    for b in range(2):
                        view = bank[:, 2 * c + b, :].bitcast(BF16)
                        mt = transposes([mc], [(view[:, k * P:(k + 1) * P], vint[:, c, (8 * b + k) * P:(8 * b + k + 1) * P]) for k in range(8)], ident_b[:])
                        act([mt], lambda e: e.copy(v_sb[:, 8 * b:8 * b + 8, c * P:(c + 1) * P], view.rearrange("p (k n) -> p k n", k=8)))
                    dve([m_sv], lambda e: e.tensor_scalar(wp[:, c, :], wp[:, c, :], sv[:, c:c + 1], None, ALU.mult))
                nc.scalar.wait_ge(s_g, 32)
                act([], lambda e: e.activation(tgates[:], gates[:], ACT.Tanh))
                led.meet()

            attn = sa("attn", [P, NT + 1, C])
            q_cur = sa("q_cur", [P, H, P], BF16)
            prob = sa("prob", [P, 2, NTOK], U16)
            probT = sa("probT", [P, 2, NTOK], BF16)
            top = sa("top", [P, 2, 2])
            shift = sa("shift", [P, 2])
            bias = sa("bias", [P, 2])
            norm = sa("norm", [P, H, 2])
            rnorm = sa("rnorm", [P, H])
            zeros = sa("zeros", [P, 1024])

            HALF = NTOK // 2
            LN255 = float(np.log(255.0))
            score = [flat(2 * b, 2 * b + 2) for b in range(3)]
            tbank = bank[:, 6, :]
            obank = bank[:, 7, 0:C]

            s_qk = sem("scores_ready")
            s_exp = sem("exp_finished")
            s_bias = sem("bias_ready")
            s_t0, s_t1 = sem("half0_transposed"), sem("half1_transposed")
            s_e0, s_e1 = sem("half0_evacuated"), sem("half1_evacuated")
            s_o, s_ofree = sem("outputs_ready"), sem("outputs_taken")
            s_qfree, s_qcur = sem("head_multiplied"), sem("query_pair_copied")
            s_v = sem("vector_finished")

            m_z = pool([], lambda e: e.memset(zeros[:], 0.0))
            led.wait("sp", [m_z])
            for r in range(E0 * CAP // 512):
                nc.sync.dma_start(dispatched[512 * r:512 * (r + 1), :].rearrange("(p f) c -> p (f c)", p=P), zeros[:]).then_inc(s_zero, 16)

            m = [pool([], lambda e: e.memset(q_cur[:], 0.0)),
                 dve([], lambda e: e.memset(prob[:], 0x6400)),
                 dve([], lambda e: e.memset(probT[:], 0.0)),
                 dve([], lambda e: e.memset(norm[:], 1.0)),
                 dve([], lambda e: e.memset(rnorm[:], 1.0)),
                 dve([], lambda e: e.memset(tbank, 0.0)),
                 dve([], lambda e: e.memset(obank, 0.0))]
            for p in range(NPAIR):
                pool(m, lambda e: e.tensor_copy(q_cur[0:KB, 2 * p, :], qT_all[0:KB, p, 0:P]))
                mq = pool(m, lambda e: e.tensor_copy(q_cur[KB:P, 2 * p + 1, :], qT_all[KB:P, p, 0:P]))
            led.meet()

            def scores(g, u):
                for v in range(2):
                    k0 = u * HALF + v * 512
                    mm = nc.tensor.matmul(score[(2 * g + u) % 3][:, v * 512:(v + 1) * 512], q_cur[:, g, :], kT[:, g // 2, k0:k0 + 512],
                                          start=True, stop=True)
                mm.then_inc(s_qk, 1)

            def maximum(g, u):
                nc.vector.tensor_reduce(top[:, g % 2, u:u + 1], score[(2 * g + u) % 3], AX.X, ALU.max).then_inc(s_v, 1)

            def make_bias(g, t, n):
                nc.vector.wait_ge(s_v, n)
                nc.vector.scalar_tensor_tensor(shift[:, g % 2:g % 2 + 1], top[:, g % 2, 0:1], top[:, g % 2, 1:2],
                                               nsq_all[:, ds(t * H + g, 1)], ALU.max, ALU.mult).then_inc(s_v, 1)
                nc.vector.wait_ge(s_v, n + 1)
                nc.vector.tensor_scalar(bias[:, g % 2:g % 2 + 1], shift[:, g % 2:g % 2 + 1], LN255, None, ALU.add).then_inc(s_bias, 1)

            def exponentials(g, u, t):
                low = prob[:, g % 2, :].bitcast(U8)[:, u * NTOK:(u + 1) * NTOK:2]
                nc.scalar.activation(low, score[(2 * g + u) % 3], ACT.Exp, bias=bias[:, g % 2:g % 2 + 1],
                                     scale=sq_all[:, ds(t * H + g, 1)], accum_out=norm[:, g, u:u + 1]).then_inc(s_exp, 1)

            def transpose_half(h, u, signal):
                words = prob[:, h % 2, :].bitcast(F32)
                for c in range(4):
                    mm = nc.tensor.transpose(tbank[:, c * P:(c + 1) * P], words[:, (4 * u + c) * P:(4 * u + c + 1) * P], ident[:])
                mm.then_inc(signal, 1)

            def values(h):
                pt = probT[:, h % 2, :].rearrange("p (c q two) -> p c q two", c=8, two=2)
                for r in range(NT):
                    mm = nc.tensor.matmul(obank[:, h * HD:(h + 1) * HD], pt[:, r // 2, :, r % 2], v_sb[:, r, h * HD:(h + 1) * HD],
                                          start=(r == 0), stop=(r == NT - 1))
                return mm

            def take_outputs(slot):
                nc.vector.tensor_tensor(attn[:, slot, :].rearrange("p (h d) -> p h d", h=H), obank.rearrange("p (h d) -> p h d", h=H),
                                        rnorm[:].unsqueeze(2).broadcast_to([P, H, HD]), ALU.mult).then_inc(s_ofree, 1)

            def normaliser(h0, n):
                nc.vector.tensor_tensor(rnorm[:, h0:h0 + 8], norm[:, h0:h0 + 8, 0], norm[:, h0:h0 + 8, 1], ALU.add).then_inc(s_v, 1)
                nc.vector.wait_ge(s_v, n + 1)
                nc.vector.reciprocal(rnorm[:, h0:h0 + 8], rnorm[:, h0:h0 + 8]).then_inc(s_v, 1)

            for j in range(3):
                scores(j // 2, j % 2)
            for j in range(3):
                nc.vector.wait_ge(s_qk, j + 1)
                maximum(j // 2, j % 2)
                if j == 1:
                    make_bias(0, 0, 2)
            nc.vector.nop().then_inc(s_qk, -3)
            nc.vector.wait_ge(s_v, 4)
            nc.vector.nop().then_inc(s_v, -4)
            nc.tensor.nop().then_inc(s_t1, 1)
            nc.gpsimd.nop().then_inc(s_qcur, H)

            with nc.Fori(0, NT) as t:
                n_v = 0
                for h in range(H):
                    g, tg = (h + 1, t) if h + 1 < H else (0, t + 1)
                    g2 = h + 2 if h + 2 < H else h + 2 - H

                    pe = nc.tensor
                    pe.wait_ge(s_exp, 2 * h + 1 if h < H - 1 else 2 * H)
                    if h == H - 1:
                        pass
                    scores(g, 1)
                    pe.wait_ge(s_e1, h + 1)
                    transpose_half(h, 0, s_t0)
                    if h == 1:
                        pe.wait_ge(s_ofree, 1)
                    mm = values((h - 1) % H)
                    mm.then_inc(s_o if h == 0 else s_qfree, 1)
                    pe.wait_ge(s_exp, 2 * h + 2 if h < H - 2 else 2 * h + 3 if h == H - 2 else 2 * H)
                    if g2 % 2 == 0:
                        pe.wait_ge(s_qcur, H + 2 if g2 == 0 else g2 + 2)
                    scores(g2, 0)
                    pe.wait_ge(s_exp, min(2 * h + 2, 2 * H))
                    pe.wait_ge(s_e0, h + 1)
                    transpose_half(h, 1, s_t1)

                    ve = nc.vector
                    ve.wait_ge(s_qk, 2 * h + 1)
                    maximum(g, 1)
                    n_v += 1
                    make_bias(g, tg, n_v)
                    n_v += 1
                    ve.wait_ge(s_t0, h + 1)
                    ve.tensor_scalar(probT[:, h % 2, 0:HALF], tbank.bitcast(F16), -1024.0, None, ALU.add).then_inc(s_e0, 1)
                    if h == 0:
                        normaliser(8, n_v)
                        n_v += 2
                        ve.wait_ge(s_v, n_v)
                        ve.wait_ge(s_o, 1)
                        take_outputs(t)
                    if h == 9:
                        normaliser(0, n_v)
                        n_v += 2
                    ve.wait_ge(s_qk, 2 * h + 2)
                    maximum(g2, 0)
                    n_v += 1

                    ac = nc.scalar
                    ac.wait_ge(s_bias, h + 1)
                    exponentials(h, 0, t)
                    ac.wait_ge(s_t1, h + 1)
                    ac.activation(probT[:, (h - 1) % 2, HALF:], tbank.bitcast(F16), ACT.Copy, bias=-1024.0).then_inc(s_e1, 1)
                    exponentials(h, 1, t)

                    if h % 2 == 0:
                        p = h // 2
                        po = nc.gpsimd
                        po.wait_ge(s_qfree, max(1, h))
                        po.tensor_copy(q_cur[0:KB, h, :], qT_all[0:KB, p, ds(t * P + P, P)]).then_inc(s_qcur, 1)
                        po.tensor_copy(q_cur[KB:P, h + 1, :], qT_all[KB:P, p, ds(t * P + P, P)]).then_inc(s_qcur, 1)

                ve.wait_ge(s_v, n_v)
                for e, s, n in ((pe, s_exp, 2 * H), (pe, s_e1, H), (pe, s_e0, H), (pe, s_ofree, 1), (pe, s_qcur, H),
                                (ve, s_qk, 2 * H), (ve, s_t0, H), (ve, s_o, 1), (ve, s_v, n_v),
                                (ac, s_bias, H), (ac, s_t1, H), (po, s_qfree, H - 1)):
                    if s is s_qfree:
                        po.wait_ge(s_qfree, H - 1)
                    e.nop().then_inc(s, -n)

            nc.scalar.wait_ge(s_t1, 1)
            m = act([], lambda e: e.activation(probT[:, 1, HALF:], tbank.bitcast(F16), ACT.Copy, bias=-1024.0))
            led.wait("pe", [m])
            nc.tensor.wait_ge(s_qcur, H)
            m_o = led.done("pe", values(H - 1))
            nc.vector.tensor_tensor(rnorm[:, 8:16], norm[:, 8:16, 0], norm[:, 8:16, 1], ALU.add).then_inc(s_v, 1)
            nc.vector.wait_ge(s_v, 1)
            m = dve([], lambda e: e.reciprocal(rnorm[:, 8:16], rnorm[:, 8:16]))
            led.wait("dve", [m, m_o])
            take_outputs(NT)
            dve([], lambda e: e.memset(top[:], 0.0))
            led.wait("pool", [m_o])
            pool([], lambda e: e.memset(q_cur[:, 0, 0:1], 0.0))
            led.meet()

            a_g = sa("a_g", [P, G, C])
            aT = sa("aT", [P, CK, G * P])
            with led.repeat(NG, pe=2, act=1, dve=G, pool=1) as i:
                previous_iteration("pe", "act", "dve")
                previous_iteration("act", "pe")
                previous_iteration("pool", "pe")
                m = pool([], lambda e: e.tensor_copy(a_g[:], attn[:, ds(i * G + 1, G), :]))
                m = transposes([m], [(flat(0, 2)[:, (c * G + k) * P:(c * G + k + 1) * P], a_g[:, k, c * P:(c + 1) * P])
                                     for k in range(G) for c in range(CK)], ident[:])
                m = act([m], lambda e: e.copy(aT[:].rearrange("p c n -> p (c n)"), flat(0, 2)))
                m = matmuls([m], [(flat(2, 4)[:, k * C:(k + 1) * C],
                                   [(ones_row[:], bp_row[:])] + [(aT[:, c, k * P:(k + 1) * P], wp[:, c, :]) for c in range(CK)]) for k in range(G)])
                for k in range(G):
                    dve([m], lambda e: e.scalar_tensor_tensor(x_sb[:, i * G + k, :], flat(2, 4)[:, k * C:(k + 1) * C], tgates[:, 0:1],
                                                              x_sb[:, i * G + k, :], ALU.mult, ALU.add))
            led.meet()

        def load(s, dst, src):
            nc.sync.dma_start(dst, src).then_inc(s, 16)

        def silu_times_up(after, rhs, gate_w, up_w, widths, hT, sil, free):
            mh = None
            for c, w in enumerate(widths):
                b = free["n"] % 2
                free["n"] += 1
                mg = matmuls(after + [free["gate", b]], [(bank[0:w, b, :], [(gate_w(c, k), rhs(k)) for k in range(CK)])])
                mu = matmuls([free["up", b]], [(bank[0:w, 2 + b, :], [(up_w(c, k), rhs(k)) for k in range(CK)])])
                ms = act([mg, free["up", b]], lambda e: e.activation(sil[0:w, b, :], bank[0:w, b, :], ACT.Silu))
                mh = dve([ms, mu, free["hidden"]], lambda e: e.tensor_tensor(hT[0:w, c, :], sil[0:w, b, :], bank[0:w, 2 + b, :], ALU.mult))
                free["gate", b], free["up", b] = ms, mh
            return mh

        def nothing_read():
            return {("gate", 0): None, ("gate", 1): None, ("up", 0): None, ("up", 1): None, "hidden": None, "n": 0}

        def top_experts(sr, logits, E, K, tag):
            pr = sr(tag + "pr", [P, NT, E])
            top8, idx8 = sr(tag + "top8", [P, NT, 8]), sr(tag + "idx8", [P, NT, 8], U32)
            idxf, iota_i, iota_f = sr(tag + "idxf", [P, NT * K]), sr(tag + "iota_i", [P, E], U32), sr(tag + "iota_f", [P, E])
            hot = sr(tag + "hot", [P, NT * K, E])
            r1, r2 = sr(tag + "r1", [P, NT]), sr(tag + "r2", [P, NT])
            mi = pool([], lambda e: e.iota(iota_i[:], pattern=[[1, E]], base=0, channel_multiplier=0))
            mi = pool([mi], lambda e: e.tensor_copy(iota_f[:], iota_i[:]))
            m = dve([], lambda e: e.tensor_reduce(r1[:], logits, AX.X, ALU.max))
            m = dve([m], lambda e: e.tensor_tensor(pr[:], logits, r1[:].unsqueeze(2).broadcast_to([P, NT, E]), ALU.subtract))
            m = act([m], lambda e: e.activation(pr[:], pr[:], ACT.Exp))
            m = dve([m], lambda e: e.tensor_reduce(r2[:], pr[:], AX.X, ALU.add))
            m = dve([m], lambda e: e.reciprocal(r2[:], r2[:]))
            m = dve([m], lambda e: e.tensor_tensor(pr[:], pr[:], r2[:].unsqueeze(2).broadcast_to([P, NT, E]), ALU.mult))
            led.wait("dve", [m])
            for t in range(NT):
                m = dve([], lambda e: e.max(top8[:, t, :], pr[:, t, :]))
            led.wait("dve", [m])
            for t in range(NT):
                m = dve([], lambda e: e.max_index(idx8[:, t, :], top8[:, t, :], pr[:, t, :]))
            m = dve([m], lambda e: e.tensor_copy(idxf[:].rearrange("p (t k) -> p t k", k=K), idx8[:, :, 0:K]))
            m = dve([m, mi], lambda e: e.tensor_tensor(hot[:], iota_f[:].unsqueeze(1).broadcast_to([P, NT * K, E]),
                                                       idxf[:].unsqueeze(2).broadcast_to([P, NT * K, E]), ALU.is_equal))
            return top8, hot, m

        s_wf, s_wn = sem("ffn0_weights_loaded"), sem("ffn0_norm_loaded")
        s_scatter = sem("rows_dispatched")
        WID0 = [P] * -(-FS0 // P)
        with ExitStack() as ffn:
            sf = buffers(ffn)
            acc = sf("acc", [P, NT, C])
            xT = sf("xT", [P, CK, NTOK])
            logits = sf("logits", [P, NT, E0 + 1])
            wrt = sf("wrt", [P, CK, E0 + 1])
            wn = sf("wn", [P, C])
            dest = sf("dest", [P, NT, K0], U32)
            wts = sf("wts", [P, NT, K0])
            sgate = sf("sgate", [P, NT])
            ss = sf("ss", [P, NT])
            rinv = sf("rinv", [P, NT])

            load(s_wn, wn[:], a["L0_ffn_w_norm"].partition_broadcast(P))
            load(s_wn, wrt[:, :, 0:E0], a["L0_ffn_w_router"].rearrange("(c p) n -> p c n", p=P))
            with nc.allow_non_contiguous_dma(reason="256 weights, one column"):
                load(s_wn, wrt[:, :, E0:E0 + 1], a["L0_ffn_w_shared_gate"].rearrange("(c p) n -> p c n", p=P))

            with ExitStack() as shared:
                sh_ = buffers(shared)
                rows = sh_("rows", [P, NT, C])
                swg, swu = sh_("swg", [P, CK, len(WID0) * P]), sh_("swu", [P, CK, len(WID0) * P])
                swd = sh_("swd", [P, len(WID0), C])
                m = [pool([], lambda e: e.memset(swg[:, :, FS0:], 0.0)), pool([], lambda e: e.memset(swu[:, :, FS0:], 0.0)),
                     pool([], lambda e: e.memset(swd[:, FS0 // P, :], 0.0))]
                led.wait("sp", m)
                load(s_wf, swg[:, :, 0:FS0], a["L0_ffn_sw_gate"].rearrange("(c p) n -> p c n", p=P))
                load(s_wf, swu[:, :, 0:FS0], a["L0_ffn_sw_up"].rearrange("(c p) n -> p c n", p=P))
                full = FS0 // P * P
                load(s_wf, swd[:, 0:FS0 // P, :], a["L0_ffn_sw_down"][0:full, :].rearrange("(c p) n -> p c n", p=P))
                load(s_wf, swd[0:FS0 - full, FS0 // P, :], a["L0_ffn_sw_down"][full:, :])

                with ExitStack() as routing:
                    sr = buffers(routing)
                    xg, xgT = sr("xg", [P, G, C]), sr("xgT", [P, CK, G * P])
                    sqr = sr("sqr", [P, G, C])
                    m_stats = layer_stats([])
                    with led.repeat(NG, dve=4, act=4) as i:
                        for k in range(G):
                            m = dve([m_stats], lambda e: e.tensor_scalar(acc[:, i * G + k, :], x_sb[:, i * G + k, :], rstd[:, ds(i * G + k, 1)],
                                                                         nmr[:, ds(i * G + k, 1)], ALU.mult, ALU.add))
                        previous_iteration("act", "act")
                        for k in range(G):
                            m2 = act([m], lambda e: e.activation(sqr[:, k, :], acc[:, i * G + k, :], ACT.Square, accum_out=ss[:, ds(i * G + k, 1)]))
                    m = act([m2], lambda e: e.activation(ss[:], ss[:], ACT.Sqrt, bias=eps_rms[:], scale=1.0 / C))
                    m_r = dve([m], lambda e: e.reciprocal(rinv[:], ss[:]))
                    nc.vector.wait_ge(s_wn, 48)
                    nc.tensor.wait_ge(s_wn, 48)
                    with led.repeat(NG, pe=2, dve=5, act=1, pool=2) as i:
                        previous_iteration("dve", "pe", "pool")
                        previous_iteration("pe", "act", "dve")
                        previous_iteration("act", "pe", "pool")
                        for k in range(G):
                            m = dve([m_r], lambda e: e.scalar_tensor_tensor(xg[:, k, :], acc[:, i * G + k, :], rinv[:, ds(i * G + k, 1)], wn[:],
                                                                            ALU.mult, ALU.mult))
                        pool([m], lambda e: e.tensor_copy(rows[:, ds(i * G, G), :], xg[:]))
                        m = transposes([m], [(flat(0, 2)[:, (c * G + k) * P:(c * G + k + 1) * P], xg[:, k, c * P:(c + 1) * P])
                                             for c in range(CK) for k in range(G)], ident[:])
                        m = act([m], lambda e: e.copy(xgT[:].rearrange("p c n -> p (c n)"), flat(0, 2)))
                        pool([m], lambda e: e.tensor_copy(xT[:, :, ds(i * G * P, G * P)], xgT[:]))
                        m = matmuls([m], [(bank[:, 2, k * (E0 + 1):(k + 1) * (E0 + 1)], [(xgT[:, c, k * P:(k + 1) * P], wrt[:, c, :]) for c in range(CK)])
                                          for k in range(G)])
                        dve([m], lambda e: e.tensor_copy(logits[:, ds(i * G, G), :], bank[:, 2, 0:G * (E0 + 1)].rearrange("p (k n) -> p k n", k=G)))
                    led.meet()

                    before, every = sr("before", [P, P], BF16), sr("every", [P, P], BF16)
                    mask, prefix = sr("mask", [P, NT, E0], BF16), sr("prefix", [P, NT, E0], BF16)
                    first, slot, far = sr("first", [P, E0]), sr("slot", [P, NT, E0]), sr("far", [P, NT, E0])
                    first_i, picked = sr("first_i", [P, E0], U32), sr("picked", [P, NT * K0, E0])
                    destf = sr("destf", [P, NT * K0])
                    mc = pool([], lambda e: e.memset(every[:], 1.0))
                    mc = pool([mc], lambda e: e.affine_select(out=before[:], in_=every[:], compare_op=ALU.is_gt, fill=0.0, base=0,
                                                              pattern=[[1, P]], channel_multiplier=-1))
                    mf = pool([], lambda e: e.iota(first_i[:], pattern=[[CAP, E0]], base=0, channel_multiplier=0))
                    mf = pool([mf], lambda e: e.tensor_copy(first[:], first_i[:]))
                    top8, hot, m = top_experts(sr, logits[:, :, 0:E0], E0, K0, "r0_")
                    with nc.allow_low_precision(reason="counts up to 16 are exact in bfloat16"):
                        m = dve([m], lambda e: e.tensor_reduce(mask[:], hot[:].rearrange("p (t k) e -> p t e k", k=K0), AX.X, ALU.add))
                    m2 = dve([], lambda e: e.memset(prefix[:, 0, :], 0.0))
                    for t in range(1, NT):
                        m2 = dve([m, m2], lambda e: e.tensor_tensor(prefix[:, t, :], prefix[:, t - 1, :], mask[:, t - 1, :], ALU.add))
                    m = matmuls([m2, mc], [(bank[:, 7, :], [(before[:], mask[:].rearrange("p t e -> p (t e)")),
                                                            (every[:], prefix[:].rearrange("p t e -> p (t e)"))])])
                    place = bank[:, 7, :].rearrange("p (t e) -> p t e", e=E0)
                    m1 = dve([m], lambda e: e.tensor_scalar(far[:], place, float(CAP), FAR, ALU.is_ge, ALU.mult))
                    m = dve([mf], lambda e: e.tensor_tensor(slot[:], place, first[:].unsqueeze(1).broadcast_to([P, NT, E0]), ALU.add))
                    m = dve([m, m1], lambda e: e.tensor_tensor(slot[:], slot[:], far[:], ALU.add))
                    m = dve([m], lambda e: e.tensor_tensor(picked[:].rearrange("p (t k) e -> p t k e", k=K0), hot[:].rearrange("p (t k) e -> p t k e", k=K0),
                                                           slot[:].unsqueeze(2).broadcast_to([P, NT, K0, E0]), ALU.mult))
                    m = dve([m], lambda e: e.tensor_reduce(destf[:], picked[:], AX.X, ALU.add))
                    m_d = dve([m], lambda e: e.tensor_copy(dest[:].rearrange("p t k -> p (t k)"), destf[:]))
                    dve([m], lambda e: e.scalar_tensor_tensor(wts[:], destf[:].rearrange("p (t k) -> p t k", k=K0), float(E0 * CAP),
                                                              top8[:, :, 0:K0], ALU.is_lt, ALU.mult))
                    m = dve([], lambda e: e.tensor_scalar(sgate[:], logits[:, :, E0], -1.0, 87.0, ALU.mult, ALU.min))
                    m = act([m], lambda e: e.activation(sgate[:], sgate[:], ACT.Exp))
                    m = dve([m], lambda e: e.tensor_scalar(sgate[:], sgate[:], 1.0, None, ALU.add))
                    m_sg = dve([m], lambda e: e.reciprocal(sgate[:], sgate[:]))

                    led.wait("pool", [m_d])
                    nc.gpsimd.wait_ge(s_zero, 16 * (E0 * CAP // 512))
                    for t in range(NT):
                        for k in range(K0):
                            nc.gpsimd.indirect_dma_start(out=dispatched, out_offset=bass.IndirectOffsetOnAxis(ap=dest[:, t, k:k + 1], axis=0),
                                                         in_=rows[:, t, :], in_offset=None, bounds_check=E0 * CAP - 1,
                                                         oob_is_err=False).then_inc(s_scatter, 16)

                    hT, sil = sr("hT", [P, len(WID0), 512]), sr("sil", [P, 2, 512])
                    nc.tensor.wait_ge(s_wf, 64)
                    led.wait("dve", [m_sg])
                    with led.repeat(NG, pe=13, act=6, dve=10) as i:
                        previous_iteration("pe", "act", "dve")
                        previous_iteration("act", "dve")
                        previous_iteration("dve", "pe")
                        m = silu_times_up([], lambda k: xT[:, k, ds(i * G * P, G * P)],
                                          lambda c, k: swg[:, k, c * P:c * P + WID0[c]], lambda c, k: swu[:, k, c * P:c * P + WID0[c]],
                                          WID0, hT, sil, nothing_read())
                        m = matmuls([m], [(flat(4, 6)[:, k * C:(k + 1) * C], [(hT[0:w, c, k * P:(k + 1) * P], swd[0:w, c, :]) for c, w in enumerate(WID0)])
                                          for k in range(G)])
                        for k in range(G):
                            dve([m], lambda e: e.scalar_tensor_tensor(acc[:, i * G + k, :], flat(4, 6)[:, k * C:(k + 1) * C], sgate[:, ds(i * G + k, 1)],
                                                                      acc[:, i * G + k, :], ALU.mult, ALU.add))
                    led.meet()
                    for e in ("sp", "pool"):
                        led.engines[e].wait_ge(s_scatter, 16 * NT * K0)

            with ExitStack() as experts:
                se = buffers(experts)
                SLOTS = 4
                wgu = se("wgu", [P, SLOTS, 2, CK, F0])
                wdn = se("wdn", [FC, SLOTS, 2, C])
                erow, erowT = se("erow", [P, SLOTS, C]), se("erowT", [P, SLOTS, CK, P])
                esil, eh = se("esil", [FC, SLOTS, 2, P]), se("eh", [FC, SLOTS, 2, P])
                yrow = se("yrow", [P, SLOTS, C])
                s_ew = [sem(f"expert_loaded_{s}") for s in range(SLOTS)]
                s_ey = [sem(f"answer_stored_{s}") for s in range(SLOTS)]
                for s in range(SLOTS):
                    nc.scalar.nop().then_inc(s_ey[s], 16)
                with led.repeat(E0 // SLOTS, pe=3 * SLOTS, act=3 * SLOTS, dve=SLOTS) as i:
                    previous_iteration("pe", "act", "dve")
                    previous_iteration("act", "dve", "pe")
                    previous_iteration("dve", "pe")
                    m_t, m_tT, m_gu, m_s, m_h, m_y = {}, {}, {}, {}, {}, {}
                    per_iter = 3 * SLOTS
                    for s in range(SLOTS):
                        if s == 0:
                            led.wait("sp", [Mark("pe", per_iter, led.loop)], back=1)
                        load(s_ew[s], erow[:, s, :], dispatched[ds((i * SLOTS + s) * CAP, CAP), :])
                        load(s_ew[s], wgu[:, s, 0, :, :], a["L0_ffn_w_gate"][i * SLOTS + s].rearrange("(c p) n -> p c n", p=P))
                        load(s_ew[s], wgu[:, s, 1, :, :], a["L0_ffn_w_up"][i * SLOTS + s].rearrange("(c p) n -> p c n", p=P))
                        load(s_ew[s], wdn[:, s, :, :], a["L0_ffn_w_down"][i * SLOTS + s].rearrange("(c p) n -> p c n", p=FC))

                    def turn_rows(s):
                        nc.tensor.wait_ge(s_ew[s], 64)
                        nc.tensor.nop().then_inc(s_ew[s], -64)
                        m_t[s] = transposes([m_tT.get(s - 2)], [(bank[:, s % 2, c * P:(c + 1) * P], erow[:, s, c * P:(c + 1) * P]) for c in range(CK)], ident[:])
                        m_tT[s] = act([m_t[s]], lambda e: e.copy(erowT[:, s, :, :].rearrange("p c n -> p (c n)"), bank[:, s % 2, 0:CK * P]))

                    def hidden(s):
                        m_gu[s] = matmuls([m_tT[s], m_h.get(s - 2)],
                                          [(bank[0:FC, 2 + s % 2, (2 * u + c) * P:(2 * u + c + 1) * P],
                                            [(wgu[:, s, u, k, c * FC:(c + 1) * FC], erowT[:, s, k, :]) for k in range(CK)]) for u in range(2) for c in range(2)])
                        m_s[s] = act([m_gu[s]], lambda e: e.activation(esil[:, s, :, :].rearrange("p c n -> p (c n)"), bank[0:FC, 2 + s % 2, 0:2 * P], ACT.Silu))
                        m_h[s] = dve([m_s[s]], lambda e: e.tensor_tensor(eh[:, s, :, :].rearrange("p c n -> p (c n)"), esil[:, s, :, :].rearrange("p c n -> p (c n)"),
                                                                         bank[0:FC, 2 + s % 2, 2 * P:4 * P], ALU.mult))

                    def answer(s):
                        md = matmuls([m_h[s], m_y.get(s - 2)], [(bank[:, 4 + s % 2, 0:C], [(eh[:, s, c, :], wdn[:, s, c, :]) for c in range(2)])])
                        nc.scalar.wait_ge(s_ey[s], 16)
                        nc.scalar.nop().then_inc(s_ey[s], -16)
                        m_y[s] = act([md], lambda e: e.copy(yrow[:, s, :], bank[:, 4 + s % 2, 0:C]))
                        led.wait("act", [m_y[s]])
                        nc.scalar.dma_start(answered[ds((i * SLOTS + s) * CAP, CAP), :], yrow[:, s, :]).then_inc(s_ey[s], 16)

                    turn_rows(0)
                    for s in range(SLOTS):
                        if s + 1 < SLOTS:
                            turn_rows(s + 1)
                        hidden(s)
                        if s:
                            answer(s - 1)
                    answer(SLOTS - 1)
                for s in range(SLOTS):
                    nc.scalar.wait_ge(s_ey[s], 16)
                m_all = act([], lambda e: e.copy(ss[:], rinv[:]))
                led.meet()

            with ExitStack() as combine:
                sc_ = buffers(combine)
                TAKE = 4
                got = sc_("got", [P, TAKE, K0, C])
                where = sc_("where", [P, TAKE, K0], U32)
                s_got = [sem(f"answers_fetched_{s}") for s in range(TAKE)]
                s_where = sem("slots_copied")
                m = dve([], lambda e: e.memset(got[:], 0.0))
                led.wait("pool", [m])
                with led.repeat(NT // TAKE, dve=TAKE * (K0 + 1)) as i:
                    for s in range(TAKE):
                        led.wait("pool", [Mark("dve", (s + 1) * (K0 + 1), led.loop)], back=1)
                        nc.gpsimd.tensor_copy(where[:, s, :], dest[:, i * TAKE + s, :]).then_inc(s_where, 1)
                        nc.gpsimd.wait_ge(s_where, 1)
                        nc.gpsimd.nop().then_inc(s_where, -1)
                        for k in range(K0):
                            nc.gpsimd.indirect_dma_start(out=got[:, s, k, :], out_offset=None, in_=answered,
                                                         in_offset=bass.IndirectOffsetOnAxis(ap=where[:, s, k:k + 1], axis=0),
                                                         bounds_check=E0 * CAP - 1, oob_is_err=False).then_inc(s_got[s], 16)
                        nc.vector.wait_ge(s_got[s], i * (16 * K0) + 16 * K0)
                        m = None
                        for k in range(K0):
                            m = dve([m], lambda e: e.scalar_tensor_tensor(acc[:, i * TAKE + s, :], got[:, s, k, :], wts[:, i * TAKE + s, k:k + 1],
                                                                          acc[:, i * TAKE + s, :], ALU.mult, ALU.add))
                        dve([m], lambda e: e.scalar_tensor_tensor(x_sb[:, i * TAKE + s, :], acc[:, i * TAKE + s, :], tgates[:, 2:3],
                                                                  x_sb[:, i * TAKE + s, :], ALU.mult, ALU.add))
                led.meet()

        def normalised_groups(stack, tag, m_stats, destT, extra=None):
            s = buffers(stack)
            xg, xgT = s(tag + "xg", [P, G, C]), s(tag + "xgT", [P, CK, G * P])
            per = dict(pe=1, dve=4, act=1, pool=1)
            if extra:
                per = dict(pe=2, dve=5, act=1, pool=1)
            with led.repeat(NG, **per) as i:
                previous_iteration("dve", "pe")
                previous_iteration("pe", "act", "dve")
                previous_iteration("act", "pe", "pool")
                for k in range(G):
                    m = dve([m_stats], lambda e: e.tensor_scalar(xg[:, k, :], x_sb[:, i * G + k, :], rstd[:, ds(i * G + k, 1)],
                                                                 nmr[:, ds(i * G + k, 1)], ALU.mult, ALU.add))
                m = transposes([m], [(flat(0, 2)[:, (c * G + k) * P:(c * G + k + 1) * P], xg[:, k, c * P:(c + 1) * P])
                                     for c in range(CK) for k in range(G)], ident[:])
                m = act([m], lambda e: e.copy(xgT[:].rearrange("p c n -> p (c n)"), flat(0, 2)))
                pool([m], lambda e: e.tensor_copy(destT[:, :, ds(i * G * P, G * P)], xgT[:]))
                if extra:
                    extra(i, xgT, m)

        s_td = sem("decay_weights_loaded")
        with ExitStack() as mixing:
            sm = buffers(mixing)
            kc = sm("kc", [P, CK, NTOK])
            decay, u_first = sm("decay", [P, CK]), sm("u_first", [P, CK])
            fade = sm("fade", [P, NTOK])
            ek, ekv = sm("ek", [P, NTOK]), sm("ekv", [P, NTOK])
            sumk, sumkv = sm("sumk", [P, NTOK]), sm("sumkv", [P, NTOK])
            ceil, eu, ec = sm("ceil", [P, NTOK]), sm("eu", [P, NTOK]), sm("ec", [P, NTOK])
            with nc.allow_non_contiguous_dma(reason="256 values, one per partition"):
                load(s_td, decay[:], a["L1_xattn_time_decay"].rearrange("(c p) -> p c", p=P))
                load(s_td, u_first[:], a["L1_xattn_time_first"].rearrange("(c p) -> p c", p=P))
            m_stats = layer_stats([])
            normalised_groups(mixing, "mix_", m_stats, kc)
            led.meet()
            nc.scalar.wait_ge(s_td, 32)
            nc.vector.wait_ge(s_td, 32)
            m = dve([], lambda e: e.tensor_scalar(decay[:], decay[:], 80.0, None, ALU.min))
            m = act([m], lambda e: e.activation(decay[:], decay[:], ACT.Exp))
            m_dec = act([m], lambda e: e.activation(decay[:], decay[:], ACT.Exp, scale=-1.0))
            for c in range(CK):
                k_, v_ = kc[:, c, :], ctxT[:, c, :]
                m_k = act([], lambda e: e.activation(ek[:], k_, ACT.Exp))
                m_c = dve([], lambda e: e.tensor_scalar(ceil[:], k_, u_first[:, c:c + 1], 0.0, ALU.add, ALU.max))
                m_f = dve([], lambda e: e.memset(fade[:], 1.0))
                m_f = dve([m_f, m_dec], lambda e: e.tensor_scalar(fade[:], fade[:], decay[:, c:c + 1], None, ALU.mult))
                m_f = dve([m_f], lambda e: e.memset(fade[:, 0:NTOK:T], 0.0))
                m_ec = act([m_c], lambda e: e.activation(ec[:], ceil[:], ACT.Exp, scale=-1.0))
                m_kc = pool([m_ec], lambda e: e.tensor_tensor(ceil[:], k_, ceil[:], ALU.subtract))
                m_eu = act([m_kc], lambda e: e.activation(eu[:], ceil[:], ACT.Exp, bias=u_first[:, c:c + 1]))
                m_sk = dve([m_f, m_k], lambda e: e.tensor_tensor_scan(sumk[:], fade[:], ek[:], 0.0, ALU.mult, ALU.add))
                m_kv = dve([m_k], lambda e: e.tensor_tensor(ekv[:], ek[:], v_, ALU.mult))
                m_skv = dve([m_kv], lambda e: e.tensor_tensor_scan(sumkv[:], fade[:], ekv[:], 0.0, ALU.mult, ALU.add))
                m_d = dve([m_sk, m_ec, m_kv], lambda e: e.tensor_tensor(ek[:, 1:], ec[:, 1:], sumk[:, 0:NTOK - 1], ALU.mult))
                m_d = dve([m_d, m_eu], lambda e: e.tensor_tensor(ek[:, 1:], ek[:, 1:], eu[:, 1:], ALU.add))
                m_d = dve([m_d], lambda e: e.reciprocal(ek[:, 1:], ek[:, 1:]))
                m_ev = pool([m_eu], lambda e: e.tensor_tensor(ceil[:], eu[:], v_, ALU.mult))
                m_n = dve([m_skv, m_ec], lambda e: e.tensor_tensor(ekv[:, 1:], ec[:, 1:], sumkv[:, 0:NTOK - 1], ALU.mult))
                m_n = dve([m_n, m_ev], lambda e: e.tensor_tensor(ekv[:, 1:], ekv[:, 1:], ceil[:, 1:], ALU.add))
                m_n = dve([m_n, m_d], lambda e: e.tensor_tensor(kc[:, c, 1:], ekv[:, 1:], ek[:, 1:], ALU.mult))
                dve([m_n], lambda e: e.tensor_copy(kc[:, c, 0:NTOK:T], ctxT[:, c, 0:NTOK:T]))
                led.meet()

            y_g = sm("y_g", [P, CK, G * P])
            with led.repeat(NG, pe=1, pool=1, dve=G) as i:
                previous_iteration("pe", "dve")
                previous_iteration("pool", "pe")
                m = pool([], lambda e: e.tensor_copy(y_g[:], kc[:, :, ds(i * G * P, G * P)]))
                m = transposes([m], [(flat(0, 2)[:, k * C + c * P:k * C + (c + 1) * P], y_g[:, c, k * P:(k + 1) * P])
                                     for k in range(G) for c in range(CK)], ident[:])
                for k in range(G):
                    dve([m], lambda e: e.scalar_tensor_tensor(x_sb[:, i * G + k, :], flat(0, 2)[:, k * C:(k + 1) * C], tgates[:, 1:2],
                                                              x_sb[:, i * G + k, :], ALU.mult, ALU.add))
            led.meet()

        s_w1 = sem("ffn1_weights_loaded")
        s_out = sem("output_stored")
        WID1 = [P] * (FS1 // P) + ([FS1 % P] if FS1 % P else [])
        with ExitStack() as ffn1:
            s1 = buffers(ffn1)
            hT_in = s1("hT_in", [P, CK, NTOK])
            w1r = s1("w1r", [P, CK, E1])
            w1g, w1u = s1("w1g", [P, E1, CK, F1]), s1("w1u", [P, E1, CK, F1])
            w1d = s1("w1d", [FC, E1, 2, C])
            v1g, v1u = s1("v1g", [P, CK, FS1]), s1("v1u", [P, CK, FS1])
            v1d = s1("v1d", [P, len(WID1), C])
            logits1 = s1("logits1", [P, NT, E1])
            load(s_w1, w1r[:], a["L1_ffn_gate_w"].rearrange("(c p) n -> p c n", p=P))
            for e in range(E1):
                load(s_w1, w1g[:, e, :, :], a["L1_ffn_w_gate"][e].rearrange("(c p) n -> p c n", p=P))
                load(s_w1, w1u[:, e, :, :], a["L1_ffn_w_up"][e].rearrange("(c p) n -> p c n", p=P))
                load(s_w1, w1d[:, e, :, :], a["L1_ffn_w_down"][e].rearrange("(c p) n -> p c n", p=FC))
            load(s_w1, v1g[:], a["L1_ffn_sw_gate"].rearrange("(c p) n -> p c n", p=P))
            load(s_w1, v1u[:], a["L1_ffn_sw_up"].rearrange("(c p) n -> p c n", p=P))
            for c, w in enumerate(WID1):
                load(s_w1, v1d[0:w, c, :], a["L1_ffn_sw_down"][c * P:c * P + w, :])
            nc.tensor.wait_ge(s_w1, 16 * (3 + 3 * E1 + len(WID1)))

            def router1(i, xgT, m):
                m = matmuls([m], [(bank[:, 2, k * E1:(k + 1) * E1], [(xgT[:, c, k * P:(k + 1) * P], w1r[:, c, :]) for c in range(CK)]) for k in range(G)])
                dve([m], lambda e: e.tensor_copy(logits1[:, ds(i * G, G), :], bank[:, 2, 0:G * E1].rearrange("p (k n) -> p k n", k=G)))

            m_stats = layer_stats([])
            normalised_groups(ffn1, "ffn1_", m_stats, hT_in, router1)
            led.meet()
            comb = s1("comb", [P, NT, E1])
            top8, hot, m = top_experts(s1, logits1[:], E1, K1, "r1_")
            m = dve([m], lambda e: e.tensor_tensor(hot[:].rearrange("p (t k) e -> p t k e", k=K1), hot[:].rearrange("p (t k) e -> p t k e", k=K1),
                                                   top8[:, :, 0:K1].unsqueeze(3).broadcast_to([P, NT, K1, E1]), ALU.mult))
            m_comb = dve([m], lambda e: e.tensor_reduce(comb[:], hot[:].rearrange("p (t k) e -> p t e k", k=K1), AX.X, ALU.add))
            led.meet()

            hid, sil1 = s1("hid", [P, 2, len(WID1), 512]), s1("sil1", [P, 2, 512])
            sumy = s1("sumy", [P, G, C])
            PER = 2 * 2 * E1 + 2 * len(WID1)
            with led.repeat(NG, pe=PER + E1 + 1, act=PER // 2, dve=PER // 2 + G * (E1 + 2)) as i:
                previous_iteration("pe", "act", "dve")
                previous_iteration("act", "dve")
                previous_iteration("dve", "pe")
                led.wait("dve", [])
                free = nothing_read()
                down, taken, sums = {}, {}, [None] * G
                nc.vector.wait_ge(s_out, i * 16)

                def add_down(j, m_h):
                    b = 4 + 2 * (j % 2)
                    slots = hid[:, j % 2, :, :]
                    n, wd = (2, [w1d[:, j, c, :] for c in range(2)]) if j < E1 else (len(WID1), [v1d[0:w, c, :] for c, w in enumerate(WID1)])
                    wid = [FC] * 2 if j < E1 else WID1
                    down[j] = matmuls([m_h, taken.get(j - 2)],
                                      [(flat(b, b + 2)[:, k * C:(k + 1) * C], [(slots[0:wid[c], c, k * P:(k + 1) * P], wd[c]) for c in range(n)]) for k in range(G)])
                    for k in range(G):
                        src = flat(b, b + 2)[:, k * C:(k + 1) * C]
                        if j == 0:
                            sums[k] = dve([down[j]], lambda e: e.tensor_scalar(sumy[:, k, :], src, comb[:, i * G + k, j:j + 1], None, ALU.mult))
                        elif j < E1:
                            sums[k] = dve([down[j], sums[k]], lambda e: e.scalar_tensor_tensor(sumy[:, k, :], src, comb[:, i * G + k, j:j + 1], sumy[:, k, :], ALU.mult, ALU.add))
                        else:
                            sums[k] = dve([down[j], sums[k]], lambda e: e.tensor_tensor(sumy[:, k, :], src, sumy[:, k, :], ALU.add))
                    taken[j] = sums[G - 1]

                m_h = {}
                for j in range(E1 + 1):
                    free["hidden"] = down.get(j - 2)
                    if j < E1:
                        m_h[j] = silu_times_up([], lambda k: hT_in[:, k, ds(i * G * P, G * P)],
                                               lambda c, k: w1g[:, j, k, c * FC:(c + 1) * FC], lambda c, k: w1u[:, j, k, c * FC:(c + 1) * FC],
                                               [FC] * 2, hid[:, j % 2, :, :], sil1, free)
                    else:
                        m_h[j] = silu_times_up([], lambda k: hT_in[:, k, ds(i * G * P, G * P)],
                                               lambda c, k: v1g[:, k, c * P:c * P + WID1[c]], lambda c, k: v1u[:, k, c * P:c * P + WID1[c]],
                                               WID1, hid[:, j % 2, :, :], sil1, free)
                    if j:
                        add_down(j - 1, m_h[j - 1])
                add_down(E1, m_h[E1])
                for k in range(G):
                    m = dve([sums[k]], lambda e: e.scalar_tensor_tensor(sumy[:, k, :], sumy[:, k, :], tgates[:, 3:4], x_sb[:, i * G + k, :], ALU.mult, ALU.add))
                led.wait("sp", [m])
                nc.sync.dma_start(outr[:, ds(i * G, G), :], sumy[:]).then_inc(s_out, 16)
            nc.sync.wait_ge(s_out, 16 * NG)
            led.meet()


def kernel(**inputs):
    import numpy as _np
    import concourse.bacc as _bacc
    from concourse.bass_utils import run_bass_kernel_spmd as _run

    nc = _bacc.Bacc("TRN2", target_bir_lowering=False, num_devices=1)
    arrays, args = {}, {}
    for name, value in inputs.items():
        arrays[f"in_{name}"] = _np.ascontiguousarray(value)
        args[name] = nc.dram_tensor(f"in_{name}", arrays[f"in_{name}"].shape, mybir.dt.from_np(arrays[f"in_{name}"].dtype),
                                    kind="ExternalInput").ap()
    result = nc.dram_tensor("result", inputs["x"].shape, F32, kind="ExternalOutput").ap()
    program(nc, args, result)
    return _run(nc, [arrays], core_ids=[0]).results[0]["result"]
```

```python
from contextlib import ExitStack, contextmanager

import numpy as np

import concourse.bass as bass
from concourse import mybir

ALU = mybir.AluOpType
ACT = mybir.ActivationFunctionType
AX = mybir.AxisListType
F32 = mybir.dt.float32
BF16 = mybir.dt.bfloat16
F16 = mybir.dt.float16
U8 = mybir.dt.uint8
U16 = mybir.dt.uint16
U32 = mybir.dt.uint32
ds = bass.ds

P = 128
ROUND = 12582912.0
LN_EPS = 1e-5
RMS_EPS = 1e-6
FAR = float(1 << 20)


class Mark:

    def __init__(self, name, rel, loop):
        self.name, self.rel, self.loop = name, rel, loop


class Loop:
    def __init__(self, number, i, n, per, start):
        self.number, self.i, self.n, self.per, self.start, self.open = number, i, n, per, start, True


class Ledger:

    HEAD_START = 1024

    def __init__(self, nc, ctx):
        self.nc = nc
        self.engines = {"pe": nc.tensor, "dve": nc.vector, "act": nc.scalar, "pool": nc.gpsimd, "sp": nc.sync}
        self.sem = {n: ctx.enter_context(nc.semaphore(f"finished_{n}")) for n in ("pe", "dve", "act", "pool")}
        self.count = {n: self.HEAD_START for n in self.sem}
        self.loop = None
        self.loops = 0
        self.seen = {}
        for n in self.sem:
            self.engines[n].sem_inc(self.sem[n], self.HEAD_START)

    def done(self, name, instruction):
        self.count[name] += 1
        instruction.then_inc(self.sem[name], 1)
        return Mark(name, self.count[name], self.loop)

    def wait(self, waiter, marks, back=0):
        best = {}
        for m in marks:
            if m is None:
                continue
            key = (m.name, m.loop.number if m.loop else 0)
            if key not in best or best[key].rel < m.rel:
                best[key] = m
        for m in best.values():
            lp = m.loop
            if lp is None:
                known, value = m.rel, m.rel
            elif lp.open:
                known, value = None, lp.i * lp.per[m.name] + (lp.start[m.name] + m.rel - back * lp.per[m.name])
            else:
                known = value = lp.start[m.name] + (lp.n - 1) * lp.per[m.name] + m.rel
            key = (waiter, m.name)
            if known is not None:
                if self.seen.get(key, 0) >= known:
                    continue
                self.seen[key] = known
            else:
                key = (waiter, m.name, lp.number)
                if self.seen.get(key, -10**9) >= m.rel - back * lp.per[m.name]:
                    continue
                self.seen[key] = m.rel - back * lp.per[m.name]
            self.engines[waiter].wait_ge(self.sem[m.name], value)

    def run(self, name, after, build):
        self.wait(name, after)
        return self.done(name, build(self.engines[name]))

    @contextmanager
    def repeat(self, n, **per):
        per = {e: per.get(e, 0) for e in self.sem}
        start = dict(self.count)
        with self.nc.Fori(0, n) as i:
            self.loops += 1
            self.loop = Loop(self.loops, i, n, per, start)
            self.count = {e: 0 for e in self.sem}
            yield i
            assert self.count == per, f"counts in one iteration: {self.count}"
        self.loop.open = False
        self.loop = None
        self.count = {e: start[e] + n * per[e] for e in self.sem}

    def meet(self):
        marks = [Mark(n, self.count[n], None) for n in self.sem]
        for waiter in self.engines:
            self.wait(waiter, marks)


def program(nc, a, out, stop=None):
    x, ctx_in = a["x"], a["ctx_2048"]
    B, T, C = x.shape
    NT = B
    NTOK = NT * T
    H = 16
    HD = C // H
    CK = C // P
    NPAIR = H // 2
    KB = 64
    E0, K0, F0 = a["L0_ffn_w_gate"].shape[0], 4, a["L0_ffn_w_gate"].shape[2]
    CAP = 128
    FS0 = a["L0_ffn_sw_gate"].shape[1]
    E1, K1, F1 = a["L1_ffn_w_gate"].shape[0], 2, a["L1_ffn_w_gate"].shape[2]
    FS1 = a["L1_ffn_sw_gate"].shape[1]
    FC = F0 // 2
    G = 4
    NG = NT // G
    assert T == P and F0 == F1 and CK == 2 and NTOK == 2048

    dispatched = nc.dram_tensor("dispatched_rows", [E0 * CAP, C], F32).ap()
    answered = nc.dram_tensor("answered_rows", [E0 * CAP, C], F32).ap()
    NBLOCKS1 = -(-(NTOK * K1 // P + E1) // 8) * 8
    dispatched1 = nc.dram_tensor("dispatched_rows_1", [NBLOCKS1 * P, C], F32).ap()
    answered1 = nc.dram_tensor("answered_rows_1", [NBLOCKS1 * P, C], F32).ap()
    ZEROED = (E0 * CAP + NBLOCKS1 * P) // 512

    with ExitStack() as whole:
        led = Ledger(nc, whole)

        def sem(name):
            return whole.enter_context(nc.semaphore(name))

        def dve(after, build):
            return led.run("dve", after, build)

        def act(after, build):
            return led.run("act", after, build)

        def pool(after, build):
            return led.run("pool", after, build)

        def buffers(stack):
            return lambda name, shape, dt=F32: stack.enter_context(nc.sbuf_tensor(name, shape, dt))

        sb = buffers(whole)
        bank = whole.enter_context(nc.psum_tensor("bank", [P, 8, 512], F32))

        def flat(b0, b1):
            return bank[:, b0:b1, :].rearrange("p b n -> p (b n)")

        def matmuls(after, groups):
            led.wait("pe", after)
            for dst, terms in groups:
                for n, (lhsT, rhs) in enumerate(terms):
                    mm = nc.tensor.matmul(dst, lhsT, rhs, start=(n == 0), stop=(n == len(terms) - 1))
            return led.done("pe", mm)

        def transposes(after, pairs, ident):
            led.wait("pe", after)
            for dst, src in pairs:
                mm = nc.tensor.transpose(dst, src, ident)
            return led.done("pe", mm)

        def previous_iteration(waiter, *names):
            for n in names:
                led.wait(waiter, [Mark(n, led.loop.per[n], led.loop)], back=1)

        x_sb = sb("x_sb", [P, NT, C])
        ctxT = sb("ctxT", [P, CK, NTOK])
        ident = sb("ident", [P, P])
        ident_b = sb("ident_b", [P, P], BF16)
        ones_row = sb("ones_row", [1, P])
        eps_ln = sb("eps_ln", [P, 1])
        eps_rms = sb("eps_rms", [P, 1])
        gates = sb("gates", [P, 4])
        tgates = sb("tgates", [P, 4])
        stats = sb("stats", [P, NT, 6])
        mv = sb("mv", [P, NT, 2])
        std = sb("std", [P, NT])
        rstd = sb("rstd", [P, NT])
        nmr = sb("nmr", [P, NT])

        s_x, s_ctx, s_wa, s_g = sem("x_loaded"), sem("ctx_loaded"), sem("attention_weights_loaded"), sem("gates_loaded")
        s_zero = sem("dispatched_rows_zeroed")

        xr = x.rearrange("t p c -> p t c")
        cr = ctx_in.rearrange("t p c -> p t c")
        outr = out.rearrange("t p c -> p t c")

        with ExitStack() as attention:
            sa = buffers(attention)
            kT = sa("kT", [P, NPAIR, NTOK], BF16)
            qT_all = sa("qT_all", [P, NPAIR, (NT + 1) * P], BF16)
            v_sb = sa("v_sb", [P, NT, C], BF16)
            sq_all = sa("sq_all", [P, (NT + 1) * H])
            nsq_all = sa("nsq_all", [P, (NT + 1) * H])
            wp = sa("wp", [P, CK, C])
            bp_row = sa("bp_row", [1, C])

            with ExitStack() as prepare:
                sp_ = buffers(prepare)
                ctx_sb = sp_("ctx_sb", [P, NT, C])
                vT = sp_("vT", [P, CK, NTOK])
                wq, wkv = sp_("wq", [P, CK, C]), sp_("wkv", [P, CK, 2 * C])
                bq_row, bk_row = sp_("bq_row", [1, C]), sp_("bk_row", [1, C])
                bv = sp_("bv", [P, CK])
                xn = sp_("xn", [P, G, C])
                xnT = sp_("xnT", [P, CK, G * P])
                cT = sp_("cT", [P, CK, G * P])
                y1, y2 = sp_("y1", [P, G, C]), sp_("y2", [P, G, C])
                qint = sp_("qint", [P, G, C], BF16)
                qrep = sp_("qrep", [P, G, H, KB], BF16)
                ksplit = sp_("ksplit", [P, G, H, KB], BF16)
                small = sp_("small", [P, 6, G * H])

                for g in range(NG):
                    nc.sync.dma_start(x_sb[:, g * G:(g + 1) * G, :], xr[:, g * G:(g + 1) * G, :]).then_inc(s_x, 16)
                    nc.scalar.dma_start(ctx_sb[:, g * G:(g + 1) * G, :], cr[:, g * G:(g + 1) * G, :]).then_inc(s_ctx, 16)
                nc.sync.dma_start(wq[:], a["L0_xattn_Wq"].rearrange("(c p) n -> p c n", p=P)).then_inc(s_wa, 16)
                nc.sync.dma_start(wkv[:], a["L0_xattn_Wkv"].rearrange("(c p) n -> p c n", p=P)).then_inc(s_wa, 16)
                nc.sync.dma_start(wp[:], a["L0_xattn_Wp"].rearrange("(c p) n -> p c n", p=P)).then_inc(s_wa, 16)
                nc.sync.dma_start(bq_row[:], a["L0_xattn_bq"].rearrange("(a n) -> a n", a=1)).then_inc(s_wa, 16)
                nc.sync.dma_start(bk_row[:], a["L0_xattn_bkv"][0:C].rearrange("(a n) -> a n", a=1)).then_inc(s_wa, 16)
                with nc.allow_non_contiguous_dma(reason="256 biases, one per partition"):
                    nc.sync.dma_start(bv[:], a["L0_xattn_bkv"][C:2 * C].rearrange("(c p) -> p c", p=P)).then_inc(s_wa, 16)
                nc.sync.dma_start(bp_row[:], a["L0_xattn_bp"].rearrange("(a n) -> a n", a=1)).then_inc(s_wa, 16)
                nc.sync.dma_start(gates[:, 0:2], a["g_xattn"].partition_broadcast(P)).then_inc(s_g, 16)
                nc.sync.dma_start(gates[:, 2:4], a["g_ffn"].partition_broadcast(P)).then_inc(s_g, 16)

                m = pool([], lambda e: e.memset(ident[:], 0.0))
                m_id = pool([m], lambda e: e.affine_select(out=ident[:], in_=ident[:], compare_op=ALU.not_equal, fill=1.0,
                                                           base=0, pattern=[[-1, P]], channel_multiplier=1))
                m_idb = pool([m_id], lambda e: e.tensor_copy(ident_b[:], ident[:]))
                pool([], lambda e: e.memset(ones_row[:], 1.0))
                m_pad = [pool([], lambda e: e.memset(qrep[:, :, :, 3 * HD:KB], 0.0)),
                         pool([], lambda e: e.memset(ksplit[:, :, :, 3 * HD:KB], 0.0)),
                         pool([], lambda e: e.memset(qT_all[:, :, NT * P:], 0.0)),
                         pool([], lambda e: e.memset(sq_all[:, NT * H:], 0.0)),
                         pool([], lambda e: e.memset(nsq_all[:, NT * H:], 0.0))]
                m_eps = dve([], lambda e: e.memset(eps_ln[:], LN_EPS))
                dve([], lambda e: e.memset(eps_rms[:], RMS_EPS))

                def layer_stats(ready):
                    led.wait("dve", ready)
                    for t in range(NT):
                        m = dve([], lambda e: e.bn_stats(stats[:, t, :], x_sb[:, t, :]))
                    led.wait("dve", [m])
                    for t in range(NT):
                        m = dve([], lambda e: e.bn_aggr(mv[:, t, :], stats[:, t, :]))
                    m = act([m, m_eps], lambda e: e.activation(std[:], mv[:, :, 1], ACT.Sqrt, bias=eps_ln[:], scale=1.0))
                    m = dve([m], lambda e: e.reciprocal(rstd[:], std[:]))
                    return dve([m], lambda e: e.scalar_tensor_tensor(nmr[:], mv[:, :, 0], -1.0, rstd[:], ALU.mult, ALU.mult))

                nc.vector.wait_ge(s_x, 16 * NG)
                m_stats = layer_stats([])

                for e in ("pe", "act", "dve", "pool"):
                    led.engines[e].wait_ge(s_wa, 16 * 7)
                led.wait("pe", [m_idb])
                nc.gpsimd.wait_ge(s_ctx, 16 * NG)
                led.wait("act", m_pad)
                led.wait("pool", m_pad)
                with led.repeat(NG, pe=13, dve=25, act=13, pool=3) as i:
                    previous_iteration("dve", "pe", "act", "pool")
                    previous_iteration("pe", "act", "dve")
                    previous_iteration("act", "pe", "pool", "dve")
                    previous_iteration("pool", "pe", "dve", "act")
                    for k in range(G):
                        m_xn = dve([m_stats], lambda e: e.tensor_scalar(xn[:, k, :], x_sb[:, i * G + k, :], rstd[:, ds(i * G + k, 1)],
                                                                         nmr[:, ds(i * G + k, 1)], ALU.mult, ALU.add))
                    m_x = transposes([m_xn], [(flat(0, 2)[:, (c * G + k) * P:(c * G + k + 1) * P], xn[:, k, c * P:(c + 1) * P])
                                              for c in range(CK) for k in range(G)], ident[:])
                    m_cs = pool([], lambda e: e.tensor_copy(y1[:], ctx_sb[:, ds(i * G, G), :]))
                    m_c = transposes([m_cs], [(flat(2, 4)[:, (c * G + k) * P:(c * G + k + 1) * P], y1[:, k, c * P:(c + 1) * P])
                                              for c in range(CK) for k in range(G)], ident[:])
                    m_xT = act([m_x], lambda e: e.copy(xnT[:].rearrange("p c n -> p (c n)"), flat(0, 2)))
                    m_cT = act([m_c], lambda e: e.copy(cT[:].rearrange("p c n -> p (c n)"), flat(2, 4)))
                    m_cT2 = pool([m_cT], lambda e: e.tensor_copy(ctxT[:, :, ds(i * G * P, G * P)], cT[:]))

                    def project(m_in, srcT, w, c0, bias, banks):
                        return matmuls(m_in, [(flat(*banks)[:, k * C:(k + 1) * C],
                                               [(ones_row[:], bias[:])] + [(srcT[:, c, k * P:(k + 1) * P], w[:, c, c0:c0 + C]) for c in range(CK)])
                                              for k in range(G)])

                    m_q = project([m_xT], xnT, wq, 0, bq_row, (4, 6))
                    m_k = project([m_cT], cT, wkv, 0, bk_row, (6, 8))
                    m_v = matmuls([], [(bank[:, c, :], [(wkv[:, k, C + c * P:C + (c + 1) * P], cT[:, k, :]) for k in range(CK)]) for c in range(CK)])
                    for c in range(CK):
                        m_vT = act([m_v], lambda e: e.activation(vT[:, c, ds(i * G * P, G * P)], bank[:, c, :], ACT.Identity,
                                                                 bias=bv[:, c:c + 1], scale=1.0))

                    def quantise(m_in, banks, premult, n):
                        src = flat(*banks).rearrange("p (t h d) -> p (t h) d", t=G, h=H)
                        y = y1[:].rearrange("p t (h d) -> p (t h) d", h=H)
                        am, sc, rc = small[:, n, :], small[:, n + 1, :], small[:, n + 2, :]
                        m = dve([m_in], lambda e: e.tensor_reduce(am, src, AX.X, ALU.max, apply_absolute_value=True))
                        m_s = dve([m], lambda e: e.tensor_scalar(sc, am, premult / 127.0, 1e-8, ALU.mult, ALU.max))
                        m = dve([m_s], lambda e: e.reciprocal(rc, sc))
                        if premult != 1.0:
                            m = dve([m], lambda e: e.tensor_scalar(rc, rc, premult, None, ALU.mult))
                        m = dve([m, m_c], lambda e: e.tensor_tensor(y, src, rc.unsqueeze(2).broadcast_to([P, G * H, HD]), ALU.mult))
                        m = dve([m], lambda e: e.tensor_scalar(y, y, 127.0, -127.0, ALU.min, ALU.max))
                        return sc, m_s, m

                    sc, m_s, m = quantise(m_q, (4, 6), 0.25, 0)
                    m_sq = pool([m_s], lambda e: e.tensor_copy(sq_all[:, ds(i * G * H, G * H)], sc))
                    dve([m_s], lambda e: e.tensor_scalar(nsq_all[:, ds(i * G * H, G * H)], sc, -1.0, None, ALU.mult))
                    m = dve([m], lambda e: e.tensor_scalar(qint[:], y1[:], ROUND, -ROUND, ALU.add, ALU.add))
                    for r in range(3):
                        m_qr = act([m], lambda e: e.copy(qrep[:, :, :, r * HD:(r + 1) * HD].rearrange("p t h d -> p (t h) d"),
                                                         qint[:].rearrange("p t (h d) -> p (t h) d", h=H)))

                    sc, m_s, m = quantise(m_k, (6, 8), 1.0, 3)
                    m = dve([m], lambda e: e.tensor_scalar(y1[:], y1[:], ROUND, -ROUND, ALU.add, ALU.add))
                    y1h = y1[:].rearrange("p t (h d) -> p (t h) d", h=H)
                    y2h = y2[:].rearrange("p t (h d) -> p (t h) d", h=H)
                    part = [ksplit[:, :, :, r * HD:(r + 1) * HD].rearrange("p t h d -> p (t h) d") for r in range(3)]
                    m = dve([m], lambda e: e.tensor_tensor(y1h, y1h, sc.unsqueeze(2).broadcast_to([P, G * H, HD]), ALU.mult))
                    m_hi = act([m], lambda e: e.copy(part[0], y1h))
                    m = dve([m_hi], lambda e: e.tensor_tensor(y2h, y1h, part[0], ALU.subtract))
                    m_mid = act([m], lambda e: e.copy(part[1], y2h))
                    m = dve([m_mid], lambda e: e.tensor_tensor(part[2], y2h, part[1], ALU.subtract))
                    m_ks = m

                    def turn(m_in, free, src, banks, put):
                        for k in range(G):
                            view = bank[:, banks[k], :].bitcast(BF16)
                            mt = transposes([m_in, free[k]], [(view[:, p * P:(p + 1) * P], src[:, k, 2 * p:2 * p + 2, :].rearrange("p h d -> p (h d)"))
                                                              for p in range(NPAIR)], ident_b[:])
                            put(k, mt, view.rearrange("p (a n) -> p a n", a=NPAIR))

                    turned = {}

                    def put_q(k, mt, view):
                        turned[k] = act([mt], lambda e: e.copy(qT_all[:, :, ds(i * G * P + k * P, P)], view))

                    def put_k(k, mt, view):
                        dve([mt], lambda e: e.tensor_copy(kT[:, :, ds(i * G * P + (k // 2) * 2 * P + k % 2, P, step=2)], view))

                    turn(m_qr, [m_cT, m_cT, m_ks, m_ks], qrep, (2, 3, 4, 5), put_q)
                    turn(m_ks, [m_ks, m_ks, m_vT, m_vT], ksplit, (6, 7, 0, 1), put_k)
                led.meet()

                sv, rv = small[:, 0, 0:CK], small[:, 1, 0:CK]
                m = dve([], lambda e: e.tensor_reduce(sv, vT[:], AX.X, ALU.max, apply_absolute_value=True))
                m_sv = dve([m], lambda e: e.tensor_scalar(sv, sv, 1.0 / 127.0, 1e-8, ALU.mult, ALU.max))
                m = dve([m_sv], lambda e: e.reciprocal(rv, sv))
                vint = ctx_sb[:].rearrange("p t c -> p (t c)").bitcast(BF16)[:, 0:CK * NTOK].rearrange("p (c n) -> p c n", c=CK)
                for c in range(CK):
                    mc = dve([m], lambda e: e.tensor_scalar(vT[:, c, :], vT[:, c, :], rv[:, c:c + 1], 127.0, ALU.mult, ALU.min))
                    mc = dve([mc], lambda e: e.tensor_scalar(vT[:, c, :], vT[:, c, :], -127.0, ROUND, ALU.max, ALU.add))
                    mc = dve([mc], lambda e: e.tensor_scalar(vint[:, c, :], vT[:, c, :], -ROUND, None, ALU.add))
                    for b in range(2):
                        view = bank[:, 2 * c + b, :].bitcast(BF16)
                        mt = transposes([mc], [(view[:, k * P:(k + 1) * P], vint[:, c, (8 * b + k) * P:(8 * b + k + 1) * P]) for k in range(8)], ident_b[:])
                        act([mt], lambda e: e.copy(v_sb[:, 8 * b:8 * b + 8, c * P:(c + 1) * P], view.rearrange("p (k n) -> p k n", k=8)))
                    dve([m_sv], lambda e: e.tensor_scalar(wp[:, c, :], wp[:, c, :], sv[:, c:c + 1], None, ALU.mult))
                nc.scalar.wait_ge(s_g, 32)
                act([], lambda e: e.activation(tgates[:], gates[:], ACT.Tanh))
                led.meet()

            attn = sa("attn", [P, NT + 1, C])
            q_cur = sa("q_cur", [P, H, P], BF16)
            prob = sa("prob", [P, 2, NTOK], U16)
            probT = sa("probT", [P, 2, NTOK], BF16)
            top = sa("top", [P, 2, 3])
            shift = sa("shift", [P, 2])
            bias = sa("bias", [P, 2])
            norm = sa("norm", [P, H, 2])
            rnorm = sa("rnorm", [P, H])
            zeros = sa("zeros", [P, 1024])

            HALF = NTOK // 2
            LN255 = float(np.log(255.0))
            score = [flat(2 * b, 2 * b + 2) for b in range(3)]
            tbank = bank[:, 6, :]
            obank = bank[:, 7, 0:C]

            s_qk = sem("scores_ready")
            s_exp = sem("exp_finished")
            s_bias = sem("bias_ready")
            s_t0, s_t1 = sem("half0_transposed"), sem("half1_transposed")
            s_e0, s_e1 = sem("half0_evacuated"), sem("half1_evacuated")
            s_o, s_ofree = sem("outputs_ready"), sem("outputs_taken")
            s_qfree, s_qcur = sem("head_multiplied"), sem("query_pair_copied")
            s_v = sem("vector_finished")

            m_z = pool([], lambda e: e.memset(zeros[:], 0.0))
            led.wait("sp", [m_z])
            for rows in [dispatched[512 * r:512 * (r + 1), :] for r in range(E0 * CAP // 512)] + \
                        [dispatched1[512 * r:512 * (r + 1), :] for r in range(NBLOCKS1 * P // 512)]:
                nc.sync.dma_start(rows.rearrange("(p f) c -> p (f c)", p=P), zeros[:]).then_inc(s_zero, 16)

            m = [pool([], lambda e: e.memset(q_cur[:], 0.0)),
                 dve([], lambda e: e.memset(prob[:], 0x6400)),
                 dve([], lambda e: e.memset(probT[:], 0.0)),
                 dve([], lambda e: e.memset(norm[:], 1.0)),
                 dve([], lambda e: e.memset(rnorm[:], 1.0)),
                 dve([], lambda e: e.memset(tbank, 0.0)),
                 dve([], lambda e: e.memset(obank, 0.0))]
            for p in range(NPAIR):
                pool(m, lambda e: e.tensor_copy(q_cur[0:KB, 2 * p, :], qT_all[0:KB, p, 0:P]))
                mq = pool(m, lambda e: e.tensor_copy(q_cur[KB:P, 2 * p + 1, :], qT_all[KB:P, p, 0:P]))
            led.meet()

            def scores(g, u, n):
                for v in range(2):
                    k0 = u * HALF + v * 512
                    mm = nc.tensor.matmul(score[n % 3][:, v * 512:(v + 1) * 512], q_cur[:, g, :], kT[:, g // 2, k0:k0 + 512],
                                          start=True, stop=True)
                    if u == 1 or v == 1:
                        mm.then_inc(s_qk, 1)

            def maximum(g, u, v, n):
                src = score[n % 3] if u == 0 else score[n % 3][:, v * 512:(v + 1) * 512]
                c = 0 if u == 0 else 1 + v
                nc.vector.tensor_reduce(top[:, g % 2, c:c + 1], src, AX.X, ALU.max).then_inc(s_v, 1)

            def make_bias(g, t, n):
                nc.vector.wait_ge(s_v, n)
                nc.vector.tensor_reduce(shift[:, g % 2:g % 2 + 1], top[:, g % 2, :], AX.X, ALU.max).then_inc(s_v, 1)
                nc.vector.wait_ge(s_v, n + 1)
                nc.vector.tensor_scalar(bias[:, g % 2:g % 2 + 1], shift[:, g % 2:g % 2 + 1], nsq_all[:, ds(t * H + g, 1)], LN255,
                                        ALU.mult, ALU.add).then_inc(s_bias, 1)

            def exponentials(g, u, t, n):
                low = prob[:, g % 2, :].bitcast(U8)[:, u * NTOK:(u + 1) * NTOK:2]
                nc.scalar.activation(low, score[n % 3], ACT.Exp, bias=bias[:, g % 2:g % 2 + 1],
                                     scale=sq_all[:, ds(t * H + g, 1)], accum_out=norm[:, g, u:u + 1]).then_inc(s_exp, 1)

            def transpose_half(h, u, signal):
                words = prob[:, h % 2, :].bitcast(F32)
                for c in range(4):
                    mm = nc.tensor.transpose(tbank[:, c * P:(c + 1) * P], words[:, (4 * u + c) * P:(4 * u + c + 1) * P], ident[:])
                mm.then_inc(signal, 1)

            def values(h):
                pt = probT[:, h % 2, :].rearrange("p (c q two) -> p c q two", c=8, two=2)
                for r in range(NT):
                    mm = nc.tensor.matmul(obank[:, h * HD:(h + 1) * HD], pt[:, r // 2, :, r % 2], v_sb[:, r, h * HD:(h + 1) * HD],
                                          start=(r == 0), stop=(r == NT - 1))
                return mm

            def take_outputs(slot):
                nc.vector.tensor_tensor(attn[:, slot, :].rearrange("p (h d) -> p h d", h=H), obank.rearrange("p (h d) -> p h d", h=H),
                                        rnorm[:].unsqueeze(2).broadcast_to([P, H, HD]), ALU.mult).then_inc(s_ofree, 1)

            def normaliser(h0, n):
                nc.vector.tensor_tensor(rnorm[:, h0:h0 + 8], norm[:, h0:h0 + 8, 0], norm[:, h0:h0 + 8, 1], ALU.add).then_inc(s_v, 1)
                nc.vector.wait_ge(s_v, n + 1)
                nc.vector.reciprocal(rnorm[:, h0:h0 + 8], rnorm[:, h0:h0 + 8]).then_inc(s_v, 1)

            for n in range(3):
                scores(n // 2, n % 2, n)
            for n, v in ((0, None), (1, 0), (1, 1)):
                nc.vector.wait_ge(s_qk, 1 + n + (v or 0))
                maximum(n // 2, n % 2, v, n)
            make_bias(0, 0, 3)
            nc.vector.wait_ge(s_qk, 4)
            maximum(1, 0, None, 2)
            nc.vector.nop().then_inc(s_qk, -4)
            nc.vector.wait_ge(s_v, 5)
            nc.vector.nop().then_inc(s_v, -5)
            nc.tensor.nop().then_inc(s_t1, 1)
            nc.gpsimd.nop().then_inc(s_qcur, H)

            def tiles(t0, ntiles):
                pe, ve, ac, po = nc.tensor, nc.vector, nc.scalar, nc.gpsimd
                n_v = 0
                for n in range(ntiles * H):
                    j, h = divmod(n, H)
                    t = t0 + j
                    g, tg = (h + 1, t) if h + 1 < H else (0, t + 1)
                    g2 = (h + 2) % H

                    pe.wait_ge(s_exp, 2 * n + 1)
                    scores(g, 1, 2 * n + 3)
                    pe.wait_ge(s_e1, n + 1)
                    transpose_half(h, 0, s_t0)
                    if h == 1:
                        pe.wait_ge(s_ofree, j + 1)
                    mm = values((h - 1) % H)
                    mm.then_inc(s_o if h == 0 else s_qfree, 1)
                    pe.wait_ge(s_exp, 2 * n + 2)
                    if g2 % 2 == 0:
                        pe.wait_ge(s_qcur, H * j + (H + 2 if g2 == 0 else g2 + 2))
                    scores(g2, 0, 2 * n + 4)
                    pe.wait_ge(s_e0, n + 1)
                    transpose_half(h, 1, s_t1)

                    for v in range(2):
                        ve.wait_ge(s_qk, 3 * n + 1 + v)
                        maximum(g, 1, v, 2 * n + 3)
                        n_v += 1
                    make_bias(g, tg, n_v)
                    n_v += 1
                    ve.wait_ge(s_t0, n + 1)
                    ve.tensor_scalar(probT[:, h % 2, 0:HALF], tbank.bitcast(F16), -1024.0, None, ALU.add).then_inc(s_e0, 1)
                    if h == 0:
                        normaliser(8, n_v)
                        n_v += 2
                        ve.wait_ge(s_v, n_v)
                        ve.wait_ge(s_o, j + 1)
                        take_outputs(t)
                    if h == 9:
                        normaliser(0, n_v)
                        n_v += 2
                    ve.wait_ge(s_qk, 3 * n + 3)
                    maximum(g2, 0, None, 2 * n + 4)
                    n_v += 1

                    ac.wait_ge(s_bias, n + 1)
                    exponentials(h, 0, t, 2 * n)
                    ac.wait_ge(s_t1, n + 1)
                    ac.activation(probT[:, (h - 1) % 2, HALF:], tbank.bitcast(F16), ACT.Copy, bias=-1024.0).then_inc(s_e1, 1)
                    exponentials(h, 1, t, 2 * n + 1)

                    if h % 2 == 0:
                        p = h // 2
                        po.wait_ge(s_qfree, (H - 1) * j + max(1, h))
                        po.tensor_copy(q_cur[0:KB, h, :], qT_all[0:KB, p, ds(t * P + P, P)]).then_inc(s_qcur, 1)
                        po.tensor_copy(q_cur[KB:P, h + 1, :], qT_all[KB:P, p, ds(t * P + P, P)]).then_inc(s_qcur, 1)

                ve.wait_ge(s_v, n_v)
                po.wait_ge(s_qfree, (H - 1) * ntiles)
                N = ntiles * H
                for e, s, count in ((pe, s_exp, 2 * N), (pe, s_e1, N), (pe, s_e0, N), (pe, s_ofree, ntiles), (pe, s_qcur, N),
                                    (ve, s_qk, 3 * N), (ve, s_t0, N), (ve, s_o, ntiles), (ve, s_v, n_v),
                                    (ac, s_bias, N), (ac, s_t1, N), (po, s_qfree, (H - 1) * ntiles)):
                    e.nop().then_inc(s, -count)

            RING = 3
            with nc.Fori(0, NT // RING) as r:
                tiles(r * RING, RING)
            for t in range(NT // RING * RING, NT):
                tiles(t, 1)

            nc.scalar.wait_ge(s_t1, 1)
            m = act([], lambda e: e.activation(probT[:, 1, HALF:], tbank.bitcast(F16), ACT.Copy, bias=-1024.0))
            led.wait("pe", [m])
            nc.tensor.wait_ge(s_qcur, H)
            m_o = led.done("pe", values(H - 1))
            nc.vector.tensor_tensor(rnorm[:, 8:16], norm[:, 8:16, 0], norm[:, 8:16, 1], ALU.add).then_inc(s_v, 1)
            nc.vector.wait_ge(s_v, 1)
            m = dve([], lambda e: e.reciprocal(rnorm[:, 8:16], rnorm[:, 8:16]))
            led.wait("dve", [m, m_o])
            take_outputs(NT)
            dve([], lambda e: e.memset(top[:], 0.0))
            led.wait("pool", [m_o])
            pool([], lambda e: e.memset(q_cur[:, 0, 0:1], 0.0))
            led.meet()

            a_g = sa("a_g", [P, G, C])
            aT = sa("aT", [P, CK, G * P])
            with led.repeat(NG, pe=2, act=1, dve=G, pool=1) as i:
                previous_iteration("pe", "act", "dve")
                previous_iteration("act", "pe")
                previous_iteration("pool", "pe")
                m = pool([], lambda e: e.tensor_copy(a_g[:], attn[:, ds(i * G + 1, G), :]))
                m = transposes([m], [(flat(0, 2)[:, (c * G + k) * P:(c * G + k + 1) * P], a_g[:, k, c * P:(c + 1) * P])
                                     for k in range(G) for c in range(CK)], ident[:])
                m = act([m], lambda e: e.copy(aT[:].rearrange("p c n -> p (c n)"), flat(0, 2)))
                m = matmuls([m], [(flat(2, 4)[:, k * C:(k + 1) * C],
                                   [(ones_row[:], bp_row[:])] + [(aT[:, c, k * P:(k + 1) * P], wp[:, c, :]) for c in range(CK)]) for k in range(G)])
                for k in range(G):
                    dve([m], lambda e: e.scalar_tensor_tensor(x_sb[:, i * G + k, :], flat(2, 4)[:, k * C:(k + 1) * C], tgates[:, 0:1],
                                                              x_sb[:, i * G + k, :], ALU.mult, ALU.add))
            led.meet()

        def load(s, dst, src):
            nc.sync.dma_start(dst, src).then_inc(s, 16)

        def silu_times_up(after, rhs, gate_w, up_w, widths, hT, sil, free):
            mh = None
            for c, w in enumerate(widths):
                b = free["n"] % 2
                free["n"] += 1
                mg = matmuls(after + [free["gate", b]], [(bank[0:w, b, :], [(gate_w(c, k), rhs(k)) for k in range(CK)])])
                mu = matmuls([free["up", b]], [(bank[0:w, 2 + b, :], [(up_w(c, k), rhs(k)) for k in range(CK)])])
                ms = act([mg, free["up", b]], lambda e: e.activation(sil[0:w, b, :], bank[0:w, b, :], ACT.Silu))
                mh = dve([ms, mu, free["hidden"]], lambda e: e.tensor_tensor(hT[0:w, c, :], sil[0:w, b, :], bank[0:w, 2 + b, :], ALU.mult))
                free["gate", b], free["up", b] = ms, mh
            return mh

        def nothing_read():
            return {("gate", 0): None, ("gate", 1): None, ("up", 0): None, ("up", 1): None, "hidden": None, "n": 0}

        def top_experts(sr, logits, E, K, tag, ready):
            pr = sr(tag + "pr", [P, NT, E])
            top8, idx8 = sr(tag + "top8", [P, NT, 8]), sr(tag + "idx8", [P, NT, 8], U32)
            idxf, iota_i, iota_f = sr(tag + "idxf", [P, NT * K]), sr(tag + "iota_i", [P, E], U32), sr(tag + "iota_f", [P, E])
            hot = sr(tag + "hot", [P, NT * K, E])
            r1, r2 = sr(tag + "r1", [P, NT]), sr(tag + "r2", [P, NT])
            mi = pool([], lambda e: e.iota(iota_i[:], pattern=[[1, E]], base=0, channel_multiplier=0))
            mi = pool([mi], lambda e: e.tensor_copy(iota_f[:], iota_i[:]))
            m = dve(ready, lambda e: e.tensor_reduce(r1[:], logits, AX.X, ALU.max))
            m = dve([m], lambda e: e.tensor_tensor(pr[:], logits, r1[:].unsqueeze(2).broadcast_to([P, NT, E]), ALU.subtract))
            m = act([m], lambda e: e.activation(pr[:], pr[:], ACT.Exp))
            m = dve([m], lambda e: e.tensor_reduce(r2[:], pr[:], AX.X, ALU.add))
            m = dve([m], lambda e: e.reciprocal(r2[:], r2[:]))
            m = dve([m], lambda e: e.tensor_tensor(pr[:], pr[:], r2[:].unsqueeze(2).broadcast_to([P, NT, E]), ALU.mult))
            led.wait("dve", [m])
            for t in range(NT):
                m = dve([], lambda e: e.max(top8[:, t, :], pr[:, t, :]))
            led.wait("dve", [m])
            for t in range(NT):
                m = dve([], lambda e: e.max_index(idx8[:, t, :], top8[:, t, :], pr[:, t, :]))
            m = dve([m], lambda e: e.tensor_copy(idxf[:].rearrange("p (t k) -> p t k", k=K), idx8[:, :, 0:K]))
            m = dve([m, mi], lambda e: e.tensor_tensor(hot[:], iota_f[:].unsqueeze(1).broadcast_to([P, NT * K, E]),
                                                       idxf[:].unsqueeze(2).broadcast_to([P, NT * K, E]), ALU.is_equal))
            return top8, hot, m

        def route(tag, stack, logits, E, K, ready, capacity, dest, wts, owner=None, put=None):
            s = buffers(stack)
            before, every = s(tag + "before", [P, P], BF16), s(tag + "every", [P, P], BF16)
            mask, prefix = s(tag + "mask", [P, NT, E], BF16), s(tag + "prefix", [P, NT, E], BF16)
            first, slot = s(tag + "first", [P, E]), s(tag + "slot", [P, NT, E])
            picked, destf = s(tag + "picked", [P, NT * K, E]), s(tag + "destf", [P, NT * K])
            mc = pool([], lambda e: e.memset(every[:], 1.0))
            mc = pool([mc], lambda e: e.affine_select(out=before[:], in_=every[:], compare_op=ALU.is_gt, fill=0.0, base=0,
                                                      pattern=[[1, P]], channel_multiplier=-1))
            top8, hot, m = top_experts(s, logits, E, K, tag, ready)
            hot4 = hot[:].rearrange("p (t k) e -> p t k e", k=K)
            with nc.allow_low_precision(reason="counts up to 16 are exact in bfloat16"):
                m = dve([m], lambda e: e.tensor_reduce(mask[:], hot4.rearrange("p t k e -> p t e k"), AX.X, ALU.add))
            m2 = dve([], lambda e: e.memset(prefix[:, 0, :], 0.0))
            for t in range(1, NT):
                m2 = dve([m, m2], lambda e: e.tensor_tensor(prefix[:, t, :], prefix[:, t - 1, :], mask[:, t - 1, :], ALU.add))
            groups = [(bank[:, 7, 0:NT * E], [(before[:], mask[:].rearrange("p t e -> p (t e)")), (every[:], prefix[:].rearrange("p t e -> p (t e)"))])]
            if capacity is None:
                groups.append((bank[:, 6, 0:E], [(every[:], prefix[:, NT - 1, :]), (every[:], mask[:, NT - 1, :])]))
            m = matmuls([m2, mc], groups)
            place = bank[:, 7, 0:NT * E].rearrange("p (t e) -> p t e", e=E)
            if capacity is not None:
                first_i, far = s(tag + "first_i", [P, E], U32), s(tag + "far", [P, NT, E])
                mf = pool([], lambda e: e.iota(first_i[:], pattern=[[capacity, E]], base=0, channel_multiplier=0))
                mf = pool([mf], lambda e: e.tensor_copy(first[:], first_i[:]))
                m1 = dve([m], lambda e: e.tensor_scalar(far[:], place, float(capacity), FAR, ALU.is_ge, ALU.mult))
                m = dve([m, mf], lambda e: e.tensor_tensor(slot[:], place, first[:].unsqueeze(1).broadcast_to([P, NT, E]), ALU.add))
                m = dve([m, m1], lambda e: e.tensor_tensor(slot[:], slot[:], far[:], ALU.add))
            else:
                nblocks = owner.shape[1]
                blocks, upto, one = s(tag + "blocks", [P, E]), s(tag + "upto", [P, E]), s(tag + "one", [P, E])
                num_i, num = s(tag + "num_i", [P, nblocks], U32), s(tag + "num", [P, nblocks])
                past, own = s(tag + "past", [P, nblocks, E]), s(tag + "own", [P, nblocks])
                mn = pool([], lambda e: e.iota(num_i[:], pattern=[[1, nblocks]], base=0, channel_multiplier=0))
                mn = pool([mn], lambda e: e.tensor_copy(num[:], num_i[:]))
                mb = dve([m], lambda e: e.tensor_scalar(blocks[:], bank[:, 6, 0:E], 63.5, 1.0 / 128.0, ALU.add, ALU.mult))
                mb = dve([mb], lambda e: e.tensor_scalar(blocks[:], blocks[:], ROUND, -ROUND, ALU.add, ALU.add))
                mo = dve([], lambda e: e.memset(one[:], 1.0))
                mu = dve([mb, mo], lambda e: e.tensor_tensor_scan(upto[:], one[:], blocks[:], 0.0, ALU.mult, ALU.add))
                mf = dve([mu], lambda e: e.tensor_tensor(first[:], upto[:], blocks[:], ALU.subtract))
                mf = dve([mf], lambda e: e.tensor_scalar(first[:], first[:], float(P), None, ALU.mult))
                mp = dve([mu, mn], lambda e: e.tensor_tensor(past[:], upto[:].unsqueeze(1).broadcast_to([P, nblocks, E]),
                                                             num[:].unsqueeze(2).broadcast_to([P, nblocks, E]), ALU.is_le))
                mp = dve([mp], lambda e: e.tensor_reduce(own[:], past[:], AX.X, ALU.add))
                mp = dve([mp], lambda e: e.tensor_scalar(own[:], own[:], float(E - 1), None, ALU.min))
                dve([mp], lambda e: e.tensor_copy(owner, own[:]))
                m = dve([m, mf], lambda e: e.tensor_tensor(slot[:], place, first[:].unsqueeze(1).broadcast_to([P, NT, E]), ALU.add))
            m = dve([m], lambda e: e.tensor_tensor(picked[:].rearrange("p (t k) e -> p t k e", k=K), hot4,
                                                   slot[:].unsqueeze(2).broadcast_to([P, NT, K, E]), ALU.mult))
            m = dve([m], lambda e: e.tensor_reduce(destf[:], picked[:], AX.X, ALU.add))
            m_r = m
            m_d = dve([m], lambda e: e.tensor_copy((dest if put is None else put)[:].rearrange("p t k -> p (t k)"), destf[:]))
            if capacity is not None:
                dve([m_r], lambda e: e.tensor_scalar(dest[:].rearrange("p t k -> p (t k)"), destf[:], float(E * capacity - 1), None, ALU.min))
                m = dve([m], lambda e: e.scalar_tensor_tensor(wts[:], destf[:].rearrange("p (t k) -> p t k", k=K), float(E * capacity),
                                                              top8[:, :, 0:K], ALU.is_lt, ALU.mult))
            else:
                m = dve([], lambda e: e.tensor_copy(wts[:], top8[:, :, 0:K]))
            return m_d

        def dispatch(s_done, dest, K, rows, target, m_d):
            led.wait("pool", [m_d])
            for t in range(NT):
                for k in range(K):
                    nc.gpsimd.indirect_dma_start(out=target, out_offset=bass.IndirectOffsetOnAxis(ap=dest[:, t, k:k + 1], axis=0),
                                                 in_=rows[:, t, :], in_offset=None, bounds_check=target.shape[0] - 1,
                                                 oob_is_err=False).then_inc(s_done, 16)

        def shared_block(i, xT, gate_w, up_w, down_w, widths, hT, sil, acc, gate, before_acc, between):
            m = silu_times_up([], lambda k: xT[:, k, ds(i * (G * P), G * P)], gate_w, up_w, widths, hT, sil, nothing_read())
            m = matmuls([m], [(flat(4, 6)[:, k * C:(k + 1) * C], [(hT[0:w, c, k * P:(k + 1) * P], down_w(c)) for c, w in enumerate(widths)])
                              for k in range(G)])
            if between:
                between()
            led.wait("dve", before_acc)
            for k in range(G):
                src = flat(4, 6)[:, k * C:(k + 1) * C]
                if gate is None:
                    m2 = dve([m], lambda e: e.tensor_copy(acc[:, i * G + k, :], src))
                else:
                    m2 = dve([m], lambda e: e.scalar_tensor_tensor(acc[:, i * G + k, :], src, gate[:, ds(i * G + k, 1)],
                                                                   acc[:, i * G + k, :], ALU.mult, ALU.add))
            return m2

        def expert_blocks(tag, stack, nblocks, source, target, load_weights, weights):
            s_ = buffers(stack)
            SLOTS, STORES, TURN, F2 = 8, 4, 8, 2 * F0
            erow, erowT = s_(tag + "erow", [P, SLOTS, C]), s_(tag + "erowT", [P, 2, CK, P])
            esil, eh, ehT = s_(tag + "esil", [P, 2, F0]), s_(tag + "eh", [P, 2, F0]), s_(tag + "ehT", [FC, 2, 2, P])
            yrow = s_(tag + "yrow", [P, STORES, C])
            s_ew = [sem(f"{tag}expert_loaded_{s}") for s in range(SLOTS)]
            s_ey = [sem(f"{tag}answer_stored_{s}") for s in range(STORES)]
            for s in range(STORES):
                nc.scalar.nop().then_inc(s_ey[s], 16)
            order = []
            for s in range(TURN + 2):
                order += [("rows", s + 1)] if s + 1 < TURN else []
                order += [("hidden", s)] if s < TURN else []
                order += [("turn", s - 1)] if 0 <= s - 1 < TURN else []
                order += [("answer", s - 2)] if 0 <= s - 2 < TURN else []
            order = [("rows", 0)] + order
            last_product = {s: n + 1 for n, (what, s) in enumerate(order) if what == "answer"}
            with led.repeat(nblocks // TURN, pe=4 * TURN, act=3 * TURN, dve=2 * TURN) as i:
                for e in ("pe", "act", "dve"):
                    previous_iteration(e, *[x for x in ("pe", "act", "dve") if x != e])
                m = {}

                def fetch(s):
                    if s < SLOTS:
                        led.wait("sp", [Mark("pe", last_product[s + TURN - SLOTS], led.loop)], back=1)
                    else:
                        led.wait("sp", [m["answer", s - SLOTS]])
                    load(s_ew[s % SLOTS], erow[:, s % SLOTS, :], source[ds((i * TURN + s) * P, P), :])
                    return 16 * (1 + load_weights(s % SLOTS, i * TURN + s, s_ew[s % SLOTS]))

                def rows(s):
                    n = fetched.pop(s)
                    nc.tensor.wait_ge(s_ew[s % SLOTS], n)
                    nc.tensor.nop().then_inc(s_ew[s % SLOTS], -n)
                    mt = transposes([m.get(("rowsT", s - 2))], [(bank[:, s % 2, c * P:(c + 1) * P], erow[:, s % SLOTS, c * P:(c + 1) * P]) for c in range(CK)], ident[:])
                    m["rowsT", s] = act([mt, m.get(("hidden", s - 2))],
                                        lambda e: e.copy(erowT[:, s % 2, :, :].rearrange("p c n -> p (c n)"), bank[:, s % 2, 0:CK * P]))

                def hidden(s):
                    gate_up, _ = weights(s % SLOTS, i * TURN + s)
                    m["hidden", s] = matmuls([m["rowsT", s], m.get(("h", s - 2))],
                                             [(bank[:, 2 + s % 2, 0:F2], [(erowT[:, s % 2, k, :], gate_up(k)) for k in range(CK)])])
                    ms = act([m["hidden", s], m.get(("h", s - 2))], lambda e: e.activation(esil[:, s % 2, :], bank[:, 2 + s % 2, 0:F0], ACT.Silu))
                    m["h", s] = dve([ms, m.get(("turn", s - 2))], lambda e: e.tensor_tensor(eh[:, s % 2, :], esil[:, s % 2, :], bank[:, 2 + s % 2, F0:F2], ALU.mult))

                def turn(s):
                    m["turn", s] = transposes([m["h", s], m.get(("hT", s - 2))],
                                              [(bank[0:FC, 4 + s % 2, c * P:(c + 1) * P], eh[:, s % 2, c * FC:(c + 1) * FC]) for c in range(2)], ident[:])
                    m["hT", s] = dve([m["turn", s], m.get(("answer", s - 2))],
                                     lambda e: e.tensor_copy(ehT[:, s % 2, :, :].rearrange("p c n -> p (c n)"), bank[0:FC, 4 + s % 2, 0:2 * P]))

                def answer(s):
                    _, down = weights(s % SLOTS, i * TURN + s)
                    m["answer", s] = matmuls([m["hT", s], m.get(("y", s - 2))], [(bank[:, 6 + s % 2, 0:C], [(ehT[:, s % 2, c, :], down(c)) for c in range(2)])])
                    nc.scalar.wait_ge(s_ey[s % STORES], 16)
                    nc.scalar.nop().then_inc(s_ey[s % STORES], -16)
                    m["y", s] = act([m["answer", s]], lambda e: e.copy(yrow[:, s % STORES, :], bank[:, 6 + s % 2, 0:C]))
                    led.wait("act", [m["y", s]])
                    nc.scalar.dma_start(target[ds((i * TURN + s) * P, P), :], yrow[:, s % STORES, :]).then_inc(s_ey[s % STORES], 16)
                    if s + SLOTS < TURN:
                        fetched[s + SLOTS] = fetch(s + SLOTS)

                fetched = {s: fetch(s) for s in range(SLOTS)}
                for what, s in order:
                    {"rows": rows, "hidden": hidden, "turn": turn, "answer": answer}[what](s)
                for s in range(TURN):
                    assert m["answer", s].rel == last_product[s]
            for s in range(STORES):
                nc.scalar.wait_ge(s_ey[s], 16)
            act([], lambda e: e.copy(mark[:], eps_ln[:]))

        def combine(tag, stack, K, source, dest, wts, acc, tgate, shared, store=None):
            s_ = buffers(stack)
            got = s_(tag + "got", [P, NT, K, C])
            s_got = [sem(f"{tag}answers_fetched_{t}") for t in range(NT)]
            for t in range(NT):
                for k in range(K):
                    nc.gpsimd.indirect_dma_start(out=got[:, t, k, :], out_offset=None, in_=source,
                                                 in_offset=bass.IndirectOffsetOnAxis(ap=dest[:, t, k:k + 1], axis=0),
                                                 bounds_check=source.shape[0] - 1, oob_is_err=False).then_inc(s_got[t], 16)

            def add(first, after=()):
                m = {}
                led.wait("dve", after)
                for t in range(first, first + G):
                    nc.vector.wait_ge(s_got[t], 16 * K)
                for k in range(K):
                    for t in range(first, first + G):
                        m[t] = dve([m.get(t)], lambda e: e.scalar_tensor_tensor(acc[:, t, :], got[:, t, k, :], wts[:, t, k:k + 1],
                                                                                acc[:, t, :], ALU.mult, ALU.add))
                for t in range(first, first + G):
                    last = dve([m[t]], lambda e: e.scalar_tensor_tensor(x_sb[:, t, :], acc[:, t, :], tgate, x_sb[:, t, :], ALU.mult, ALU.add))
                if store:
                    store(first, last)
                return last

            for i in (2, 3):
                m = shared(i, between=lambda: add(G * (i - 2)))
            add(2 * G, [m])
            add(3 * G)

        mark = sb("mark", [P, 1])

        s_wf, s_wn = sem("ffn0_weights_loaded"), sem("ffn0_norm_loaded")
        s_scatter = sem("rows_dispatched")
        WID0 = [P] * -(-FS0 // P)
        NW0 = len(WID0)
        with ExitStack() as ffn:
            sf = buffers(ffn)
            acc = sf("acc", [P, NT, C])
            xT = sf("xT", [P, CK, NTOK])
            dest = sf("dest", [P, NT, K0], U32)
            wts = sf("wts", [P, NT, K0])
            sgate = sf("sgate", [P, NT])
            swg, swu = sf("swg", [P, CK, NW0 * P]), sf("swu", [P, CK, NW0 * P])
            swd = sf("swd", [P, NW0, C])
            hT, sil = sf("hT", [P, NW0, 512]), sf("sil", [P, 2, 512])

            def shared0(i, before_acc=(), between=None):
                return shared_block(i, xT, lambda c, k: swg[:, k, c * P:(c + 1) * P], lambda c, k: swu[:, k, c * P:(c + 1) * P],
                                    lambda c: swd[:, c, :], WID0, hT, sil, acc, sgate, list(before_acc), between)

            with ExitStack() as routing:
                sr = buffers(routing)
                put = sr("put", [P, NT, K0], U32)
                rows0 = sr("rows0", [P, NT, C])
                logits = sr("logits", [P, NT, E0 + 1])
                wrt, wn = sr("wrt", [P, CK, E0 + 1]), sr("wn", [P, C])
                ss, rinv = sr("ss", [P, NT]), sr("rinv", [P, NT])
                xg, xgT, sqr = sr("xg", [P, G, C]), sr("xgT", [P, CK, G * P]), sr("sqr", [P, G, C])
                load(s_wn, wn[:], a["L0_ffn_w_norm"].partition_broadcast(P))
                load(s_wn, wrt[:, :, 0:E0], a["L0_ffn_w_router"].rearrange("(c p) n -> p c n", p=P))
                with nc.allow_non_contiguous_dma(reason="256 weights, one column"):
                    load(s_wn, wrt[:, :, E0:E0 + 1], a["L0_ffn_w_shared_gate"].rearrange("(c p) n -> p c n", p=P))
                full = FS0 // P * P
                m = [pool([], lambda e: e.memset(swg[:, :, FS0:], 0.0)), pool([], lambda e: e.memset(swu[:, :, FS0:], 0.0)),
                     pool([], lambda e: e.memset(swd[:, NW0 - 1, :], 0.0))]
                led.wait("sp", m)
                load(s_wf, swg[:, :, 0:FS0], a["L0_ffn_sw_gate"].rearrange("(c p) n -> p c n", p=P))
                load(s_wf, swu[:, :, 0:FS0], a["L0_ffn_sw_up"].rearrange("(c p) n -> p c n", p=P))
                load(s_wf, swd[:, 0:FS0 // P, :], a["L0_ffn_sw_down"][0:full, :].rearrange("(c p) n -> p c n", p=P))
                load(s_wf, swd[0:FS0 - full, FS0 // P, :], a["L0_ffn_sw_down"][full:, :])

                m_stats = layer_stats([])
                with led.repeat(NG, dve=4, act=4) as i:
                    for k in range(G):
                        m = dve([m_stats], lambda e: e.tensor_scalar(acc[:, i * G + k, :], x_sb[:, i * G + k, :], rstd[:, ds(i * G + k, 1)],
                                                                     nmr[:, ds(i * G + k, 1)], ALU.mult, ALU.add))
                    previous_iteration("act", "act")
                    for k in range(G):
                        m2 = act([m], lambda e: e.activation(sqr[:, k, :], acc[:, i * G + k, :], ACT.Square, accum_out=ss[:, ds(i * G + k, 1)]))
                m = act([m2], lambda e: e.activation(ss[:], ss[:], ACT.Sqrt, bias=eps_rms[:], scale=1.0 / C))
                m_r = dve([m], lambda e: e.reciprocal(rinv[:], ss[:]))
                nc.vector.wait_ge(s_wn, 48)
                nc.tensor.wait_ge(s_wn, 48)
                with led.repeat(NG, pe=2, dve=5, act=1, pool=2) as i:
                    previous_iteration("dve", "pe", "pool")
                    previous_iteration("pe", "act", "dve")
                    previous_iteration("act", "pe", "pool")
                    for k in range(G):
                        m = dve([m_r], lambda e: e.scalar_tensor_tensor(xg[:, k, :], acc[:, i * G + k, :], rinv[:, ds(i * G + k, 1)], wn[:],
                                                                        ALU.mult, ALU.mult))
                    pool([m], lambda e: e.tensor_copy(rows0[:, ds(i * G, G), :], xg[:]))
                    m = transposes([m], [(flat(0, 2)[:, (c * G + k) * P:(c * G + k + 1) * P], xg[:, k, c * P:(c + 1) * P])
                                         for c in range(CK) for k in range(G)], ident[:])
                    m = act([m], lambda e: e.copy(xgT[:].rearrange("p c n -> p (c n)"), flat(0, 2)))
                    pool([m], lambda e: e.tensor_copy(xT[:, :, ds(i * G * P, G * P)], xgT[:]))
                    m = matmuls([m], [(bank[:, 2, k * (E0 + 1):(k + 1) * (E0 + 1)], [(xgT[:, c, k * P:(k + 1) * P], wrt[:, c, :]) for c in range(CK)])
                                      for k in range(G)])
                    dve([m], lambda e: e.tensor_copy(logits[:, ds(i * G, G), :], bank[:, 2, 0:G * (E0 + 1)].rearrange("p (k n) -> p k n", k=G)))
                led.meet()

                m_d = route("r0_", routing, logits[:, :, 0:E0], E0, K0, [], CAP, dest, wts, put=put)
                m = dve([], lambda e: e.tensor_scalar(sgate[:], logits[:, :, E0], -1.0, 87.0, ALU.mult, ALU.min))
                m = act([m], lambda e: e.activation(sgate[:], sgate[:], ACT.Exp))
                m = dve([m], lambda e: e.tensor_scalar(sgate[:], sgate[:], 1.0, None, ALU.add))
                m_sg = dve([m], lambda e: e.reciprocal(sgate[:], sgate[:]))
                nc.gpsimd.wait_ge(s_zero, 16 * ZEROED)
                dispatch(s_scatter, put, K0, rows0, dispatched, m_d)

                nc.tensor.wait_ge(s_wf, 64)
                with led.repeat(2, pe=13, act=6, dve=10) as i:
                    previous_iteration("pe", "act", "dve")
                    previous_iteration("act", "dve")
                    previous_iteration("dve", "pe")
                    shared0(i, [m_sg])
                led.meet()
                for e in ("sp", "pool"):
                    led.engines[e].wait_ge(s_scatter, 16 * NT * K0)

            with ExitStack() as experts:
                se = buffers(experts)
                wgu, wdn = se("wgu", [P, 8, CK, 2, F0]), se("wdn", [FC, 8, 2, C])

                def load_expert(s, e, signal):
                    load(signal, wgu[:, s, :, 0, :], a["L0_ffn_w_gate"][e].rearrange("(c p) n -> p c n", p=P))
                    load(signal, wgu[:, s, :, 1, :], a["L0_ffn_w_up"][e].rearrange("(c p) n -> p c n", p=P))
                    load(signal, wdn[:, s, :, :], a["L0_ffn_w_down"][e].rearrange("(c p) n -> p c n", p=FC))
                    return 3

                expert_blocks("x0_", experts, E0, dispatched, answered, load_expert,
                              lambda s, e: (lambda k: wgu[:, s, k, :, :].rearrange("p u n -> p (u n)"), lambda c: wdn[:, s, c, :]))
                led.meet()
            with ExitStack() as combining:
                combine("c0_", combining, K0, answered, dest, wts, acc, tgates[:, 2:3], shared0)
                led.meet()

        def normalised_groups(stack, tag, m_stats, destT, extra=None, rows=None):
            s = buffers(stack)
            xg, xgT = s(tag + "xg", [P, G, C]), s(tag + "xgT", [P, CK, G * P])
            per = dict(pe=1, dve=4, act=1, pool=1)
            if extra:
                per = dict(pe=2, dve=5, act=1, pool=2)
            with led.repeat(NG, **per) as i:
                previous_iteration("dve", "pe", "pool")
                previous_iteration("pe", "act", "dve")
                previous_iteration("act", "pe", "pool")
                for k in range(G):
                    m = dve([m_stats], lambda e: e.tensor_scalar(xg[:, k, :], x_sb[:, i * G + k, :], rstd[:, ds(i * G + k, 1)],
                                                                 nmr[:, ds(i * G + k, 1)], ALU.mult, ALU.add))
                if rows is not None:
                    pool([m], lambda e: e.tensor_copy(rows[:, ds(i * G, G), :], xg[:]))
                m = transposes([m], [(flat(0, 2)[:, (c * G + k) * P:(c * G + k + 1) * P], xg[:, k, c * P:(c + 1) * P])
                                     for c in range(CK) for k in range(G)], ident[:])
                m = act([m], lambda e: e.copy(xgT[:].rearrange("p c n -> p (c n)"), flat(0, 2)))
                pool([m], lambda e: e.tensor_copy(destT[:, :, ds(i * G * P, G * P)], xgT[:]))
                if extra:
                    extra(i, xgT, m)

        s_td = sem("decay_weights_loaded")
        with ExitStack() as mixing:
            sm = buffers(mixing)
            kc = sm("kc", [P, CK, NTOK])
            decay, u_first = sm("decay", [P, CK]), sm("u_first", [P, CK])
            fade = sm("fade", [P, NTOK])
            ek, ekv = sm("ek", [P, NTOK]), sm("ekv", [P, NTOK])
            sumk, sumkv = sm("sumk", [P, NTOK]), sm("sumkv", [P, NTOK])
            ceil, eu, ec = sm("ceil", [P, NTOK]), sm("eu", [P, NTOK]), sm("ec", [P, NTOK])
            with nc.allow_non_contiguous_dma(reason="256 values, one per partition"):
                load(s_td, decay[:], a["L1_xattn_time_decay"].rearrange("(c p) -> p c", p=P))
                load(s_td, u_first[:], a["L1_xattn_time_first"].rearrange("(c p) -> p c", p=P))
            m_stats = layer_stats([])
            normalised_groups(mixing, "mix_", m_stats, kc)
            led.meet()
            nc.scalar.wait_ge(s_td, 32)
            nc.vector.wait_ge(s_td, 32)
            m = dve([], lambda e: e.tensor_scalar(decay[:], decay[:], 80.0, None, ALU.min))
            m = act([m], lambda e: e.activation(decay[:], decay[:], ACT.Exp))
            m_dec = act([m], lambda e: e.activation(decay[:], decay[:], ACT.Exp, scale=-1.0))
            for c in range(CK):
                k_, v_ = kc[:, c, :], ctxT[:, c, :]
                m_k = act([], lambda e: e.activation(ek[:], k_, ACT.Exp))
                m_c = dve([], lambda e: e.tensor_scalar(ceil[:], k_, u_first[:, c:c + 1], 0.0, ALU.add, ALU.max))
                m_f = dve([], lambda e: e.memset(fade[:], 1.0))
                m_f = dve([m_f, m_dec], lambda e: e.tensor_scalar(fade[:], fade[:], decay[:, c:c + 1], None, ALU.mult))
                m_f = dve([m_f], lambda e: e.memset(fade[:, 0:NTOK:T], 0.0))
                m_ec = act([m_c], lambda e: e.activation(ec[:], ceil[:], ACT.Exp, scale=-1.0))
                m_kc = pool([m_ec], lambda e: e.tensor_tensor(ceil[:], k_, ceil[:], ALU.subtract))
                m_eu = act([m_kc], lambda e: e.activation(eu[:], ceil[:], ACT.Exp, bias=u_first[:, c:c + 1]))
                m_sk = dve([m_f, m_k], lambda e: e.tensor_tensor_scan(sumk[:], fade[:], ek[:], 0.0, ALU.mult, ALU.add))
                m_kv = dve([m_k], lambda e: e.tensor_tensor(ekv[:], ek[:], v_, ALU.mult))
                m_skv = dve([m_kv], lambda e: e.tensor_tensor_scan(sumkv[:], fade[:], ekv[:], 0.0, ALU.mult, ALU.add))
                m_d = dve([m_sk, m_ec, m_kv], lambda e: e.tensor_tensor(ek[:, 1:], ec[:, 1:], sumk[:, 0:NTOK - 1], ALU.mult))
                m_d = dve([m_d, m_eu], lambda e: e.tensor_tensor(ek[:, 1:], ek[:, 1:], eu[:, 1:], ALU.add))
                m_d = dve([m_d], lambda e: e.reciprocal(ek[:, 1:], ek[:, 1:]))
                m_ev = pool([m_eu], lambda e: e.tensor_tensor(ceil[:], eu[:], v_, ALU.mult))
                m_n = dve([m_skv, m_ec], lambda e: e.tensor_tensor(ekv[:, 1:], ec[:, 1:], sumkv[:, 0:NTOK - 1], ALU.mult))
                m_n = dve([m_n, m_ev], lambda e: e.tensor_tensor(ekv[:, 1:], ekv[:, 1:], ceil[:, 1:], ALU.add))
                m_n = dve([m_n, m_d], lambda e: e.tensor_tensor(kc[:, c, 1:], ekv[:, 1:], ek[:, 1:], ALU.mult))
                dve([m_n], lambda e: e.tensor_copy(kc[:, c, 0:NTOK:T], ctxT[:, c, 0:NTOK:T]))
                led.meet()

            y_g = sm("y_g", [P, CK, G * P])
            with led.repeat(NG, pe=1, pool=1, dve=G) as i:
                previous_iteration("pe", "dve")
                previous_iteration("pool", "pe")
                m = pool([], lambda e: e.tensor_copy(y_g[:], kc[:, :, ds(i * G * P, G * P)]))
                m = transposes([m], [(flat(0, 2)[:, k * C + c * P:k * C + (c + 1) * P], y_g[:, c, k * P:(k + 1) * P])
                                     for k in range(G) for c in range(CK)], ident[:])
                for k in range(G):
                    dve([m], lambda e: e.scalar_tensor_tensor(x_sb[:, i * G + k, :], flat(0, 2)[:, k * C:(k + 1) * C], tgates[:, 1:2],
                                                              x_sb[:, i * G + k, :], ALU.mult, ALU.add))
            led.meet()

        s_w1, s_v1 = sem("ffn1_weights_loaded"), sem("ffn1_router_loaded")
        s_scatter1 = sem("rows_dispatched_1")
        s_out = sem("output_stored")
        WID1 = [P] * (FS1 // P) + ([FS1 % P] if FS1 % P else [])
        with ExitStack() as ffn1:
            s1 = buffers(ffn1)
            acc1 = s1("acc1", [P, NT, C])
            xT1 = s1("xT1", [P, CK, NTOK])
            dest1, wts1 = s1("dest1", [P, NT, K1], U32), s1("wts1", [P, NT, K1])
            owner = s1("owner", [P, NBLOCKS1], U32)
            w1gu = s1("w1gu", [P, E1, CK, 2 * F1])
            w1d = s1("w1d", [FC, E1, 2, C])
            v1g, v1u = s1("v1g", [P, CK, FS1]), s1("v1u", [P, CK, FS1])
            v1d = s1("v1d", [P, len(WID1), C])
            hT1, sil1 = s1("hT1", [P, len(WID1), 512]), s1("sil1", [P, 2, 512])

            def shared1(i, before_acc=(), between=None):
                return shared_block(i, xT1, lambda c, k: v1g[:, k, c * P:c * P + WID1[c]], lambda c, k: v1u[:, k, c * P:c * P + WID1[c]],
                                    lambda c: v1d[0:WID1[c], c, :], WID1, hT1, sil1, acc1, None, list(before_acc), between)

            with ExitStack() as routing1:
                sr = buffers(routing1)
                rows1 = sr("rows1", [P, NT, C])
                w1r, logits1 = sr("w1r", [P, CK, E1]), sr("logits1", [P, NT, E1])
                load(s_v1, w1r[:], a["L1_ffn_gate_w"].rearrange("(c p) n -> p c n", p=P))
                load(s_v1, v1g[:], a["L1_ffn_sw_gate"].rearrange("(c p) n -> p c n", p=P))
                load(s_v1, v1u[:], a["L1_ffn_sw_up"].rearrange("(c p) n -> p c n", p=P))
                for c, w in enumerate(WID1):
                    load(s_v1, v1d[0:w, c, :], a["L1_ffn_sw_down"][c * P:c * P + w, :])
                for e in range(E1):
                    load(s_w1, w1gu[:, e, :, 0:F1], a["L1_ffn_w_gate"][e].rearrange("(c p) n -> p c n", p=P))
                    load(s_w1, w1gu[:, e, :, F1:], a["L1_ffn_w_up"][e].rearrange("(c p) n -> p c n", p=P))
                    load(s_w1, w1d[:, e, :, :], a["L1_ffn_w_down"][e].rearrange("(c p) n -> p c n", p=FC))
                nc.tensor.wait_ge(s_v1, 16 * (3 + len(WID1)))

                def router1(i, xgT, m):
                    m = matmuls([m], [(bank[:, 2, k * E1:(k + 1) * E1], [(xgT[:, c, k * P:(k + 1) * P], w1r[:, c, :]) for c in range(CK)]) for k in range(G)])
                    dve([m], lambda e: e.tensor_copy(logits1[:, ds(i * G, G), :], bank[:, 2, 0:G * E1].rearrange("p (k n) -> p k n", k=G)))

                m_stats = layer_stats([])
                normalised_groups(routing1, "ffn1_", m_stats, xT1, router1, rows1)
                led.meet()
                m_d = route("r1_", routing1, logits1[:], E1, K1, [], None, dest1, wts1, owner[:])
                dispatch(s_scatter1, dest1, K1, rows1, dispatched1, m_d)
                with led.repeat(2, pe=7, act=3, dve=7) as i:
                    previous_iteration("pe", "act", "dve")
                    previous_iteration("act", "dve")
                    previous_iteration("dve", "pe")
                    shared1(i)
                led.meet()
                for e in ("sp", "pool"):
                    led.engines[e].wait_ge(s_scatter1, 16 * NT * K1)

            with ExitStack() as experts1:
                nc.tensor.wait_ge(s_w1, 16 * 3 * E1)
                expert_of = {}

                def weights1(s, block):
                    if s not in expert_of or expert_of[s][0] is not led.loop or expert_of[s][2] == 2:
                        expert_of[s] = [led.loop, nc.tensor.value_load(owner[0:1, ds(block, 1)], min_val=0, max_val=E1 - 1), 0]
                    expert_of[s][2] += 1
                    r = expert_of[s][1]
                    return lambda k: w1gu[:, r, k, :], lambda c: w1d[:, r, c, :]

                expert_blocks("x1_", experts1, NBLOCKS1, dispatched1, answered1, lambda s, block, signal: 0, weights1)
                led.meet()

                def store(t, m):
                    led.wait("sp", [m])
                    nc.sync.dma_start(outr[:, t:t + G, :], x_sb[:, t:t + G, :]).then_inc(s_out, 16)

                combine("c1_", experts1, K1, answered1, dest1, wts1, acc1, tgates[:, 3:4], shared1, store)
                nc.sync.wait_ge(s_out, 16 * NG)
                led.meet()


def kernel(**inputs):
    import numpy as _np
    import concourse.bacc as _bacc
    from concourse.bass_utils import run_bass_kernel_spmd as _run

    nc = _bacc.Bacc("TRN2", target_bir_lowering=False, num_devices=1)
    arrays, args = {}, {}
    for name, value in inputs.items():
        arrays[f"in_{name}"] = _np.ascontiguousarray(value)
        args[name] = nc.dram_tensor(f"in_{name}", arrays[f"in_{name}"].shape, mybir.dt.from_np(arrays[f"in_{name}"].dtype),
                                    kind="ExternalInput").ap()
    result = nc.dram_tensor("result", inputs["x"].shape, F32, kind="ExternalOutput").ap()
    program(nc, args, result)
    return _run(nc, [arrays], core_ids=[0]).results[0]["result"]
```

```python
from contextlib import ExitStack, contextmanager

import numpy as np

import concourse.bass as bass
from concourse import mybir

ALU = mybir.AluOpType
ACT = mybir.ActivationFunctionType
AX = mybir.AxisListType
F32 = mybir.dt.float32
BF16 = mybir.dt.bfloat16
F16 = mybir.dt.float16
U8 = mybir.dt.uint8
U16 = mybir.dt.uint16
U32 = mybir.dt.uint32
ds = bass.ds

P = 128
ROUND = 12582912.0
LN_EPS = 1e-5
RMS_EPS = 1e-6
FAR = float(1 << 20)


class Mark:

    def __init__(self, name, rel, loop):
        self.name, self.rel, self.loop = name, rel, loop


class Loop:
    def __init__(self, number, i, n, per, start):
        self.number, self.i, self.n, self.per, self.start, self.open = number, i, n, per, start, True


class Ledger:

    HEAD_START = 1024

    def __init__(self, nc, ctx):
        self.nc = nc
        self.engines = {"pe": nc.tensor, "dve": nc.vector, "act": nc.scalar, "pool": nc.gpsimd, "sp": nc.sync}
        self.sem = {n: ctx.enter_context(nc.semaphore(f"finished_{n}")) for n in ("pe", "dve", "act", "pool")}
        self.count = {n: self.HEAD_START for n in self.sem}
        self.loop = None
        self.loops = 0
        self.seen = {}
        for n in self.sem:
            self.engines[n].sem_inc(self.sem[n], self.HEAD_START)

    def done(self, name, instruction):
        self.count[name] += 1
        instruction.then_inc(self.sem[name], 1)
        return Mark(name, self.count[name], self.loop)

    def wait(self, waiter, marks, back=0):
        best = {}
        for m in marks:
            if m is None:
                continue
            key = (m.name, m.loop.number if m.loop else 0)
            if key not in best or best[key].rel < m.rel:
                best[key] = m
        for m in best.values():
            lp = m.loop
            if lp is None:
                known, value = m.rel, m.rel
            elif lp.open:
                known, value = None, lp.i * lp.per[m.name] + (lp.start[m.name] + m.rel - back * lp.per[m.name])
            else:
                known = value = lp.start[m.name] + (lp.n - 1) * lp.per[m.name] + m.rel
            key = (waiter, m.name)
            if known is not None:
                if self.seen.get(key, 0) >= known:
                    continue
                self.seen[key] = known
            else:
                key = (waiter, m.name, lp.number)
                if self.seen.get(key, -10**9) >= m.rel - back * lp.per[m.name]:
                    continue
                self.seen[key] = m.rel - back * lp.per[m.name]
            self.engines[waiter].wait_ge(self.sem[m.name], value)

    def run(self, name, after, build):
        self.wait(name, after)
        return self.done(name, build(self.engines[name]))

    @contextmanager
    def repeat(self, n, **per):
        per = {e: per.get(e, 0) for e in self.sem}
        start = dict(self.count)
        with self.nc.Fori(0, n) as i:
            self.loops += 1
            self.loop = Loop(self.loops, i, n, per, start)
            self.count = {e: 0 for e in self.sem}
            yield i
            assert self.count == per, f"counts in one iteration: {self.count}"
        self.loop.open = False
        self.loop = None
        self.count = {e: start[e] + n * per[e] for e in self.sem}

    def meet(self):
        marks = [Mark(n, self.count[n], None) for n in self.sem]
        for waiter in self.engines:
            self.wait(waiter, marks)


def program(nc, a, out):
    x, ctx_in = a["x"], a["ctx_2048"]
    B, T, C = x.shape
    NT = B
    NTOK = NT * T
    H = 16
    HD = C // H
    CK = C // P
    NPAIR = H // 2
    KB = 64
    E0, K0, F0 = a["L0_ffn_w_gate"].shape[0], 4, a["L0_ffn_w_gate"].shape[2]
    CAP = 128
    FS0 = a["L0_ffn_sw_gate"].shape[1]
    E1, K1, F1 = a["L1_ffn_w_gate"].shape[0], 2, a["L1_ffn_w_gate"].shape[2]
    FS1 = a["L1_ffn_sw_gate"].shape[1]
    FC = F0 // 2
    G = 4
    NG = NT // G
    assert T == P and F0 == F1 and CK == 2 and NTOK == 2048

    dispatched = nc.dram_tensor("dispatched_rows", [E0 * CAP, C], F32).ap()
    answered = nc.dram_tensor("answered_rows", [E0 * CAP, C], F32).ap()
    NBLOCKS1 = -(-(NTOK * K1 // P + E1) // 8) * 8
    dispatched1 = nc.dram_tensor("dispatched_rows_1", [NBLOCKS1 * P, C], F32).ap()
    answered1 = nc.dram_tensor("answered_rows_1", [NBLOCKS1 * P, C], F32).ap()
    ZEROED = (E0 * CAP + NBLOCKS1 * P) // 512

    with ExitStack() as whole:
        led = Ledger(nc, whole)

        def sem(name):
            return whole.enter_context(nc.semaphore(name))

        def dve(after, build):
            return led.run("dve", after, build)

        def act(after, build):
            return led.run("act", after, build)

        def pool(after, build):
            return led.run("pool", after, build)

        def buffers(stack):
            return lambda name, shape, dt=F32: stack.enter_context(nc.sbuf_tensor(name, shape, dt))

        sb = buffers(whole)
        bank = whole.enter_context(nc.psum_tensor("bank", [P, 8, 512], F32))

        def flat(b0, b1):
            return bank[:, b0:b1, :].rearrange("p b n -> p (b n)")

        def matmuls(after, groups):
            led.wait("pe", after)
            for dst, terms in groups:
                for n, (lhsT, rhs) in enumerate(terms):
                    mm = nc.tensor.matmul(dst, lhsT, rhs, start=(n == 0), stop=(n == len(terms) - 1))
            return led.done("pe", mm)

        def transposes(after, pairs, ident):
            led.wait("pe", after)
            for dst, src in pairs:
                mm = nc.tensor.transpose(dst, src, ident)
            return led.done("pe", mm)

        def previous_iteration(waiter, *names):
            for n in names:
                led.wait(waiter, [Mark(n, led.loop.per[n], led.loop)], back=1)

        x_sb = sb("x_sb", [P, NT, C])
        ctxT = sb("ctxT", [P, CK, NTOK])
        ident = sb("ident", [P, P])
        ident_b = sb("ident_b", [P, P], BF16)
        ones_row = sb("ones_row", [1, P])
        eps_ln = sb("eps_ln", [P, 1])
        eps_rms = sb("eps_rms", [P, 1])
        gates = sb("gates", [P, 4])
        tgates = sb("tgates", [P, 4])
        stats = sb("stats", [P, NT, 6])
        mv = sb("mv", [P, NT, 2])
        std = sb("std", [P, NT])
        rstd = sb("rstd", [P, NT])
        nmr = sb("nmr", [P, NT])

        s_x = [sem(f"x_loaded_{g}") for g in range(NG)]
        s_ctx = [sem(f"ctx_loaded_{g}") for g in range(NG)]
        s_wa, s_wp, s_g = sem("attention_weights_loaded"), sem("projection_weights_loaded"), sem("gates_loaded")
        s_zero = sem("dispatched_rows_zeroed")

        xr = x.rearrange("t p c -> p t c")
        cr = ctx_in.rearrange("t p c -> p t c")
        outr = out.rearrange("t p c -> p t c")

        with ExitStack() as attention:
            sa = buffers(attention)
            kT = sa("kT", [P, NPAIR, NTOK], BF16)
            qT_all = sa("qT_all", [P, NPAIR, (NT + 1) * P], BF16)
            v_sb = sa("v_sb", [P, NT, C], BF16)
            sq_all = sa("sq_all", [P, (NT + 1) * H])
            nsq_all = sa("nsq_all", [P, (NT + 1) * H])
            wp = sa("wp", [P, CK, C])
            q_cur = sa("q_cur", [P, H, P], BF16)
            bp_all = sa("bp_all", [P, C])

            with ExitStack() as prepare:
                sp_ = buffers(prepare)
                ctx_sb = sp_("ctx_sb", [P, NT, C])
                vT = sp_("vT", [P, CK, NTOK])
                wq, wkv = sp_("wq", [P, CK, C]), sp_("wkv", [P, CK, 2 * C])
                bq_row, bk_row = sp_("bq_row", [1, C]), sp_("bk_row", [1, C])
                bv = sp_("bv", [P, CK])
                xn = sp_("xn", [P, G, C])
                xnT = sp_("xnT", [P, CK, G * P])
                y1, y2 = sp_("y1", [P, G, C]), sp_("y2", [P, G, C])
                qint = sp_("qint", [P, G, C], BF16)
                qrep = sp_("qrep", [P, G, H, KB], BF16)
                ksplit = sp_("ksplit", [P, G, H, KB], BF16)
                small = sp_("small", [P, 3, G * H])
                vmax = sp_("vmax", [P, CK, NG])

                def fetch_tokens(g):
                    nc.sync.dma_start(x_sb[:, g * G:(g + 1) * G, :], xr[:, g * G:(g + 1) * G, :]).then_inc(s_x[g], 16)
                    nc.scalar.dma_start(ctx_sb[:, g * G:(g + 1) * G, :], cr[:, g * G:(g + 1) * G, :]).then_inc(s_ctx[g], 16)

                fetch_tokens(0)
                nc.sync.dma_start(wq[:], a["L0_xattn_Wq"].rearrange("(c p) n -> p c n", p=P)).then_inc(s_wa, 16)
                nc.sync.dma_start(bq_row[:], a["L0_xattn_bq"].rearrange("(a n) -> a n", a=1)).then_inc(s_wa, 16)
                nc.scalar.dma_start(wkv[:], a["L0_xattn_Wkv"].rearrange("(c p) n -> p c n", p=P)).then_inc(s_wa, 16)
                nc.scalar.dma_start(bk_row[:], a["L0_xattn_bkv"][0:C].rearrange("(a n) -> a n", a=1)).then_inc(s_wa, 16)
                with nc.allow_non_contiguous_dma(reason="256 biases, one per partition"):
                    nc.sync.dma_start(bv[:], a["L0_xattn_bkv"][C:2 * C].rearrange("(c p) -> p c", p=P)).then_inc(s_wa, 16)
                for g in range(1, NG):
                    fetch_tokens(g)
                nc.sync.dma_start(wp[:], a["L0_xattn_Wp"].rearrange("(c p) n -> p c n", p=P)).then_inc(s_wp, 16)
                nc.sync.dma_start(bp_all[:], a["L0_xattn_bp"].partition_broadcast(P)).then_inc(s_wp, 16)
                nc.sync.dma_start(gates[:, 0:2], a["g_xattn"].partition_broadcast(P)).then_inc(s_g, 16)
                nc.sync.dma_start(gates[:, 2:4], a["g_ffn"].partition_broadcast(P)).then_inc(s_g, 16)

                m = pool([], lambda e: e.memset(ident[:], 0.0))
                m_id = pool([m], lambda e: e.affine_select(out=ident[:], in_=ident[:], compare_op=ALU.not_equal, fill=1.0,
                                                           base=0, pattern=[[-1, P]], channel_multiplier=1))
                m_idb = pool([m_id], lambda e: e.tensor_copy(ident_b[:], ident[:]))
                pool([], lambda e: e.memset(ones_row[:], 1.0))
                m_pad = [pool([], lambda e: e.memset(qrep[:, :, :, 3 * HD:KB], 0.0)),
                         pool([], lambda e: e.memset(ksplit[:, :, :, 3 * HD:KB], 0.0)),
                         pool([], lambda e: e.memset(qT_all[:, :, NT * P:], 0.0)),
                         pool([], lambda e: e.memset(sq_all[:, NT * H:], 0.0)),
                         pool([], lambda e: e.memset(nsq_all[:, NT * H:], 0.0))]
                pool([], lambda e: e.memset(q_cur[:], 0.0))
                m_eps = dve([], lambda e: e.memset(eps_ln[:], LN_EPS))
                dve([], lambda e: e.memset(eps_rms[:], RMS_EPS))

                def tile_stats(t, ready):
                    return dve(ready, lambda e: e.bn_stats(stats[:, t, :], x_sb[:, t, :]))

                def layer_stats(m, t0=0, t1=NT):
                    led.wait("dve", [m])
                    for t in range(t0, t1):
                        m = dve([], lambda e: e.bn_aggr(mv[:, t, :], stats[:, t, :]))
                    m = act([m, m_eps], lambda e: e.activation(std[:, t0:t1], mv[:, t0:t1, 1], ACT.Sqrt, bias=eps_ln[:], scale=1.0))
                    m = dve([m], lambda e: e.reciprocal(rstd[:, t0:t1], std[:, t0:t1]))
                    return dve([m], lambda e: e.scalar_tensor_tensor(nmr[:, t0:t1], mv[:, t0:t1, 0], -1.0, rstd[:, t0:t1], ALU.mult, ALU.mult))

                def first_stats(t0, t1):
                    for t in range(t0, t1):
                        if t % G == 0:
                            nc.vector.wait_ge(s_x[t // G], 16)
                        m = tile_stats(t, [])
                    return layer_stats(m, t0, t1)

                for e in ("pe", "act"):
                    led.engines[e].wait_ge(s_wa, 16 * 5)
                led.wait("pe", [m_idb])
                led.wait("act", m_pad)
                led.wait("pool", m_pad)
                led.wait("dve", m_pad)
                M = {}

                def turned_in(src, banks, after):
                    return transposes(after, [(flat(*banks)[:, (c * G + k) * P:(c * G + k + 1) * P], src[:, k, c * P:(c + 1) * P])
                                              for c in range(CK) for k in range(G)], ident[:])

                def project(m_in, srcT, w, c0, bias, banks):
                    return matmuls(m_in, [(flat(*banks)[:, k * C:(k + 1) * C],
                                           [(ones_row[:], bias[:])] + [(srcT[:, c, k * P:(k + 1) * P], w[:, c, c0:c0 + C]) for c in range(CK)])
                                          for k in range(G)])

                def inputs(g):
                    led.wait("dve", [M.get(("turn x", g - 1)), first_stats(0, G) if g == 0 else m_stats])
                    for k in range(G):
                        t = g * G + k
                        m = dve([], lambda e: e.tensor_scalar(xn[:, k, :], x_sb[:, t, :], rstd[:, t:t + 1], nmr[:, t:t + 1], ALU.mult, ALU.add))
                    M["turn x", g] = turned_in(xn, (0, 2), [m, M.get(("v out", g - 1))])
                    M["x turned", g] = act([M["turn x", g], M.get(("q product", g - 1))],
                                           lambda e: e.copy(xnT[:].rearrange("p c n -> p (c n)"), flat(0, 2)))
                    nc.tensor.wait_ge(s_ctx[g], 16)
                    m = turned_in(ctx_sb[:, g * G:(g + 1) * G, :], (6, 8), [M.get(("k back", g - 2, 2)), M.get(("k back", g - 2, 3))])
                    M["c turned", g] = act([m], lambda e: e.copy(ctxT[:, :, g * G * P:(g + 1) * G * P], flat(6, 8).rearrange("p (c n) -> p c n", c=CK)))

                def q_products(g):
                    M["q product", g] = project([M["x turned", g], M.get(("q read", g - 1))], xnT, wq, 0, bq_row, (2, 4))

                def k_products(g):
                    cT = ctxT[:, :, g * G * P:(g + 1) * G * P]
                    M["k product", g] = project([M["c turned", g], M.get(("k read", g - 1))], cT, wkv, 0, bk_row, (4, 6))

                def v_products(g):
                    cT = ctxT[:, :, g * G * P:(g + 1) * G * P]
                    m = matmuls([], [(bank[:, c, :], [(wkv[:, k, C + c * P:C + (c + 1) * P], cT[:, k, :]) for k in range(CK)]) for c in range(CK)])
                    for c in range(CK):
                        M["v out", g] = act([m], lambda e: e.activation(vT[:, c, g * G * P:(g + 1) * G * P], bank[:, c, :], ACT.Identity,
                                                                        bias=bv[:, c:c + 1], scale=1.0))

                def value_maxima(g):
                    M["v max", g] = dve([M["v out", g]], lambda e: e.tensor_reduce(vmax[:, :, g], vT[:, :, g * G * P:(g + 1) * G * P], AX.X, ALU.max,
                                                                                   apply_absolute_value=True))

                def quantise(m_in, banks, premult, sc, rc, y):
                    src = flat(*banks).rearrange("p (t h d) -> p (t h) d", t=G, h=H)
                    m = dve([m_in], lambda e: e.tensor_reduce(rc, src, AX.X, ALU.max, apply_absolute_value=True))
                    m_s = dve([m], lambda e: e.tensor_scalar(sc, rc, premult / 127.0, 1e-8, ALU.mult, ALU.max))
                    m = dve([m_s], lambda e: e.reciprocal(rc, sc))
                    if premult != 1.0:
                        m = dve([m], lambda e: e.tensor_scalar(rc, rc, premult, None, ALU.mult))
                    m_y = dve([m], lambda e: e.tensor_tensor(y, src, rc.unsqueeze(2).broadcast_to([P, G * H, HD]), ALU.mult))
                    m = dve([m_y], lambda e: e.tensor_scalar(y, y, 127.0, -127.0, ALU.min, ALU.max))
                    return m_s, m_y, m

                def heads(buffer):
                    return buffer[:].rearrange("p t (h d) -> p (t h) d", h=H)

                def thirds(buffer, r):
                    return buffer[:, :, :, r * HD:(r + 1) * HD].rearrange("p t h d -> p (t h) d")

                def quantise_q(g):
                    sc = sq_all[:, g * G * H:(g + 1) * G * H]
                    m_s, M["q read", g], m = quantise(M["q product", g], (2, 4), 0.25, sc, small[:, 0, :], heads(y1))
                    pool([m_s], lambda e: e.tensor_scalar(nsq_all[:, g * G * H:(g + 1) * G * H], sc, -1.0, None, ALU.mult))
                    m = dve([m, M.get(("q thrice", g - 1))], lambda e: e.tensor_scalar(qint[:], y1[:], ROUND, -ROUND, ALU.add, ALU.add))
                    led.wait("act", [m, M.get(("q back", g - 1, 3))])
                    for r in range(3):
                        M["q thrice", g] = act([], lambda e: e.copy(thirds(qrep, r), heads(qint)))

                def quantise_k(g):
                    sc = small[:, 1, :]
                    _, M["k read", g], m = quantise(M["k product", g], (4, 6), 1.0, sc, small[:, 2, :], heads(y2))
                    m = dve([m], lambda e: e.tensor_scalar(y2[:], y2[:], ROUND, -ROUND, ALU.add, ALU.add))
                    m = dve([m], lambda e: e.tensor_tensor(heads(y2), heads(y2), sc.unsqueeze(2).broadcast_to([P, G * H, HD]), ALU.mult))
                    m = act([m, M.get(("k turn", g - 1, 3))], lambda e: e.copy(thirds(ksplit, 0), heads(y2)))
                    m = dve([m], lambda e: e.tensor_tensor(heads(y2), heads(y2), thirds(ksplit, 0), ALU.subtract))
                    m = act([m], lambda e: e.copy(thirds(ksplit, 1), heads(y2)))
                    M["k split", g] = dve([m], lambda e: e.tensor_tensor(thirds(ksplit, 2), heads(y2), thirds(ksplit, 1), ALU.subtract))

                def turn_back(what, g, m_in, src, put):
                    for k in range(G):
                        view = bank[:, 6 + k % 2, :].bitcast(BF16)
                        m = transposes([m_in, M.get("bank free %d" % (k % 2))],
                                       [(view[:, p * P:(p + 1) * P], src[:, k, 2 * p:2 * p + 2, :].rearrange("p h d -> p (h d)"))
                                        for p in range(NPAIR)], ident_b[:])
                        M[what + " turn", g, k] = m
                        M[what + " back", g, k] = M["bank free %d" % (k % 2)] = put(g, k, m, view.rearrange("p (a n) -> p a n", a=NPAIR))

                def put_q(g, k, m, view):
                    return act([m], lambda e: e.copy(qT_all[:, :, (g * G + k) * P:(g * G + k + 1) * P], view))

                def put_k(g, k, m, view):
                    first = g * G * P + (k // 2) * 2 * P + k % 2
                    return dve([m], lambda e: e.tensor_copy(kT[:, :, first:first + 2 * P - 1:2], view))

                inputs(0)
                m_stats = first_stats(G, NT)
                M["bank free 0"] = M["bank free 1"] = M["c turned", 0]
                q_products(0)
                k_products(0)
                v_products(0)
                for g in range(NG):
                    if g + 1 < NG:
                        inputs(g + 1)
                        M["bank free 0"] = M["bank free 1"] = M["c turned", g + 1]
                    quantise_q(g)
                    if g + 1 < NG:
                        q_products(g + 1)
                    quantise_k(g)
                    value_maxima(g)
                    if g + 1 < NG:
                        k_products(g + 1)
                    turn_back("q", g, M["q thrice", g], qrep, put_q)
                    turn_back("k", g, M["k split", g], ksplit, put_k)
                    if g + 1 < NG:
                        v_products(g + 1)
                led.meet()

                nc.scalar.wait_ge(s_g, 32)
                m_tanh = act([], lambda e: e.activation(tgates[:], gates[:], ACT.Tanh))

                nc.vector.wait_ge(s_wp, 32)
                sv, rv = small[:, 0, 0:CK], small[:, 1, 0:CK]
                m = dve([], lambda e: e.tensor_reduce(sv, vmax[:], AX.X, ALU.max))
                m_sv = dve([m], lambda e: e.tensor_scalar(sv, sv, 1.0 / 127.0, 1e-8, ALU.mult, ALU.max))
                m = dve([m_sv], lambda e: e.reciprocal(rv, sv))
                vint = ctx_sb[:].rearrange("p t c -> p (t c)").bitcast(BF16)[:, 0:CK * NTOK].rearrange("p (c n) -> p c n", c=CK)
                for c in range(CK):
                    mc = dve([m], lambda e: e.tensor_scalar(vT[:, c, :], vT[:, c, :], rv[:, c:c + 1], 127.0, ALU.mult, ALU.min))
                    mc = dve([mc], lambda e: e.tensor_scalar(vT[:, c, :], vT[:, c, :], -127.0, ROUND, ALU.max, ALU.add))
                    mc = dve([mc], lambda e: e.tensor_scalar(vint[:, c, :], vT[:, c, :], -ROUND, None, ALU.add))
                    for b in range(2):
                        view = bank[:, 2 * c + b, :].bitcast(BF16)
                        mt = transposes([mc], [(view[:, k * P:(k + 1) * P], vint[:, c, (8 * b + k) * P:(8 * b + k + 1) * P]) for k in range(8)], ident_b[:])
                        act([mt], lambda e: e.copy(v_sb[:, 8 * b:8 * b + 8, c * P:(c + 1) * P], view.rearrange("p (k n) -> p k n", k=8)))
                    dve([m_sv], lambda e: e.tensor_scalar(wp[:, c, :], wp[:, c, :], sv[:, c:c + 1], None, ALU.mult))
                dve([m_tanh], lambda e: e.tensor_scalar(bp_all[:], bp_all[:], tgates[:, 0:1], None, ALU.mult))
                led.meet()

            attn = sa("attn", [P, NT + 1, C])
            prob = sa("prob", [P, 2, NTOK], U16)
            probT = sa("probT", [P, 2, NTOK], BF16)
            top = sa("top", [P, 2, 3])
            shift = sa("shift", [P, 2])
            bias = sa("bias", [P, 2])
            norm = sa("norm", [P, H, 2])
            rnorm = sa("rnorm", [P, H])
            zeros = sa("zeros", [P, 1024])

            HALF = NTOK // 2
            LN255 = float(np.log(255.0))
            score = [flat(2 * b, 2 * b + 2) for b in range(3)]
            tbank = bank[:, 6, :]
            obank = bank[:, 7, 0:C]

            s_qk = sem("scores_ready")
            s_exp = sem("exp_finished")
            s_bias = sem("bias_ready")
            s_t0, s_t1 = sem("half0_transposed"), sem("half1_transposed")
            s_e0, s_e1 = sem("half0_evacuated"), sem("half1_evacuated")
            s_o, s_ofree = sem("outputs_ready"), sem("outputs_taken")
            s_qfree, s_qcur = sem("head_multiplied"), sem("query_pair_copied")
            s_v = sem("vector_finished")

            m_z = pool([], lambda e: e.memset(zeros[:], 0.0))
            led.wait("sp", [m_z])
            for rows in [dispatched[512 * r:512 * (r + 1), :] for r in range(E0 * CAP // 512)] + \
                        [dispatched1[512 * r:512 * (r + 1), :] for r in range(NBLOCKS1 * P // 512)]:
                nc.sync.dma_start(rows.rearrange("(p f) c -> p (f c)", p=P), zeros[:]).then_inc(s_zero, 16)

            m = [dve([], lambda e: e.memset(prob[:].bitcast(U32), 0x64006400)),
                 pool([], lambda e: e.memset(probT[:].bitcast(F32), 0.0)),
                 dve([], lambda e: e.memset(norm[:], 1.0)),
                 dve([], lambda e: e.memset(rnorm[:], 1.0)),
                 dve([], lambda e: e.memset(tbank, 0.0)),
                 dve([], lambda e: e.memset(obank, 0.0))]
            act(m, lambda e: e.copy(q_cur[0:KB, 0:H:2, :], qT_all[0:KB, :, 0:P]))
            dve(m, lambda e: e.tensor_copy(q_cur[KB:P, 1:H:2, :], qT_all[KB:P, :, 0:P]))
            led.meet()

            m_bias = pool([], lambda e: e.tensor_tensor(x_sb[:], x_sb[:], bp_all[:].unsqueeze(1).broadcast_to([P, NT, C]), ALU.add))

            def scores(g, u, n):
                for v in range(2):
                    k0 = u * HALF + v * 512
                    mm = nc.tensor.matmul(score[n % 3][:, v * 512:(v + 1) * 512], q_cur[:, g, :], kT[:, g // 2, k0:k0 + 512],
                                          start=True, stop=True)
                    if u == 1 or v == 1:
                        mm.then_inc(s_qk, 1)

            def maximum(g, u, v, n):
                src = score[n % 3] if u == 0 else score[n % 3][:, v * 512:(v + 1) * 512]
                c = 0 if u == 0 else 1 + v
                nc.vector.tensor_reduce(top[:, g % 2, c:c + 1], src, AX.X, ALU.max).then_inc(s_v, 1)

            def make_bias(g, t, n):
                nc.vector.wait_ge(s_v, n)
                nc.vector.tensor_reduce(shift[:, g % 2:g % 2 + 1], top[:, g % 2, :], AX.X, ALU.max).then_inc(s_v, 1)
                nc.vector.wait_ge(s_v, n + 1)
                nc.vector.tensor_scalar(bias[:, g % 2:g % 2 + 1], shift[:, g % 2:g % 2 + 1], nsq_all[:, ds(t * H + g, 1)], LN255,
                                        ALU.mult, ALU.add).then_inc(s_bias, 1)

            def exponentials(g, u, t, n):
                low = prob[:, g % 2, :].bitcast(U8)[:, u * NTOK:(u + 1) * NTOK:2]
                nc.scalar.activation(low, score[n % 3], ACT.Exp, bias=bias[:, g % 2:g % 2 + 1],
                                     scale=sq_all[:, ds(t * H + g, 1)], accum_out=norm[:, g, u:u + 1]).then_inc(s_exp, 1)

            def transpose_half(h, u, signal):
                words = prob[:, h % 2, :].bitcast(F32)
                for c in range(4):
                    mm = nc.tensor.transpose(tbank[:, c * P:(c + 1) * P], words[:, (4 * u + c) * P:(4 * u + c + 1) * P], ident[:])
                mm.then_inc(signal, 1)

            def values(h):
                pt = probT[:, h % 2, :].rearrange("p (c q two) -> p c q two", c=8, two=2)
                for r in range(NT):
                    mm = nc.tensor.matmul(obank[:, h * HD:(h + 1) * HD], pt[:, r // 2, :, r % 2], v_sb[:, r, h * HD:(h + 1) * HD],
                                          start=(r == 0), stop=(r == NT - 1))
                return mm

            def take_outputs(slot):
                nc.vector.tensor_tensor(attn[:, slot, :].rearrange("p (h d) -> p h d", h=H), obank.rearrange("p (h d) -> p h d", h=H),
                                        rnorm[:].unsqueeze(2).broadcast_to([P, H, HD]), ALU.mult).then_inc(s_ofree, 1)

            def normaliser(h0, n):
                nc.vector.tensor_tensor(rnorm[:, h0:h0 + 8], norm[:, h0:h0 + 8, 0], norm[:, h0:h0 + 8, 1], ALU.add).then_inc(s_v, 1)
                nc.vector.wait_ge(s_v, n + 1)
                nc.vector.reciprocal(rnorm[:, h0:h0 + 8], rnorm[:, h0:h0 + 8]).then_inc(s_v, 1)

            for n in range(3):
                scores(n // 2, n % 2, n)
            for n, v in ((0, None), (1, 0), (1, 1)):
                nc.vector.wait_ge(s_qk, 1 + n + (v or 0))
                maximum(n // 2, n % 2, v, n)
            make_bias(0, 0, 3)
            nc.vector.wait_ge(s_qk, 4)
            maximum(1, 0, None, 2)
            nc.vector.nop().then_inc(s_qk, -4)
            nc.vector.wait_ge(s_v, 5)
            nc.vector.nop().then_inc(s_v, -5)
            nc.tensor.nop().then_inc(s_t1, 1)
            led.wait("pool", [m_bias])
            nc.gpsimd.nop().then_inc(s_qcur, H)

            def tiles(t0, ntiles):
                pe, ve, ac, po = nc.tensor, nc.vector, nc.scalar, nc.gpsimd
                n_v = 0
                for n in range(ntiles * H):
                    j, h = divmod(n, H)
                    t = t0 + j
                    g, tg = (h + 1, t) if h + 1 < H else (0, t + 1)
                    g2 = (h + 2) % H

                    pe.wait_ge(s_exp, 2 * n + 1)
                    scores(g, 1, 2 * n + 3)
                    pe.wait_ge(s_e1, n + 1)
                    transpose_half(h, 0, s_t0)
                    if h == 1:
                        pe.wait_ge(s_ofree, j + 1)
                    mm = values((h - 1) % H)
                    mm.then_inc(s_o if h == 0 else s_qfree, 1)
                    pe.wait_ge(s_exp, 2 * n + 2)
                    if g2 % 2 == 0:
                        pe.wait_ge(s_qcur, H * j + (H + 2 if g2 == 0 else g2 + 2))
                    scores(g2, 0, 2 * n + 4)
                    pe.wait_ge(s_e0, n + 1)
                    transpose_half(h, 1, s_t1)

                    for v in range(2):
                        ve.wait_ge(s_qk, 3 * n + 1 + v)
                        maximum(g, 1, v, 2 * n + 3)
                        n_v += 1
                    make_bias(g, tg, n_v)
                    n_v += 1
                    ve.wait_ge(s_t0, n + 1)
                    ve.tensor_scalar(probT[:, h % 2, 0:HALF], tbank.bitcast(F16), -1024.0, None, ALU.add).then_inc(s_e0, 1)
                    if h == 0:
                        normaliser(8, n_v)
                        n_v += 2
                        ve.wait_ge(s_v, n_v)
                        ve.wait_ge(s_o, j + 1)
                        take_outputs(t)
                    if h == 9:
                        normaliser(0, n_v)
                        n_v += 2
                    ve.wait_ge(s_qk, 3 * n + 3)
                    maximum(g2, 0, None, 2 * n + 4)
                    n_v += 1

                    ac.wait_ge(s_bias, n + 1)
                    exponentials(h, 0, t, 2 * n)
                    ac.wait_ge(s_t1, n + 1)
                    ac.activation(probT[:, (h - 1) % 2, HALF:], tbank.bitcast(F16), ACT.Copy, bias=-1024.0).then_inc(s_e1, 1)
                    exponentials(h, 1, t, 2 * n + 1)

                    if h % 2 == 0:
                        p = h // 2
                        po.wait_ge(s_qfree, (H - 1) * j + max(1, h))
                        po.tensor_copy(q_cur[0:KB, h, :], qT_all[0:KB, p, ds(t * P + P, P)]).then_inc(s_qcur, 1)
                        po.tensor_copy(q_cur[KB:P, h + 1, :], qT_all[KB:P, p, ds(t * P + P, P)]).then_inc(s_qcur, 1)

                ve.wait_ge(s_v, n_v)
                po.wait_ge(s_qfree, (H - 1) * ntiles)
                N = ntiles * H
                for e, s, count in ((pe, s_exp, 2 * N), (pe, s_e1, N), (pe, s_e0, N), (pe, s_ofree, ntiles), (pe, s_qcur, N),
                                    (ve, s_qk, 3 * N), (ve, s_t0, N), (ve, s_o, ntiles), (ve, s_v, n_v),
                                    (ac, s_bias, N), (ac, s_t1, N), (po, s_qfree, (H - 1) * ntiles)):
                    e.nop().then_inc(s, -count)

            RING = 3
            with nc.Fori(0, NT // RING) as r:
                tiles(r * RING, RING)
            for t in range(NT // RING * RING, NT):
                tiles(t, 1)

            nc.scalar.wait_ge(s_t1, 1)
            m = act([], lambda e: e.activation(probT[:, 1, HALF:], tbank.bitcast(F16), ACT.Copy, bias=-1024.0))
            led.wait("pe", [m])
            nc.tensor.wait_ge(s_qcur, H)
            m_o = led.done("pe", values(H - 1))
            nc.vector.tensor_tensor(rnorm[:, 8:16], norm[:, 8:16, 0], norm[:, 8:16, 1], ALU.add).then_inc(s_v, 1)
            nc.vector.wait_ge(s_v, 1)
            m = dve([], lambda e: e.reciprocal(rnorm[:, 8:16], rnorm[:, 8:16]))
            led.wait("dve", [m, m_o])
            take_outputs(NT)
            dve([], lambda e: e.memset(top[:], 0.0))
            led.wait("pool", [m_o])
            pool([], lambda e: e.memset(q_cur[:, 0, 0:1], 0.0))
            led.meet()

            aT = sa("aT", [P, 2, CK, G * P])

            def turn_attention(g, free):
                m = transposes([free], [(flat(2 * (g % 2), 2 * (g % 2) + 2)[:, (c * G + k) * P:(c * G + k + 1) * P],
                                         attn[:, g * G + 1 + k, c * P:(c + 1) * P]) for c in range(CK) for k in range(G)], ident[:])
                return [act([m], lambda e: e.copy(aT[:, g % 2, 0, :], bank[:, 2 * (g % 2), :])),
                        dve([m], lambda e: e.tensor_copy(aT[:, g % 2, 1, :], bank[:, 2 * (g % 2) + 1, :]))]

            added = {}
            turned = {0: turn_attention(0, None)}
            for g in range(NG):
                out_banks = flat(4 + 2 * (g % 2), 6 + 2 * (g % 2))
                if g + 1 < NG:
                    turned[g + 1] = turn_attention(g + 1, product if g else None)
                product = matmuls(turned[g] + [added.get(g - 2)], [(out_banks[:, k * C:(k + 1) * C],
                                                                    [(aT[:, g % 2, c, k * P:(k + 1) * P], wp[:, c, :]) for c in range(CK)])
                                                                   for k in range(G)])
                for k in range(G):
                    added[g] = dve([product], lambda e: e.scalar_tensor_tensor(x_sb[:, g * G + k, :], out_banks[:, k * C:(k + 1) * C], tgates[:, 0:1],
                                                                               x_sb[:, g * G + k, :], ALU.mult, ALU.add))
                for k in range(G):
                    last_stats = tile_stats(g * G + k, [added[g]])
            led.meet()

        def turn_and_route(make, rows, destT, w=None, n=0, logits=None):
            made = {g: make(g) for g in range(2)}
            read, copied = {}, {}
            for g in range(NG + 1):
                if g < NG:
                    b = 2 * (g % 2)
                    m = transposes([made[g]] + read.get(g - 2, []), [(flat(b, b + 2)[:, (c * G + k) * P:(c * G + k + 1) * P], rows[:, g * G + k, c * P:(c + 1) * P])
                                                                     for c in range(CK) for k in range(G)], ident[:])
                    read[g] = [act([m], lambda e: e.copy(destT[:, 0, g * G * P:(g + 1) * G * P], bank[:, b, :])),
                               dve([m], lambda e: e.tensor_copy(destT[:, 1, g * G * P:(g + 1) * G * P], bank[:, b + 1, :]))]
                    if g + 2 < NG:
                        made[g + 2] = make(g + 2)
                if w is not None and g > 0:
                    r = g - 1
                    m = matmuls(read[r] + [copied.get(r - 2)], [(bank[:, 4 + r % 2, k * n:(k + 1) * n],
                                                                 [(destT[:, c, (r * G + k) * P:(r * G + k + 1) * P], w[:, c, :]) for c in range(CK)])
                                                                for k in range(G)])
                    copied[r] = act([m], lambda e: e.copy(logits[:, r * G:(r + 1) * G, :], bank[:, 4 + r % 2, 0:G * n].rearrange("p (k n) -> p k n", k=G)))

        def load(s, dst, src):
            nc.sync.dma_start(dst, src).then_inc(s, 16)

        def silu_times_up(after, rhs, gate_w, up_w, widths, hT, sil, free):
            mh = None
            for c, w in enumerate(widths):
                b = free["n"] % 2
                free["n"] += 1
                mg = matmuls(after + [free["gate", b]], [(bank[0:w, b, :], [(gate_w(c, k), rhs(k)) for k in range(CK)])])
                mu = matmuls([free["up", b]], [(bank[0:w, 2 + b, :], [(up_w(c, k), rhs(k)) for k in range(CK)])])
                ms = act([mg, free["up", b]], lambda e: e.activation(sil[0:w, b, :], bank[0:w, b, :], ACT.Silu))
                mh = dve([ms, mu, free["hidden"]], lambda e: e.tensor_tensor(hT[0:w, c, :], sil[0:w, b, :], bank[0:w, 2 + b, :], ALU.mult))
                free["gate", b], free["up", b] = ms, mh
            return mh

        def nothing_read():
            return {("gate", 0): None, ("gate", 1): None, ("up", 0): None, ("up", 1): None, "hidden": None, "n": 0}

        def top_experts(sr, logits, E, K, tag, ready):
            pr = sr(tag + "pr", [P, NT, E])
            top8, idx8 = sr(tag + "top8", [P, NT, 8]), sr(tag + "idx8", [P, NT, 8], U32)
            idxf, iota_i, iota_f = sr(tag + "idxf", [P, NT * K]), sr(tag + "iota_i", [P, E], U32), sr(tag + "iota_f", [P, E])
            hot = sr(tag + "hot", [P, NT * K, E])
            r1, r2 = sr(tag + "r1", [P, NT]), sr(tag + "r2", [P, NT])
            mi = pool([], lambda e: e.iota(iota_i[:], pattern=[[1, E]], base=0, channel_multiplier=0))
            mi = pool([mi], lambda e: e.tensor_copy(iota_f[:], iota_i[:]))
            m = dve(ready, lambda e: e.tensor_reduce(r1[:], logits, AX.X, ALU.max))
            m = dve([m], lambda e: e.tensor_tensor(pr[:], logits, r1[:].unsqueeze(2).broadcast_to([P, NT, E]), ALU.subtract))
            m = act([m], lambda e: e.activation(pr[:], pr[:], ACT.Exp))
            m = dve([m], lambda e: e.tensor_reduce(r2[:], pr[:], AX.X, ALU.add))
            m = dve([m], lambda e: e.reciprocal(r2[:], r2[:]))
            m = dve([m], lambda e: e.tensor_tensor(pr[:], pr[:], r2[:].unsqueeze(2).broadcast_to([P, NT, E]), ALU.mult))
            led.wait("dve", [m])
            for t in range(NT):
                m = dve([], lambda e: e.max(top8[:, t, :], pr[:, t, :]))
            led.wait("dve", [m])
            for t in range(NT):
                m = dve([], lambda e: e.max_index(idx8[:, t, :], top8[:, t, :], pr[:, t, :]))
            m = dve([m], lambda e: e.tensor_copy(idxf[:].rearrange("p (t k) -> p t k", k=K), idx8[:, :, 0:K]))
            m = dve([m, mi], lambda e: e.tensor_tensor(hot[:], iota_f[:].unsqueeze(1).broadcast_to([P, NT * K, E]),
                                                       idxf[:].unsqueeze(2).broadcast_to([P, NT * K, E]), ALU.is_equal))
            return top8, hot, m

        def route(tag, stack, logits, E, K, ready, capacity, dest, wts, owner=None, put=None):
            s = buffers(stack)
            before, every = s(tag + "before", [P, P], BF16), s(tag + "every", [P, P], BF16)
            mask, prefix = s(tag + "mask", [P, NT, E], BF16), s(tag + "prefix", [P, 2, NT, E], BF16)
            first, slot = s(tag + "first", [P, E]), s(tag + "slot", [P, NT, E])
            picked, destf = s(tag + "picked", [P, NT * K, E]), s(tag + "destf", [P, NT * K])
            mc = pool([], lambda e: e.memset(every[:], 1.0))
            mc = pool([mc], lambda e: e.affine_select(out=before[:], in_=every[:], compare_op=ALU.is_gt, fill=0.0, base=0,
                                                      pattern=[[1, P]], channel_multiplier=-1))
            top8, hot, m = top_experts(s, logits, E, K, tag, ready)
            hot4 = hot[:].rearrange("p (t k) e -> p t k e", k=K)
            with nc.allow_low_precision(reason="counts up to 16 are exact in bfloat16"):
                m = dve([m], lambda e: e.tensor_reduce(mask[:], hot4.rearrange("p t k e -> p t e k"), AX.X, ALU.add))
            m2 = [dve([], lambda e: e.memset(prefix[:, :, 0:1, :], 0.0))]
            m2 += [dve([m], lambda e: e.tensor_copy(prefix[:, 0, 1:, :], mask[:, 0:NT - 1, :]))]
            d = 1
            while d < NT:
                b = d.bit_length() % 2
                m2 = [dve(m2, lambda e: e.tensor_tensor(prefix[:, b, d:, :], prefix[:, 1 - b, d:, :], prefix[:, 1 - b, 0:NT - d, :], ALU.add)),
                      dve(m2, lambda e: e.tensor_copy(prefix[:, b, 0:d, :], prefix[:, 1 - b, 0:d, :]))]
                d *= 2
            prefix = prefix[:, b]
            groups = [(bank[:, 7, 0:NT * E], [(before[:], mask[:].rearrange("p t e -> p (t e)")), (every[:], prefix.rearrange("p t e -> p (t e)"))])]
            if capacity is None:
                groups.append((bank[:, 6, 0:E], [(every[:], prefix[:, NT - 1, :]), (every[:], mask[:, NT - 1, :])]))
            m = matmuls(m2 + [mc], groups)
            place = bank[:, 7, 0:NT * E].rearrange("p (t e) -> p t e", e=E)
            if capacity is not None:
                first_i, far = s(tag + "first_i", [P, E], U32), s(tag + "far", [P, NT, E])
                mf = pool([], lambda e: e.iota(first_i[:], pattern=[[capacity, E]], base=0, channel_multiplier=0))
                mf = pool([mf], lambda e: e.tensor_copy(first[:], first_i[:]))
                m1 = dve([m], lambda e: e.tensor_scalar(far[:], place, float(capacity), FAR, ALU.is_ge, ALU.mult))
                m = dve([m, mf], lambda e: e.tensor_tensor(slot[:], place, first[:].unsqueeze(1).broadcast_to([P, NT, E]), ALU.add))
                m = dve([m, m1], lambda e: e.tensor_tensor(slot[:], slot[:], far[:], ALU.add))
            else:
                nblocks = owner.shape[1]
                blocks, upto, one = s(tag + "blocks", [P, E]), s(tag + "upto", [P, E]), s(tag + "one", [P, E])
                num_i, num = s(tag + "num_i", [P, nblocks], U32), s(tag + "num", [P, nblocks])
                past, own = s(tag + "past", [P, nblocks, E]), s(tag + "own", [P, nblocks])
                mn = pool([], lambda e: e.iota(num_i[:], pattern=[[1, nblocks]], base=0, channel_multiplier=0))
                mn = pool([mn], lambda e: e.tensor_copy(num[:], num_i[:]))
                mb = dve([m], lambda e: e.tensor_scalar(blocks[:], bank[:, 6, 0:E], 63.5, 1.0 / 128.0, ALU.add, ALU.mult))
                mb = dve([mb], lambda e: e.tensor_scalar(blocks[:], blocks[:], ROUND, -ROUND, ALU.add, ALU.add))
                mo = dve([], lambda e: e.memset(one[:], 1.0))
                mu = dve([mb, mo], lambda e: e.tensor_tensor_scan(upto[:], one[:], blocks[:], 0.0, ALU.mult, ALU.add))
                mf = dve([mu], lambda e: e.tensor_tensor(first[:], upto[:], blocks[:], ALU.subtract))
                mf = dve([mf], lambda e: e.tensor_scalar(first[:], first[:], float(P), None, ALU.mult))
                mp = dve([mu, mn], lambda e: e.tensor_tensor(past[:], upto[:].unsqueeze(1).broadcast_to([P, nblocks, E]),
                                                             num[:].unsqueeze(2).broadcast_to([P, nblocks, E]), ALU.is_le))
                mp = dve([mp], lambda e: e.tensor_reduce(own[:], past[:], AX.X, ALU.add))
                mp = dve([mp], lambda e: e.tensor_scalar(own[:], own[:], float(E - 1), None, ALU.min))
                dve([mp], lambda e: e.tensor_copy(owner, own[:]))
                m = dve([m, mf], lambda e: e.tensor_tensor(slot[:], place, first[:].unsqueeze(1).broadcast_to([P, NT, E]), ALU.add))
            m = dve([m], lambda e: e.tensor_tensor(picked[:].rearrange("p (t k) e -> p t k e", k=K), hot4,
                                                   slot[:].unsqueeze(2).broadcast_to([P, NT, K, E]), ALU.mult))
            m = dve([m], lambda e: e.tensor_reduce(destf[:], picked[:], AX.X, ALU.add))
            m_r = m
            m_d = dve([m], lambda e: e.tensor_copy((dest if put is None else put)[:].rearrange("p t k -> p (t k)"), destf[:]))
            if capacity is not None:
                dve([m_r], lambda e: e.tensor_scalar(dest[:].rearrange("p t k -> p (t k)"), destf[:], float(E * capacity - 1), None, ALU.min))
                m = dve([m], lambda e: e.scalar_tensor_tensor(wts[:], destf[:].rearrange("p (t k) -> p t k", k=K), float(E * capacity),
                                                              top8[:, :, 0:K], ALU.is_lt, ALU.mult))
            else:
                m = dve([], lambda e: e.tensor_copy(wts[:], top8[:, :, 0:K]))
            return m_d

        def dispatch(s_done, dest, K, rows, target, m_d):
            led.wait("pool", [m_d])
            for t in range(NT):
                for k in range(K):
                    nc.gpsimd.indirect_dma_start(out=target, out_offset=bass.IndirectOffsetOnAxis(ap=dest[:, t, k:k + 1], axis=0),
                                                 in_=rows[:, t, :], in_offset=None, bounds_check=target.shape[0] - 1,
                                                 oob_is_err=False).then_inc(s_done, 16)

        def shared_block(i, xT, gate_w, up_w, down_w, widths, hT, sil, acc, gate, before_acc, between):
            m = silu_times_up([], lambda k: xT[:, k, ds(i * (G * P), G * P)], gate_w, up_w, widths, hT, sil, nothing_read())
            m = matmuls([m], [(flat(4, 6)[:, k * C:(k + 1) * C], [(hT[0:w, c, k * P:(k + 1) * P], down_w(c)) for c, w in enumerate(widths)])
                              for k in range(G)])
            if between:
                between()
            led.wait("dve", before_acc)
            for k in range(G):
                src = flat(4, 6)[:, k * C:(k + 1) * C]
                if gate is None:
                    m2 = dve([m], lambda e: e.tensor_copy(acc[:, i * G + k, :], src))
                else:
                    m2 = dve([m], lambda e: e.scalar_tensor_tensor(acc[:, i * G + k, :], src, gate[:, ds(i * G + k, 1)],
                                                                   acc[:, i * G + k, :], ALU.mult, ALU.add))
            return m2

        def expert_blocks(tag, stack, nblocks, source, target, load_weights, weights):
            s_ = buffers(stack)
            SLOTS, STORES, TURN, F2 = 8, 4, 8, 2 * F0
            erow, erowT = s_(tag + "erow", [P, SLOTS, C]), s_(tag + "erowT", [P, 2, CK, P])
            esil, eh, ehT = s_(tag + "esil", [P, 2, F0]), s_(tag + "eh", [P, 2, F0]), s_(tag + "ehT", [FC, 2, 2, P])
            yrow = s_(tag + "yrow", [P, STORES, C])
            s_ew = [sem(f"{tag}expert_loaded_{s}") for s in range(SLOTS)]
            s_ey = [sem(f"{tag}answer_stored_{s}") for s in range(STORES)]
            for s in range(STORES):
                nc.scalar.nop().then_inc(s_ey[s], 16)
            order = []
            for s in range(TURN + 2):
                order += [("rows", s + 1)] if s + 1 < TURN else []
                order += [("hidden", s)] if s < TURN else []
                order += [("turn", s - 1)] if 0 <= s - 1 < TURN else []
                order += [("answer", s - 2)] if 0 <= s - 2 < TURN else []
            order = [("rows", 0)] + order
            makes = {"rows": (("pe", "rows read"), ("act", "rowsT")), "hidden": (("pe", "hidden"), ("act", "silu"), ("dve", "h")),
                     "turn": (("pe", "turn"), ("dve", "hT")), "answer": (("pe", "answer"), ("act", "y"))}
            count, place = {"pe": 0, "act": 0, "dve": 0}, {}
            for what, s in order:
                for engine, step in makes[what]:
                    count[engine] += 1
                    place[step, s] = (engine, count[engine])
            with led.repeat(nblocks // TURN, **count) as i:
                m = {}

                def need(waiter, *steps):
                    for step, s in steps:
                        if s >= 0:
                            led.wait(waiter, [m[step, s]])
                        else:
                            engine, rel = place[step, s + TURN]
                            led.wait(waiter, [Mark(engine, rel, led.loop)], back=1)

                def fetch(s):
                    need("sp", ("answer", s - SLOTS))
                    load(s_ew[s % SLOTS], erow[:, s % SLOTS, :], source[ds((i * TURN + s) * P, P), :])
                    return 16 * (1 + load_weights(s % SLOTS, i * TURN + s, s_ew[s % SLOTS]))

                def rows(s):
                    n = fetched.pop(s)
                    nc.tensor.wait_ge(s_ew[s % SLOTS], n)
                    nc.tensor.nop().then_inc(s_ew[s % SLOTS], -n)
                    need("pe", ("rowsT", s - 2))
                    mt = transposes([], [(bank[:, s % 2, c * P:(c + 1) * P], erow[:, s % SLOTS, c * P:(c + 1) * P]) for c in range(CK)], ident[:])
                    need("act", ("hidden", s - 2))
                    m["rowsT", s] = act([mt], lambda e: e.copy(erowT[:, s % 2, :, :].rearrange("p c n -> p (c n)"), bank[:, s % 2, 0:CK * P]))

                def hidden(s):
                    gate_up, _ = weights(s % SLOTS, i * TURN + s)
                    need("pe", ("rowsT", s), ("h", s - 2))
                    m["hidden", s] = matmuls([], [(bank[:, 2 + s % 2, 0:F2], [(erowT[:, s % 2, k, :], gate_up(k)) for k in range(CK)])])
                    need("act", ("hidden", s), ("h", s - 2))
                    m["silu", s] = act([], lambda e: e.activation(esil[:, s % 2, :], bank[:, 2 + s % 2, 0:F0], ACT.Silu))
                    need("dve", ("silu", s), ("turn", s - 2))
                    m["h", s] = dve([], lambda e: e.tensor_tensor(eh[:, s % 2, :], esil[:, s % 2, :], bank[:, 2 + s % 2, F0:F2], ALU.mult))

                def turn(s):
                    need("pe", ("h", s), ("hT", s - 2))
                    m["turn", s] = transposes([], [(bank[0:FC, 4 + s % 2, c * P:(c + 1) * P], eh[:, s % 2, c * FC:(c + 1) * FC]) for c in range(2)], ident[:])
                    need("dve", ("turn", s), ("answer", s - 2))
                    m["hT", s] = dve([], lambda e: e.tensor_copy(ehT[:, s % 2, :, :].rearrange("p c n -> p (c n)"), bank[0:FC, 4 + s % 2, 0:2 * P]))

                def answer(s):
                    _, down = weights(s % SLOTS, i * TURN + s)
                    need("pe", ("hT", s), ("y", s - 2))
                    m["answer", s] = matmuls([], [(bank[:, 6 + s % 2, 0:C], [(ehT[:, s % 2, c, :], down(c)) for c in range(2)])])
                    nc.scalar.wait_ge(s_ey[s % STORES], 16)
                    nc.scalar.nop().then_inc(s_ey[s % STORES], -16)
                    m["y", s] = act([m["answer", s]], lambda e: e.copy(yrow[:, s % STORES, :], bank[:, 6 + s % 2, 0:C]))
                    led.wait("act", [m["y", s]])
                    nc.scalar.dma_start(target[ds((i * TURN + s) * P, P), :], yrow[:, s % STORES, :]).then_inc(s_ey[s % STORES], 16)

                fetched = {s: fetch(s) for s in range(SLOTS)}
                for what, s in order:
                    {"rows": rows, "hidden": hidden, "turn": turn, "answer": answer}[what](s)
            for s in range(STORES):
                nc.scalar.wait_ge(s_ey[s], 16)
            act([], lambda e: e.copy(stored[:], eps_ln[:]))

        def combine(tag, stack, K, source, dest, wts, acc, tgate, shared, store=None):
            s_ = buffers(stack)
            got = s_(tag + "got", [P, NT, K, C])
            s_got = [sem(f"{tag}answers_fetched_{t}") for t in range(NT)]
            for t in range(NT):
                for k in range(K):
                    nc.gpsimd.indirect_dma_start(out=got[:, t, k, :], out_offset=None, in_=source,
                                                 in_offset=bass.IndirectOffsetOnAxis(ap=dest[:, t, k:k + 1], axis=0),
                                                 bounds_check=source.shape[0] - 1, oob_is_err=False).then_inc(s_got[t], 16)

            def add(first, after=()):
                m = {}
                led.wait("dve", after)
                for t in range(first, first + G):
                    nc.vector.wait_ge(s_got[t], 16 * K)
                for k in range(K):
                    for t in range(first, first + G):
                        m[t] = dve([m.get(t)], lambda e: e.scalar_tensor_tensor(acc[:, t, :], got[:, t, k, :], wts[:, t, k:k + 1],
                                                                                acc[:, t, :], ALU.mult, ALU.add))
                for t in range(first, first + G):
                    last = dve([m[t]], lambda e: e.scalar_tensor_tensor(x_sb[:, t, :], acc[:, t, :], tgate, x_sb[:, t, :], ALU.mult, ALU.add))
                if store:
                    store(first, last)
                else:
                    for t in range(first, first + G):
                        last = tile_stats(t, [last])
                return last

            m = shared(2, between=lambda: add(0))
            add(G, [m])
            m = shared(3, between=lambda: add(2 * G))
            return add(3 * G, [m])

        stored = sb("stored", [P, 1])

        s_wf, s_wn = sem("ffn0_weights_loaded"), sem("ffn0_norm_loaded")
        s_scatter = sem("rows_dispatched")
        WID0 = [P] * -(-FS0 // P)
        NW0 = len(WID0)
        with ExitStack() as ffn:
            sf = buffers(ffn)
            acc = sf("acc", [P, NT, C])
            xT = sf("xT", [P, CK, NTOK])
            dest = sf("dest", [P, NT, K0], U32)
            wts = sf("wts", [P, NT, K0])
            sgate = sf("sgate", [P, NT])
            swg, swu = sf("swg", [P, CK, NW0 * P]), sf("swu", [P, CK, NW0 * P])
            swd = sf("swd", [P, NW0, C])
            hT, sil = sf("hT", [P, NW0, 512]), sf("sil", [P, 2, 512])

            def shared0(i, before_acc=(), between=None):
                return shared_block(i, xT, lambda c, k: swg[:, k, c * P:(c + 1) * P], lambda c, k: swu[:, k, c * P:(c + 1) * P],
                                    lambda c: swd[:, c, :], WID0, hT, sil, acc, sgate, list(before_acc), between)

            with ExitStack() as routing:
                sr = buffers(routing)
                put = sr("put", [P, NT, K0], U32)
                rows0 = sr("rows0", [P, NT, C])
                logits = sr("logits", [P, NT, E0 + 1])
                wrt, wn = sr("wrt", [P, CK, E0 + 1]), sr("wn", [P, C])
                ss, rinv = sr("ss", [P, NT]), sr("rinv", [P, NT])
                sqr = sr("sqr", [P, 2, C])
                load(s_wn, wn[:], a["L0_ffn_w_norm"].partition_broadcast(P))
                load(s_wn, wrt[:, :, 0:E0], a["L0_ffn_w_router"].rearrange("(c p) n -> p c n", p=P))
                with nc.allow_non_contiguous_dma(reason="256 weights, one column"):
                    load(s_wn, wrt[:, :, E0:E0 + 1], a["L0_ffn_w_shared_gate"].rearrange("(c p) n -> p c n", p=P))
                full = FS0 // P * P
                m = [pool([], lambda e: e.memset(swg[:, :, FS0:], 0.0)), pool([], lambda e: e.memset(swu[:, :, FS0:], 0.0)),
                     pool([], lambda e: e.memset(swd[:, NW0 - 1, :], 0.0))]
                led.wait("sp", m)
                load(s_wf, swg[:, :, 0:FS0], a["L0_ffn_sw_gate"].rearrange("(c p) n -> p c n", p=P))
                load(s_wf, swu[:, :, 0:FS0], a["L0_ffn_sw_up"].rearrange("(c p) n -> p c n", p=P))
                load(s_wf, swd[:, 0:FS0 // P, :], a["L0_ffn_sw_down"][0:full, :].rearrange("(c p) n -> p c n", p=P))
                load(s_wf, swd[0:FS0 - full, FS0 // P, :], a["L0_ffn_sw_down"][full:, :])

                m_stats = layer_stats(last_stats)
                led.wait("dve", [m_stats])
                for t in range(NT):
                    m = dve([], lambda e: e.tensor_scalar(acc[:, t, :], x_sb[:, t, :], rstd[:, t:t + 1], nmr[:, t:t + 1], ALU.mult, ALU.add))
                    m2 = act([m] + ([m2] if t >= 2 else []), lambda e: e.activation(sqr[:, t % 2, :], acc[:, t, :], ACT.Square, accum_out=ss[:, t:t + 1]))
                m = act([m2], lambda e: e.activation(ss[:], ss[:], ACT.Sqrt, bias=eps_rms[:], scale=1.0 / C))
                m_r = dve([m], lambda e: e.reciprocal(rinv[:], ss[:]))
                nc.vector.wait_ge(s_wn, 48)
                nc.tensor.wait_ge(s_wn, 48)
                led.wait("dve", [m_r])

                def scaled(g):
                    for t in range(g * G, (g + 1) * G):
                        m = dve([], lambda e: e.scalar_tensor_tensor(rows0[:, t, :], acc[:, t, :], rinv[:, t:t + 1], wn[:], ALU.mult, ALU.mult))
                    return m

                turn_and_route(scaled, rows0, xT, wrt, E0 + 1, logits)
                led.meet()

                m_d = route("r0_", routing, logits[:, :, 0:E0], E0, K0, [], CAP, dest, wts, put=put)
                m = dve([], lambda e: e.tensor_scalar(sgate[:], logits[:, :, E0], -1.0, 87.0, ALU.mult, ALU.min))
                m = act([m], lambda e: e.activation(sgate[:], sgate[:], ACT.Exp))
                m = dve([m], lambda e: e.tensor_scalar(sgate[:], sgate[:], 1.0, None, ALU.add))
                m_sg = dve([m], lambda e: e.reciprocal(sgate[:], sgate[:]))
                nc.gpsimd.wait_ge(s_zero, 16 * ZEROED)
                dispatch(s_scatter, put, K0, rows0, dispatched, m_d)

                nc.tensor.wait_ge(s_wf, 64)
                with led.repeat(2, pe=13, act=6, dve=10) as i:
                    previous_iteration("pe", "act", "dve")
                    previous_iteration("act", "dve")
                    previous_iteration("dve", "pe")
                    shared0(i, [m_sg])
                led.meet()
                for e in ("sp", "pool"):
                    led.engines[e].wait_ge(s_scatter, 16 * NT * K0)

            with ExitStack() as experts:
                se = buffers(experts)
                wgu, wdn = se("wgu", [P, 8, CK, 2, F0]), se("wdn", [FC, 8, 2, C])

                def load_expert(s, e, signal):
                    load(signal, wgu[:, s, :, 0, :], a["L0_ffn_w_gate"][e].rearrange("(c p) n -> p c n", p=P))
                    load(signal, wgu[:, s, :, 1, :], a["L0_ffn_w_up"][e].rearrange("(c p) n -> p c n", p=P))
                    load(signal, wdn[:, s, :, :], a["L0_ffn_w_down"][e].rearrange("(c p) n -> p c n", p=FC))
                    return 3

                expert_blocks("x0_", experts, E0, dispatched, answered, load_expert,
                              lambda s, e: (lambda k: wgu[:, s, k, :, :].rearrange("p u n -> p (u n)"), lambda c: wdn[:, s, c, :]))
                led.meet()
            with ExitStack() as combining:
                last_stats = combine("c0_", combining, K0, answered, dest, wts, acc, tgates[:, 2:3], shared0)
                led.meet()

        def normalised(rows, m_stats):
            led.wait("dve", [m_stats])

            def make(g):
                for t in range(g * G, (g + 1) * G):
                    m = dve([], lambda e: e.tensor_scalar(rows[:, t, :], x_sb[:, t, :], rstd[:, t:t + 1], nmr[:, t:t + 1], ALU.mult, ALU.add))
                return m

            return make

        s_td = sem("decay_weights_loaded")
        with ExitStack() as mixing:
            sm = buffers(mixing)
            kc = sm("kc", [P, CK, NTOK])
            decay, u_first = sm("decay", [P, CK]), sm("u_first", [P, CK])
            fade, ek, ekv = sm("fade", [P, CK, NTOK]), sm("ek", [P, CK, NTOK]), sm("ekv", [P, CK, NTOK])
            sumk, sumkv = sm("sumk", [P, CK, NTOK]), sm("sumkv", [P, CK, NTOK])
            ceil, eu, ec = sm("ceil", [P, CK, NTOK]), sm("eu", [P, CK, NTOK]), sm("ec", [P, CK, NTOK])
            rows_k = ekv[:].rearrange("p c (t n) -> p (c t) n", n=C)
            with nc.allow_non_contiguous_dma(reason="256 values, one per partition"):
                load(s_td, decay[:], a["L1_xattn_time_decay"].rearrange("(c p) -> p c", p=P))
                load(s_td, u_first[:], a["L1_xattn_time_first"].rearrange("(c p) -> p c", p=P))
            m_stats = layer_stats(last_stats)
            turn_and_route(normalised(rows_k, m_stats), rows_k, kc)
            led.meet()
            nc.scalar.wait_ge(s_td, 32)
            nc.vector.wait_ge(s_td, 32)
            m = dve([], lambda e: e.tensor_scalar(decay[:], decay[:], 80.0, None, ALU.min))
            m = act([m], lambda e: e.activation(decay[:], decay[:], ACT.Exp))
            m_dec = act([m], lambda e: e.activation(decay[:], decay[:], ACT.Exp, scale=-1.0))
            chunks = range(CK)
            k_, v_ = [kc[:, c, :] for c in chunks], [ctxT[:, c, :] for c in chunks]
            m_c = [dve([], lambda e: e.tensor_scalar(ceil[:, c, :], k_[c], u_first[:, c:c + 1], 0.0, ALU.add, ALU.max)) for c in chunks]
            m_k, m_ec, m_f, m_eu, m_kv, m_ev = {}, {}, {}, {}, {}, {}
            for c in chunks:
                m_f[c] = act([m_dec], lambda e: e.activation(fade[:, c, :], k_[c], ACT.Identity, bias=decay[:, c:c + 1], scale=0.0))
                m_k[c] = act([], lambda e: e.activation(ek[:, c, :], k_[c], ACT.Exp))
                m_ec[c] = act([m_c[c]], lambda e: e.activation(ec[:, c, :], ceil[:, c, :], ACT.Exp, scale=-1.0))
                m_kc = pool([m_c[c]], lambda e: e.tensor_tensor(eu[:, c, :], k_[c], ceil[:, c, :], ALU.subtract))
                m_eu[c] = act([m_kc], lambda e: e.activation(eu[:, c, :], eu[:, c, :], ACT.Exp, bias=u_first[:, c:c + 1]))
                m_kv[c] = pool([m_k[c]], lambda e: e.tensor_tensor(ekv[:, c, :], ek[:, c, :], v_[c], ALU.mult))
            for c in chunks:
                m_ev[c] = pool([m_eu[c], m_ec[c]], lambda e: e.tensor_tensor(ceil[:, c, :], eu[:, c, :], v_[c], ALU.mult))
            m_d, m_skv = {}, {}
            for c in chunks:
                m = dve([m_f[c]], lambda e: e.memset(fade[:, c, 0:NTOK:T], 0.0))
                m = dve([m, m_k[c]], lambda e: e.tensor_tensor_scan(sumk[:, c, :], fade[:, c, :], ek[:, c, :], 0.0, ALU.mult, ALU.add))
                m = dve([m, m_ec[c], m_kv[c]], lambda e: e.tensor_tensor(ek[:, c, 1:], ec[:, c, 1:], sumk[:, c, 0:NTOK - 1], ALU.mult))
                m = dve([m, m_eu[c]], lambda e: e.tensor_tensor(ek[:, c, 1:], ek[:, c, 1:], eu[:, c, 1:], ALU.add))
                m_skv[c] = dve([m_kv[c]], lambda e: e.tensor_tensor_scan(sumkv[:, c, :], fade[:, c, :], ekv[:, c, :], 0.0, ALU.mult, ALU.add))
                m_d[c] = dve([m], lambda e: e.reciprocal(ek[:, c, 1:], ek[:, c, 1:]))
            m_n = {}
            for c in chunks:
                m = pool([m_skv[c], m_ec[c]], lambda e: e.tensor_tensor(ekv[:, c, 1:], ec[:, c, 1:], sumkv[:, c, 0:NTOK - 1], ALU.mult))
                m_n[c] = pool([m, m_ev[c]], lambda e: e.tensor_tensor(ekv[:, c, 1:], ekv[:, c, 1:], ceil[:, c, 1:], ALU.add))
            for c in chunks:
                m = dve([m_n[c], m_d[c]], lambda e: e.tensor_tensor(kc[:, c, 1:], ekv[:, c, 1:], ek[:, c, 1:], ALU.mult))
                dve([m], lambda e: e.tensor_copy(kc[:, c, 0:NTOK:T], ctxT[:, c, 0:NTOK:T]))
            led.meet()

            for g in range(NG):
                b = 2 * (g % 2)
                m = transposes([added.get(("mixed", g - 2))], [(flat(b, b + 2)[:, k * C + c * P:k * C + (c + 1) * P], kc[:, c, (g * G + k) * P:(g * G + k + 1) * P])
                                                               for k in range(G) for c in range(CK)], ident[:])
                for k in range(G):
                    t = g * G + k
                    added["mixed", g] = dve([m], lambda e: e.scalar_tensor_tensor(x_sb[:, t, :], flat(b, b + 2)[:, k * C:(k + 1) * C], tgates[:, 1:2],
                                                                                  x_sb[:, t, :], ALU.mult, ALU.add))
                for k in range(G):
                    last_stats = tile_stats(g * G + k, [added["mixed", g]])
            led.meet()

        s_w1, s_v1 = sem("ffn1_weights_loaded"), sem("ffn1_router_loaded")
        s_scatter1 = sem("rows_dispatched_1")
        s_out = sem("output_stored")
        WID1 = [P] * (FS1 // P) + ([FS1 % P] if FS1 % P else [])
        with ExitStack() as ffn1:
            s1 = buffers(ffn1)
            acc1 = s1("acc1", [P, NT, C])
            xT1 = s1("xT1", [P, CK, NTOK])
            dest1, wts1 = s1("dest1", [P, NT, K1], U32), s1("wts1", [P, NT, K1])
            owner = s1("owner", [P, NBLOCKS1], U32)
            w1gu = s1("w1gu", [P, E1, CK, 2 * F1])
            w1d = s1("w1d", [FC, E1, 2, C])
            v1g, v1u = s1("v1g", [P, CK, FS1]), s1("v1u", [P, CK, FS1])
            v1d = s1("v1d", [P, len(WID1), C])
            hT1, sil1 = s1("hT1", [P, len(WID1), 512]), s1("sil1", [P, 2, 512])

            def shared1(i, before_acc=(), between=None):
                return shared_block(i, xT1, lambda c, k: v1g[:, k, c * P:c * P + WID1[c]], lambda c, k: v1u[:, k, c * P:c * P + WID1[c]],
                                    lambda c: v1d[0:WID1[c], c, :], WID1, hT1, sil1, acc1, None, list(before_acc), between)

            with ExitStack() as routing1:
                sr = buffers(routing1)
                rows1 = sr("rows1", [P, NT, C])
                w1r, logits1 = sr("w1r", [P, CK, E1]), sr("logits1", [P, NT, E1])
                load(s_v1, w1r[:], a["L1_ffn_gate_w"].rearrange("(c p) n -> p c n", p=P))
                load(s_v1, v1g[:], a["L1_ffn_sw_gate"].rearrange("(c p) n -> p c n", p=P))
                load(s_v1, v1u[:], a["L1_ffn_sw_up"].rearrange("(c p) n -> p c n", p=P))
                for c, w in enumerate(WID1):
                    load(s_v1, v1d[0:w, c, :], a["L1_ffn_sw_down"][c * P:c * P + w, :])
                for e in range(E1):
                    load(s_w1, w1gu[:, e, :, 0:F1], a["L1_ffn_w_gate"][e].rearrange("(c p) n -> p c n", p=P))
                    load(s_w1, w1gu[:, e, :, F1:], a["L1_ffn_w_up"][e].rearrange("(c p) n -> p c n", p=P))
                    load(s_w1, w1d[:, e, :, :], a["L1_ffn_w_down"][e].rearrange("(c p) n -> p c n", p=FC))
                nc.tensor.wait_ge(s_v1, 16 * (3 + len(WID1)))

                m_stats = layer_stats(last_stats)
                turn_and_route(normalised(rows1, m_stats), rows1, xT1, w1r, E1, logits1)
                led.meet()
                m_d = route("r1_", routing1, logits1[:], E1, K1, [], None, dest1, wts1, owner[:])
                dispatch(s_scatter1, dest1, K1, rows1, dispatched1, m_d)
                with led.repeat(2, pe=7, act=3, dve=7) as i:
                    previous_iteration("pe", "act", "dve")
                    previous_iteration("act", "dve")
                    previous_iteration("dve", "pe")
                    shared1(i)
                led.meet()
                for e in ("sp", "pool"):
                    led.engines[e].wait_ge(s_scatter1, 16 * NT * K1)

            with ExitStack() as experts1:
                nc.tensor.wait_ge(s_w1, 16 * 3 * E1)
                expert_of = {}

                def weights1(s, block):
                    if s not in expert_of or expert_of[s][0] is not led.loop or expert_of[s][2] == 2:
                        expert_of[s] = [led.loop, nc.tensor.value_load(owner[0:1, ds(block, 1)], min_val=0, max_val=E1 - 1), 0]
                    expert_of[s][2] += 1
                    r = expert_of[s][1]
                    return lambda k: w1gu[:, r, k, :], lambda c: w1d[:, r, c, :]

                expert_blocks("x1_", experts1, NBLOCKS1, dispatched1, answered1, lambda s, block, signal: 0, weights1)
                led.meet()

                def store(t, m):
                    led.wait("sp", [m])
                    nc.sync.dma_start(outr[:, t:t + G, :], x_sb[:, t:t + G, :]).then_inc(s_out, 16)

                combine("c1_", experts1, K1, answered1, dest1, wts1, acc1, tgates[:, 3:4], shared1, store)
                nc.sync.wait_ge(s_out, 16 * NG)
                led.meet()


def kernel(**inputs):
    import numpy as _np
    import concourse.bacc as _bacc
    from concourse.bass_utils import run_bass_kernel_spmd as _run

    nc = _bacc.Bacc("TRN2", target_bir_lowering=False, num_devices=1)
    arrays, args = {}, {}
    for name, value in inputs.items():
        arrays[f"in_{name}"] = _np.ascontiguousarray(value)
        args[name] = nc.dram_tensor(f"in_{name}", arrays[f"in_{name}"].shape, mybir.dt.from_np(arrays[f"in_{name}"].dtype),
                                    kind="ExternalInput").ap()
    result = nc.dram_tensor("result", inputs["x"].shape, F32, kind="ExternalOutput").ap()
    program(nc, args, result)
    return _run(nc, [arrays], core_ids=[0]).results[0]["result"]
```
